# Optimizing a Trainium2 kernel written in Bass

```python
import numpy as np
import jax
import jax.numpy as jnp

def _softmax(x, axis=-1):
    return jax.nn.softmax(x, axis=axis)

def _gelu(x):
    return jax.nn.gelu(x, approximate=True)

def _silu(x):
    return jax.nn.silu(x)

def _sigmoid(x):
    return jax.nn.sigmoid(x)

def _layernorm(x, axis=-1, eps=1e-05):
    m = jnp.mean(x, axis=axis, keepdims=True)
    v = jnp.var(x, axis=axis, keepdims=True)
    return (x - m) / jnp.sqrt(v + eps)

def _scatter_add(tgt, idx, src, axis=0):
    return tgt.at[idx].add(src)

def _segment_sum(src, seg, n):
    return jax.ops.segment_sum(src, seg, n)
kernel_name = 'mk_gnn_preln_d2_gnn_r64_08cb88'

def setup_inputs(seed: int=0):
    np.random.seed(seed)
    _w = jnp.asarray

    def _rec_inputs():
        import jax
        import jax.numpy as jnp
        _gk = jax.random.key(seed)
        x = -0.0006008 + 1.001 * jax.random.normal(jax.random.fold_in(_gk, 1), (10000, 512), jnp.float32)
        src = jax.random.randint(jax.random.fold_in(_gk, 2), (2500,), 0, 10000, jnp.int32)
        dst = jax.random.randint(jax.random.fold_in(_gk, 3), (2500,), 0, 10000, jnp.int32)
        _o = jnp.argsort(dst, stable=True)
        src = src[_o]
        dst = dst[_o]
        edge_attr_20 = jax.random.uniform(jax.random.fold_in(_gk, 12), (2500, 20), jnp.float32, 0.0, 0.999999)
        edge_attr_3 = -0.0005747 + 0.998114 * jax.random.normal(jax.random.fold_in(_gk, 13), (2500, 3), jnp.float32)
        edge_weight = jax.random.uniform(jax.random.fold_in(_gk, 15), (2500,), jnp.float32, 0.0, 0.999973)
        return (x, src, dst, edge_attr_20, edge_attr_3, edge_weight)
    x, src, dst, edge_attr_20, edge_attr_3, edge_weight = _rec_inputs()

    def _L0_gnn_setup():
        import jax, jax.numpy as jnp
        import numpy as np
        N_ATOMS = 5000
        N_EDGES = 50000
        C = 128
        F = 128
        N_RBF = 20
        LOG2 = float(np.log(2.0))
        Y0 = float(1.0 / np.sqrt(4.0 * np.pi))
        Y1_SCALE = float(np.sqrt(3.0 / (4.0 * np.pi)))

        def shifted_softplus(x):
            return jax.nn.softplus(x) - LOG2

        def _forward(x, idx_i, idx_j, f_ij, rcut_ij, r_ij, W_in2f_s, W_in2f_v, Wf1, bf1, Wf2, bf2, W1_s, W1_v, W2_s, W2_v):
            n = x.shape[0]
            e = r_ij.shape[0]
            xs = x[:, :C] @ (W_in2f_s / np.sqrt(C))
            xv = jnp.einsum('nci,cf->nfi', x[:, C:].reshape(n, C, 3), W_in2f_v) / np.sqrt(C)
            sj = xs[idx_j]
            vj = xv[idx_j]
            u = r_ij / jnp.linalg.norm(r_ij, axis=-1, keepdims=True)
            Yv = Y1_SCALE * u
            o0a = sj * Y0
            o0b = jnp.einsum('efi,ei->ef', vj, Yv) / np.sqrt(3.0)
            s2 = jnp.stack([o0a, o0b], axis=-1).reshape(e, 2 * F)
            ova = sj[:, :, None] * Yv[:, None, :]
            ovb = vj * Y0
            v2 = jnp.stack([ova, ovb], axis=2)
            w1 = jnp.cross(vj, Yv[:, None, :]) / np.sqrt(2.0)
            ax, ay, az = (vj[..., 0], vj[..., 1], vj[..., 2])
            bx, by, bz = (Yv[:, None, 0], Yv[:, None, 1], Yv[:, None, 2])
            t = jnp.stack([(ax * by + ay * bx) / np.sqrt(2.0), (ay * bz + az * by) / np.sqrt(2.0), (2.0 * az * bz - ax * bx - ay * by) / np.sqrt(6.0), (az * bx + ax * bz) / np.sqrt(2.0), (ax * bx - ay * by) / np.sqrt(2.0)], axis=-1)
            h = shifted_softplus(f_ij @ Wf1 + bf1)
            W = (h @ Wf2 + bf2) * rcut_ij[:, None]
            m_s = s2 * W[:, :2 * F]
            m_v = (v2.reshape(e, 2 * F, 3) * W[:, 2 * F:4 * F, None]).reshape(e, 6 * F)
            m_w = (w1 * W[:, 4 * F:5 * F, None]).reshape(e, 3 * F)
            m_t = (t * W[:, 5 * F:6 * F, None]).reshape(e, 5 * F)
            x_ij = jnp.concatenate([m_s, m_v, m_w, m_t], axis=1)
            agg = jax.ops.segment_sum(x_ij, idx_i, num_segments=n)
            S = agg[:, :2 * F] @ (W1_s / np.sqrt(2 * F))
            V = jnp.einsum('nmi,mc->nci', agg[:, 2 * F:8 * F].reshape(n, 2 * F, 3), W1_v) / np.sqrt(2 * F)
            S = shifted_softplus(S)
            S = S @ (W2_s / np.sqrt(C))
            V = jnp.einsum('nci,cd->ndi', V, W2_v) / np.sqrt(C)
            return jnp.concatenate([S, V.reshape(n, 3 * C)], axis=1)
        key = jax.random.key(seed)
        ks = jax.random.split(key, 16)
        f32 = jnp.float32
        x = jax.random.normal(ks[0], (N_ATOMS, 4 * C), f32)
        idx_i = jnp.sort(jax.random.randint(ks[1], (N_EDGES,), 0, N_ATOMS))
        idx_j = jax.random.randint(ks[2], (N_EDGES,), 0, N_ATOMS)
        f_ij = jax.random.uniform(ks[3], (N_EDGES, N_RBF), f32)
        rcut_ij = jax.random.uniform(ks[4], (N_EDGES,), f32)
        r_ij = jax.random.normal(ks[5], (N_EDGES, 3), f32)
        W_in2f_s = jax.random.normal(ks[6], (C, F), f32)
        W_in2f_v = jax.random.normal(ks[7], (C, F), f32)
        Wf1 = jax.random.normal(ks[8], (N_RBF, F), f32) / np.sqrt(N_RBF)
        bf1 = 0.1 * jax.random.normal(ks[9], (F,), f32)
        Wf2 = jax.random.normal(ks[10], (F, 6 * F), f32) / np.sqrt(F)
        bf2 = 0.1 * jax.random.normal(ks[11], (6 * F,), f32)
        W1_s = jax.random.normal(ks[12], (2 * F, C), f32)
        W1_v = jax.random.normal(ks[13], (2 * F, C), f32)
        W2_s = jax.random.normal(ks[14], (C, C), f32)
        W2_v = jax.random.normal(ks[15], (C, C), f32)
        return dict(x=x, idx_i=idx_i, idx_j=idx_j, f_ij=f_ij, rcut_ij=rcut_ij, r_ij=r_ij, W_in2f_s=W_in2f_s, W_in2f_v=W_in2f_v, Wf1=Wf1, bf1=bf1, Wf2=Wf2, bf2=bf2, W1_s=W1_s, W1_v=W1_v, W2_s=W2_s, W2_v=W2_v)
    _L0_gnn_all = _L0_gnn_setup()
    _L0_gnn_in = {k: v for k, v in _L0_gnn_all.items() if k in ('W_in2f_s', 'W_in2f_v', 'Wf1', 'bf1', 'Wf2', 'bf2', 'W1_s', 'W1_v', 'W2_s', 'W2_v')}
    del _L0_gnn_all

    def _L1_gnn_setup():
        import jax, jax.numpy as jnp
        import numpy as np
        NHEAD = 8
        M_NODES = 20000
        D_MODEL = 512
        N_EDGES = 10000
        key = jax.random.key(seed)
        ks = jax.random.split(key, 8)
        sc = 1.0 / np.sqrt(D_MODEL)
        return {'s': jax.random.normal(ks[0], (M_NODES, D_MODEL), dtype=jnp.float32), 'edge_index': jax.random.randint(ks[1], (2, N_EDGES), 0, M_NODES, dtype=jnp.int64), 'Wq': jax.random.normal(ks[2], (D_MODEL, D_MODEL), dtype=jnp.float32) * sc, 'bq': jax.random.normal(ks[3], (D_MODEL,), dtype=jnp.float32) * sc, 'Wkv': jax.random.normal(ks[4], (2 * D_MODEL, D_MODEL), dtype=jnp.float32) * sc, 'bkv': jax.random.normal(ks[5], (2 * D_MODEL,), dtype=jnp.float32) * sc, 'Wo': jax.random.normal(ks[6], (D_MODEL, D_MODEL), dtype=jnp.float32) * sc, 'bo': jax.random.normal(ks[7], (D_MODEL,), dtype=jnp.float32) * sc}
    _L1_gnn_all = _L1_gnn_setup()
    _L1_gnn_in = {k: v for k, v in _L1_gnn_all.items() if k in ('Wq', 'bq', 'Wkv', 'bkv', 'Wo', 'bo')}
    del _L1_gnn_all
    return {'x': x, 'src': src, 'dst': dst, 'edge_attr_20': edge_attr_20, 'edge_attr_3': edge_attr_3, 'edge_weight': edge_weight, 'L0_gnn_W_in2f_s': _L0_gnn_in['W_in2f_s'], 'L0_gnn_W_in2f_v': _L0_gnn_in['W_in2f_v'], 'L0_gnn_Wf1': _L0_gnn_in['Wf1'], 'L0_gnn_bf1': _L0_gnn_in['bf1'], 'L0_gnn_Wf2': _L0_gnn_in['Wf2'], 'L0_gnn_bf2': _L0_gnn_in['bf2'], 'L0_gnn_W1_s': _L0_gnn_in['W1_s'], 'L0_gnn_W1_v': _L0_gnn_in['W1_v'], 'L0_gnn_W2_s': _L0_gnn_in['W2_s'], 'L0_gnn_W2_v': _L0_gnn_in['W2_v'], 'L1_gnn_Wq': _L1_gnn_in['Wq'], 'L1_gnn_bq': _L1_gnn_in['bq'], 'L1_gnn_Wkv': _L1_gnn_in['Wkv'], 'L1_gnn_bkv': _L1_gnn_in['bkv'], 'L1_gnn_Wo': _L1_gnn_in['Wo'], 'L1_gnn_bo': _L1_gnn_in['bo']}

def reference(x, src, dst, edge_attr_20, edge_attr_3, edge_weight, L0_gnn_W_in2f_s, L0_gnn_W_in2f_v, L0_gnn_Wf1, L0_gnn_bf1, L0_gnn_Wf2, L0_gnn_bf2, L0_gnn_W1_s, L0_gnn_W1_v, L0_gnn_W2_s, L0_gnn_W2_v, L1_gnn_Wq, L1_gnn_bq, L1_gnn_Wkv, L1_gnn_bkv, L1_gnn_Wo, L1_gnn_bo):
    import jax
    import jax.numpy as jnp

    def _L0_gnn_ref(x, idx_i, idx_j, f_ij, rcut_ij, r_ij, W_in2f_s, W_in2f_v, Wf1, bf1, Wf2, bf2, W1_s, W1_v, W2_s, W2_v):
        import jax, jax.numpy as jnp
        import numpy as np
        N_ATOMS = 5000
        N_EDGES = 50000
        C = 128
        F = 128
        N_RBF = 20
        LOG2 = float(np.log(2.0))
        Y0 = float(1.0 / np.sqrt(4.0 * np.pi))
        Y1_SCALE = float(np.sqrt(3.0 / (4.0 * np.pi)))

        def shifted_softplus(x):
            return jax.nn.softplus(x) - LOG2

        def _forward(x, idx_i, idx_j, f_ij, rcut_ij, r_ij, W_in2f_s, W_in2f_v, Wf1, bf1, Wf2, bf2, W1_s, W1_v, W2_s, W2_v):
            n = x.shape[0]
            e = r_ij.shape[0]
            xs = x[:, :C] @ (W_in2f_s / np.sqrt(C))
            xv = jnp.einsum('nci,cf->nfi', x[:, C:].reshape(n, C, 3), W_in2f_v) / np.sqrt(C)
            sj = xs[idx_j]
            vj = xv[idx_j]
            u = r_ij / jnp.linalg.norm(r_ij, axis=-1, keepdims=True)
            Yv = Y1_SCALE * u
            o0a = sj * Y0
            o0b = jnp.einsum('efi,ei->ef', vj, Yv) / np.sqrt(3.0)
            s2 = jnp.stack([o0a, o0b], axis=-1).reshape(e, 2 * F)
            ova = sj[:, :, None] * Yv[:, None, :]
            ovb = vj * Y0
            v2 = jnp.stack([ova, ovb], axis=2)
            w1 = jnp.cross(vj, Yv[:, None, :]) / np.sqrt(2.0)
            ax, ay, az = (vj[..., 0], vj[..., 1], vj[..., 2])
            bx, by, bz = (Yv[:, None, 0], Yv[:, None, 1], Yv[:, None, 2])
            t = jnp.stack([(ax * by + ay * bx) / np.sqrt(2.0), (ay * bz + az * by) / np.sqrt(2.0), (2.0 * az * bz - ax * bx - ay * by) / np.sqrt(6.0), (az * bx + ax * bz) / np.sqrt(2.0), (ax * bx - ay * by) / np.sqrt(2.0)], axis=-1)
            h = shifted_softplus(f_ij @ Wf1 + bf1)
            W = (h @ Wf2 + bf2) * rcut_ij[:, None]
            m_s = s2 * W[:, :2 * F]
            m_v = (v2.reshape(e, 2 * F, 3) * W[:, 2 * F:4 * F, None]).reshape(e, 6 * F)
            m_w = (w1 * W[:, 4 * F:5 * F, None]).reshape(e, 3 * F)
            m_t = (t * W[:, 5 * F:6 * F, None]).reshape(e, 5 * F)
            x_ij = jnp.concatenate([m_s, m_v, m_w, m_t], axis=1)
            agg = jax.ops.segment_sum(x_ij, idx_i, num_segments=n)
            S = agg[:, :2 * F] @ (W1_s / np.sqrt(2 * F))
            V = jnp.einsum('nmi,mc->nci', agg[:, 2 * F:8 * F].reshape(n, 2 * F, 3), W1_v) / np.sqrt(2 * F)
            S = shifted_softplus(S)
            S = S @ (W2_s / np.sqrt(C))
            V = jnp.einsum('nci,cd->ndi', V, W2_v) / np.sqrt(C)
            return jnp.concatenate([S, V.reshape(n, 3 * C)], axis=1)
        return _forward(x, idx_i, idx_j, f_ij, rcut_ij, r_ij, W_in2f_s, W_in2f_v, Wf1, bf1, Wf2, bf2, W1_s, W1_v, W2_s, W2_v)

    def _L1_gnn_ref(s, edge_index, Wq, bq, Wkv, bkv, Wo, bo):
        import jax, jax.numpy as jnp
        import numpy as np
        NHEAD = 8
        M_NODES = 20000
        D_MODEL = 512
        N_EDGES = 10000
        M, C = s.shape
        H = NHEAD
        Dh = C // H
        scale = 1.0 / np.sqrt(Dh).astype(np.float32)
        q = (s @ Wq.T + bq).reshape(M, H, Dh)
        kv = (s @ Wkv.T + bkv).reshape(M, H, 2 * Dh)
        k, v = (kv[..., :Dh], kv[..., Dh:])
        src, tgt = (edge_index[0], edge_index[1])
        a = jnp.einsum('ehc,ehc->eh', q[tgt], k[src]) * scale
        a_max = jax.ops.segment_max(a, tgt, num_segments=M)
        ex = jnp.exp(a - a_max[tgt])
        denom = jax.ops.segment_sum(ex, tgt, num_segments=M)
        attn = ex / denom[tgt]
        o_msg = attn[..., None] * v[src]
        o = jax.ops.segment_sum(o_msg, tgt, num_segments=M)
        o = o.reshape(M, C)
        return o @ Wo.T + bo
    edge_index = jnp.stack([src, dst])
    h = jnp.maximum(_layernorm(x, axis=-1), 0.0)
    x = x + _L0_gnn_ref(h, src, dst, edge_attr_20, edge_weight, edge_attr_3, L0_gnn_W_in2f_s, L0_gnn_W_in2f_v, L0_gnn_Wf1, L0_gnn_bf1, L0_gnn_Wf2, L0_gnn_bf2, L0_gnn_W1_s, L0_gnn_W1_v, L0_gnn_W2_s, L0_gnn_W2_v)
    h = jnp.maximum(_layernorm(x, axis=-1), 0.0)
    x = x + _L1_gnn_ref(h, edge_index, L1_gnn_Wq, L1_gnn_bq, L1_gnn_Wkv, L1_gnn_bkv, L1_gnn_Wo, L1_gnn_bo)
    return x

_drawn_inputs = setup_inputs


def setup_inputs(seed=0):
    import zlib

    import numpy as np

    out = dict(_drawn_inputs(seed))
    spreads = {}
    factors = {'edge_attr_20': 6.135,
     'edge_attr_3': 4.402,
     'edge_weight': 5.735,
     'L0_gnn_W_in2f_s': 4.475,
     'L0_gnn_W_in2f_v': 3.918,
     'L0_gnn_Wf1': 3.073,
     'L0_gnn_bf1': 8.0,
     'L0_gnn_Wf2': 3.048,
     'L0_gnn_bf2': 8.0,
     'L0_gnn_W1_s': 8.0,
     'L0_gnn_W1_v': 3.016,
     'L0_gnn_W2_s': 8.0,
     'L0_gnn_W2_v': 2.955,
     'L1_gnn_Wq': 200.0,
     'L1_gnn_bq': 200.0,
     'L1_gnn_bkv': 176.512,
     'L1_gnn_Wkv': 8.0,
     'L1_gnn_Wo': 8.0,
     'L1_gnn_bo': 64.0}
    for name, (base, spread) in spreads.items():
        noise = np.random.default_rng([zlib.crc32(name.encode()), seed]).standard_normal(out[name].shape)
        drawn = base * np.exp(spread * noise) if base else spread * noise
        out[name] = jnp.asarray(drawn.astype(out[name].dtype))
    for name, factor in factors.items():
        out[name] = (out[name] * factor).astype(out[name].dtype)
    return out
```

```python
import math

import numpy as np

import concourse.bass as bass
from concourse import mybir
from contextlib import ExitStack

P = 128
N = 10000
E = 2500
D = 512
C = 128
H = 8
DH = D // H
NRBF = 20
NT = 20
EP = NT * P
G = P - 1
ROWS = EP + 1
KW = G * NT + 1
NONE = N
NOROW = 30000
OFF = 20000
PEEL = 4
CH = 1024
FLAT = N * D // P
EPS = 1e-5
Y0 = 1.0 / math.sqrt(4.0 * math.pi)
Y1 = math.sqrt(3.0 / (4.0 * math.pi))
BIG = 3.0e38


def wait(eng, sem, n):
    if isinstance(n, int) and n <= 0:
        return
    eng.wait_ge(sem, n)


def dma_count(t, b):
    return 8 * (t - b) + 16


def apart(eng, made, *values):
    for v in values:
        if not isinstance(v, int):
            eng.lower_val(v)
    eng.wait_ge(made, 8)


def real(t):
    return not isinstance(t, int) or 0 <= t < NT


def chunk_width(c):
    return FLAT - c * CH if isinstance(c, int) and c == 2 * NT - 1 else CH


def over_tiles(eng, lag, step):
    for tau in range(PEEL):
        step(tau, tau % 2)
    with eng.Fori(0, (NT - PEEL) // 2) as k:
        step(2 * k + PEEL, 0)
        step(2 * k + PEEL + 1, 1)
    for tau in range(NT, NT + lag):
        step(tau, tau % 2)


def gnn_kernel(nc, x, src_row, dst_row, src_cols, edge_cols, f_t, rcut_cols, r_cols,
               w_s, w_v, wf1, bf1, wf2, bf2, w1s, w1v_t, w2s, w2v,
               wq, bq, wk, bk, wv, bv, wo, bo2, out,
               psort, skey, drec, table, x1c):
    f32 = mybir.dt.float32
    i32 = mybir.dt.int32
    bf16 = mybir.dt.bfloat16
    ALU = mybir.AluOpType
    ACT = mybir.ActivationFunctionType
    AX = mybir.AxisListType

    RC, RF = 1.0 / math.sqrt(C), 1.0 / math.sqrt(2 * C)
    SC_A = Y0 * RC * RF
    SC_B = Y1 / math.sqrt(3.0) * RC * RF
    SC_C = Y1 * RC * RF * RC
    SC_D = Y0 * RC * RF * RC
    SC_S2 = RC
    SCALE = 1.0 / math.sqrt(DH)

    x_flat = x.rearrange("n d -> (n d)").rearrange("(p f) -> p f", p=P)
    out_flat = out.rearrange("n d -> (n d)").rearrange("(p f) -> p f", p=P)

    ctx = ExitStack()
    with ctx:
        def sb(name, shape, dt=f32):
            return ctx.enter_context(nc.sbuf_tensor(name, shape, dt))

        def pb(name, shape, dt=f32):
            return ctx.enter_context(nc.psum_tensor(name, shape, dt))

        def sem(name):
            return ctx.enter_context(nc.semaphore(name))

        def pair(name, shape, dt=f32):
            return [sb(f"{name}{b}", shape, dt) for b in range(2)]

        def sems(name):
            return [sem(f"{name}{b}") for b in range(2)]

        WT = sb("WT", [P, 4, EP])
        records = WT[:, :, :].bitcast(i32).rearrange("p k e -> p (k e)")[:, 0:2 * (KW + 1)]
        XO = sb("XO", [P, NT, D])
        f_sb = XO[0:NRBF, 0:5, :].rearrange("p a d -> p (a d)")
        row_i = XO[:, 10:15, :].bitcast(i32).rearrange("p a d -> p (a d)")
        row_d = XO[:, 15:20, :].bitcast(i32).rearrange("p a d -> p (a d)")

        WA = sb("WA", [P, 4, 4, D])
        wq_sb, wk_sb, wv_sb, wo_sb = (WA[:, k] for k in range(4))
        early = WA[:, 3].rearrange("p k d -> p (k d)")
        w_s_sb, w_v_sb, w1v_t_sb, w1vt_b_sb, w2v_sb, wva, wvb = (early[:, k * C:(k + 1) * C] for k in range(7))
        wf2_sb = early[:, 7 * C:11 * C].rearrange("p (k c) -> p k c", k=4)
        w1s_sb = early[:, 11 * C:13 * C].rearrange("p (k c) -> p k c", k=2)
        w2s_sb = sb("w2s_sb", [P, C])
        wf1_sb = sb("wf1_sb", [NRBF, C])
        bf1_sb = sb("bf1_sb", [P, 1])
        bf2_sb = sb("bf2_sb", [P, 4])
        bq_sb, bk_sb, bv_sb, bo_sb = (sb(n, [P, D]) for n in ("bq_sb", "bk_sb", "bv_sb", "bo_sb"))
        bo_rot = sb("bo_rot", [P, D])

        key_row = sb("key_row", [P, EP])
        key_col_i = sb("key_col_i", [P, NT], i32)
        edge_i = sb("edge_i", [P, NT, 2], i32)
        tile_no = sb("tile_no", [P, NT])
        tile_row = tile_no[:, :].unsqueeze(2).broadcast_to([P, NT, P])
        skey_col, dkey_col = sb("skey_col", [P, NT]), sb("dkey_col", [P, NT])
        xidx = sb("xidx", [P, NT], i32)
        junk_f = sb("junk_f", [P, EP // 2])
        junk = junk_f[:, :].bitcast(bf16)
        junk_t = sb("junk_t", [P, P], bf16)
        count, ties = pair("count", [P, 1]), pair("ties", [P, 1])
        rank_s, rank_d = sb("rank_s", [P, NT], i32), sb("rank_d", [P, NT], i32)
        sk_f = sb("sk_f", [P, KW + 1])
        dk_f = key_row[:, 0:KW + 1]
        ko_i, kn_i = sb("ko_i", [P, NT, 2], i32), sb("kn_i", [P, NT, 2], i32)
        sk_c, dk_c = sb("sk_c", [P, NT]), sb("dk_c", [P, NT])
        kn_f = sb("kn_f", [P, NT])
        cont = sb("cont", [P, NT])
        srow_i, drow_i = sb("srow_i", [P, NT], i32), sb("drow_i", [P, NT], i32)
        sx_i, dx_i, ds_i = sb("sx_i", [P, NT], i32), sb("dx_i", [P, NT], i32), sb("ds_i", [P, NT], i32)
        slot_i = sb("slot_i", [P, NT], i32)

        mask = pair("mask", [P, P])
        dist = mask[0]
        ident, upto, before = sb("ident", [P, P]), sb("upto", [P, P]), sb("before", [P, P])
        eps = sb("eps", [P, 1])
        half = sb("half", [P, 1])
        zero_row = sb("zero_row", [1, D])
        none_i = sb("none_i", [1, 2], i32)
        norow_i = XO[:, 5, 0:80].bitcast(i32)

        rcut = sb("rcut", [P, NT])
        r_sb, r_sq, u, ur = (sb(n, [P, NT, 3]) for n in ("r_sb", "r_sq", "u", "ur"))
        rn2, rn = sb("rn2", [P, NT]), sb("rn", [P, NT])

        st, mv = pair("st", [P, 12]), pair("mv", [P, 4])
        std, rstd, nb = pair("std", [P, 2]), pair("rstd", [P, 2]), pair("nb", [P, 2])
        h = pair("h", [P, D])
        hd = pair("hd", [P, C])
        hT = pair("hT", [P, 5 * C])
        M = pair("M", [P, 6, C])
        Pt = pair("Pt", [P, D])
        Dr = pair("Dr", [P, 3 * C])
        xg = pair("xg", [P, D])
        base = pair("base", [P, CH + 2 * H])
        fz, fe = sb("fz", [P, 2, D]), sb("fe", [P, 2, D])
        hid = sb("hid", [P, 2, D])
        sz, se, sp = ([Dr[b][:, k * C:(k + 1) * C] for b in range(2)] for k in range(3))

        hTd = [M[b][:, 0:4, :].rearrange("p k c -> p (k c)") for b in range(2)]
        hTs = [hT[b][:, 0:D] for b in range(2)]
        hs = [fe[:, b, :] for b in range(2)]
        late = WT[:, :, :].rearrange("p k e -> p (k e)")[:, 4 * EP - 4 * D:]
        xd, xb = ([late[:, (2 * k + b) * D:(2 * k + b + 1) * D] for b in range(2)] for k in range(2))
        qs, ks = [fz[:, 0, :]] * 2, [fz[:, 1, :]] * 2
        td0, td1, ts0, ts1 = (sb(n, [P, 1], i32) for n in ("td0", "td1", "ts0", "ts1"))
        a_sb = pair("a_sb", [P, H])
        aT, mT, eT = pair("aT", [H, P]), pair("mT", [H, P]), pair("eT", [H, P])
        same = sk_f[0:H, :]
        same_back = before[0:H, :]
        ex = pair("ex", [P, H])
        va = [base[b][:, D:2 * D + H] for b in range(2)]
        vw = [junk_f[:, b * (D + H):(b + 1) * (D + H)] for b in range(2)]
        rden = pair("rden", [P, H])
        o_sb = [hid[:, b, :] for b in range(2)]
        oT = [base[b][:, 0:D] for b in range(2)]
        y = Pt

        banks = [pb(f"bank{i}", [P, 512]) for i in range(8)]

        uses = {"xa": 1, "ra": 1, "pa": 1, "ka": 1, "xb": 1, "rb": 1, "eb": 2, "tb": 1, "slot": 1, "xc": 1, "sc": 1, "oc": 1}
        idx_all = sb("idx_all", [P, 2 * sum(uses.values())], i32)
        idx, at = {}, 0
        for n, k in uses.items():
            idx[n] = [idx_all[:, at + b * k:at + (b + 1) * k] for b in range(2)]
            at += 2 * k

        g_idx = {n: sem("g_idx_" + n) for n in uses}
        d_row, d_cols, d_const = sem("d_row"), sem("d_cols"), sem("d_const")
        d_wf, d_wl0, d_wl1 = sem("d_wf"), sem("d_wl0"), sem("d_wl1")
        d_rowd = sem("d_rowd")
        d_init = sem("d_init")
        g_const = sem("g_const")
        v_const = sem("v_const")
        v_keys = sem("v_keys")
        s_keys = sem("s_keys")
        v_unit, s_unit = sem("v_unit"), sem("s_unit")
        p_wv, v_wv = sem("p_wv"), sem("v_wv")
        p_pre, s_z, v_neg, s_exp, s_ln, v_hid, p_filt, s_filt = (
            sem(n) for n in ("p_pre", "s_z", "v_neg", "s_exp", "s_ln", "v_hid", "p_filt", "s_filt"))
        base_in, base_out, g_base = sems("base_in"), sems("base_out"), sem("g_base")
        a_x = sems("a_x")
        av_stats, av_mom, as_std, av_rstd, av_nb, as_h, av_hd, ap_T, as_hT, ap_X, av_M, ap_O, as_D, as_S, av_P = (
            sem(n) for n in ("av_stats", "av_mom", "as_std", "av_rstd", "av_nb", "as_h", "av_hd", "ap_T",
                             "as_hT", "ap_X", "av_M", "ap_O", "as_D", "as_S", "av_P"))
        av_count, av_rank = sem("av_count"), sem("av_rank")
        av_hdp = sem("av_hdp")
        a_scat = sems("a_scat")
        a_skey = sems("a_skey")
        d_sk, bv_sk = sem("d_sk"), sem("bv_sk")
        b_x, b_P = sems("b_x"), sems("b_P")
        bv_mask, bv_carry, bp_cum, bp_st, bv_neg, bv_pos, bs_exp, bs_ln, bv_sp, bp_s2, bv_x1, bg_xo = (
            sem(n) for n in ("bv_mask", "bv_carry", "bp_cum", "bp_st", "bv_neg", "bv_pos", "bs_exp", "bs_ln",
                             "bv_sp", "bp_s2", "bv_x1", "bg_xo"))
        bv_count, bv_rank = sem("bv_count"), sem("bv_rank")
        b_x1c = sems("b_x1c")
        b_drec, b_table = sems("b_drec"), sems("b_table")
        g_ones = sem("g_ones")
        d_dk, cv_dk, cg_src = sem("d_dk"), sem("cv_dk"), sem("cg_src")
        c_x, c_td, c_ts, c_xd, c_xs, c_out = (sems(n) for n in ("c_x", "c_td", "c_ts", "c_xd", "c_xs", "c_out"))
        (cv_stats, cv_mom, cs_std, cv_rstd, cv_nb, cs_hd, cs_hs, cp_Td, cs_hTd, cp_Ts, cv_hTs,
         cp_q, cp_k, cp_v, cv_q, cv_k, cv_prod, cv_a, cp_aT, cs_aT, cv_fwd, cv_bwd, cv_e, cp_E, cs_ex, cv_mask,
         cv_v, cv_carry, cv_vw, cp_cum, cv_den, cv_rden, cv_o, cp_oT, cs_oT, cp_y, cv_y, cg_y) = (
            sem("c_" + n) for n in (
                "stats mom std rstd nb hd hs Td hTd Ts hTs q k v qs ks prod a aTp aTs fwd bwd e E ex mask "
                "vs carry vw cum den rden o oTp oTs yp yv yg").split())

        block = ctx.enter_context(nc.Block())

        @block.sync
        def _(sp_):
            eng = sp_
            eng.dma_start(row_i[:, :], src_row.partition_broadcast(P)).then_inc(d_row, 16)
            eng.dma_start(edge_i[:, :, :], edge_cols).then_inc(d_cols, 16)
            eng.dma_start(key_col_i[:, :], src_cols).then_inc(d_cols, 16)
            eng.dma_start(f_sb, f_t).then_inc(d_wf, 16)
            eng.dma_start(wf1_sb[:, :], wf1).then_inc(d_wf, 16)
            eng.dma_start(bf1_sb[:, :], bf1).then_inc(d_wf, 16)
            eng.dma_start(wf2_sb[:, :, :], wf2).then_inc(d_wf, 16)
            eng.dma_start(bf2_sb[:, :], bf2).then_inc(d_wf, 16)
            eng.dma_start(rcut[:, :], rcut_cols).then_inc(d_wl0, 16)
            eng.dma_start(r_sb[:, :, :], r_cols).then_inc(d_wl0, 16)
            for dst, src in ((w_s_sb, w_s), (w_v_sb, w_v), (w1v_t_sb, w1v_t[0]), (w1vt_b_sb, w1v_t[1]),
                             (w2s_sb, w2s), (w2v_sb, w2v)):
                eng.dma_start(dst[:, :], src).then_inc(d_wl0, 16)
            eng.dma_start(w1s_sb[:, :, :], w1s).then_inc(d_wl0, 16)
            eng.dma_start(bo_rot[:, :], bass.AP(bo2.tensor, 0, [[0, P // 8], [D // 8, 8], [1, D]]))\
               .then_inc(d_const, 16)
            eng.wait_ge(g_const, 8)
            eng.dma_start(psort[0:1, :], zero_row[:, :]).then_inc(d_init, 16)
            eng.dma_start(skey[0:1, :], none_i[:, 0:1]).then_inc(d_init, 16)
            eng.dma_start(drec[0:1, :], none_i[:, :]).then_inc(d_init, 16)
            eng.dma_start(table.rearrange("(p f) one -> p (f one)", p=P), norow_i).then_inc(d_init, 16)
            eng.dma_start(row_d[:, :], dst_row.partition_broadcast(P)).then_inc(d_rowd, 16)
            for dst, src in ((wq_sb, wq), (wk_sb, wk), (wv_sb, wv)):
                eng.dma_start(dst, src).then_inc(d_wl1, 16)
            for dst, src in ((bq_sb, bq), (bk_sb, bk), (bv_sb, bv), (bo_sb, bo2[:, 0:D])):
                eng.dma_start(dst[:, :], src.partition_broadcast(P)).then_inc(d_wl1, 16)

            def base_load(c, b):
                w = chunk_width(c)
                wait(eng, base_out[b], dma_count(c - 2, b))
                eng.dma_start(base[b][:, 0:w], x_flat[:, bass.ds(c * CH, w)]).then_inc(base_in[b], 16)

            def base_store(c, b):
                w = chunk_width(c)
                wait(eng, g_base, c + 1)
                eng.dma_start(out_flat[:, bass.ds(c * CH, w)], base[b][:, 0:w]).then_inc(base_out[b], 16)

            def step_a(tau, b):
                if real(tau):
                    base_load(tau, b)
                if real(tau - 1):
                    base_store(tau - 1, 1 - b)
            over_tiles(eng, 2, step_a)

            for b in range(2):
                eng.wait_ge(a_skey[b], 8 * NT)
            with nc.allow_non_contiguous_dma(reason="columns of keys"):
                eng.dma_start(ko_i[:, :, 0], bass.AP(skey.tensor, 0, [[1, P], [G, NT]])).then_inc(d_sk, 16)
                eng.dma_start(kn_i[:, :, 0], bass.AP(skey.tensor, 1, [[1, P], [G, NT]])).then_inc(d_sk, 16)
            eng.wait_ge(bv_sk, 1)
            eng.dma_start(row_i[:, 0:KW + 1], bass.AP(skey.tensor, 0, [[0, P], [1, KW + 1]])).then_inc(d_sk, 16)
            for b in range(2):
                eng.wait_ge(a_scat[b], 8 * NT)
            eng.wait_ge(d_init, 64)
            eng.dma_start(wo_sb, wo).then_inc(d_wl1, 16)

            def step_b(tau, b):
                if real(tau):
                    wait(eng, bp_st, tau - 1)
                    eng.dma_start(Pt[b][:, :], psort[bass.ds(G * tau, P), :]).then_inc(b_P[b], 16)
                if real(tau - 2):
                    base_load(tau - 2 + NT, b)
                    if not isinstance(tau, int) or tau > 2:
                        base_store(tau - 3 + NT, 1 - b)
                    wait(eng, bv_x1, tau - 1)
                    eng.dma_start(x1c[bass.ds(P * (tau - 2), P), :], XO[:, tau - 2, :]).then_inc(b_x1c[b], 16)
            over_tiles(eng, 2, step_b)
            base_store(2 * NT - 1, 1)

            for b in range(2):
                eng.wait_ge(b_drec[b], 8 * NT)
            with nc.allow_non_contiguous_dma(reason="columns of keys"):
                eng.dma_start(ko_i[:, :, :], bass.AP(drec.tensor, 0, [[2, P], [2 * G, NT], [1, 2]]))\
                   .then_inc(d_dk, 16)
                eng.dma_start(kn_i[:, :, :], bass.AP(drec.tensor, 2, [[2, P], [2 * G, NT], [1, 2]]))\
                   .then_inc(d_dk, 16)
            eng.dma_start(records,
                          bass.AP(drec.tensor, 0, [[0, P], [1, 2 * (KW + 1)]])).then_inc(d_dk, 16)
            for b in range(2):
                eng.wait_ge(base_out[b], 16 * NT)
                eng.wait_ge(b_x1c[b], 8 * NT)
                eng.wait_ge(c_out[b], 8 * NT)

        @block.gpsimd
        def _(eng):
            eng.iota(dist[:, :], [[1, P]], base=0, channel_multiplier=-1,
                     allow_small_or_imprecise_dtypes=True).then_inc(g_const, 1)
            eng.memset(zero_row[:, :], 0.0).then_inc(g_const, 1)
            eng.memset(none_i[:, :], NONE).then_inc(g_const, 1)
            eng.memset(eps[:, :], EPS).then_inc(g_const, 1)
            eng.memset(half[:, :], 0.5).then_inc(g_const, 1)
            eng.memset(norow_i, NOROW).then_inc(g_const, 1)
            eng.iota(slot_i[:, :], [[P, NT]], base=0, channel_multiplier=1).then_inc(g_const, 1)
            eng.iota(tile_no[:, :], [[1, NT]], base=0, channel_multiplier=0,
                     allow_small_or_imprecise_dtypes=True).then_inc(g_const, 1)

            def wait_apart(eng, s, n):
                if not isinstance(n, int):
                    apart(eng, g_const, n)
                wait(eng, s, n)

            def gather(dst, src, idx, rows, s):
                eng.indirect_dma_start(out=dst, out_offset=None, in_=src,
                                       in_offset=bass.IndirectOffsetOnAxis(ap=idx, axis=0),
                                       bounds_check=rows - 1, oob_is_err=False).then_inc(s, 16)

            def scatter(dst, idx, src, rows, s):
                eng.indirect_dma_start(out=dst, out_offset=bass.IndirectOffsetOnAxis(ap=idx, axis=0),
                                       in_=src, in_offset=None,
                                       bounds_check=rows - 1, oob_is_err=False).then_inc(s, 16)

            def pick(name, t, b, column, users):
                s = g_idx[name]
                for u_ in users:
                    wait_apart(eng, u_[b], dma_count(t - 2, b))
                eng.tensor_copy(idx[name][b][:, :], column[:, t] if len(column.shape) == 3
                                else column[:, bass.ds(t, 1)]).then_inc(s, 1)
                wait_apart(eng, s, t + 1)
                return idx[name][b][:, :]

            def base_add(c, b):
                width = chunk_width(c)
                wait_apart(eng, base_in[b], dma_count(c, b))
                k = max(width // D, 1)
                v = base[b][:, 0:width].rearrange("p (k d) -> p k d", k=k)
                w = min(width, D)
                eng.tensor_tensor(v, v, bo_rot[:, 0:w].unsqueeze(1).broadcast_to([P, k, w]), ALU.add)\
                   .then_inc(g_base, 1)

            eng.wait_ge(v_keys, 2)
            eng.wait_ge(d_const, 16)
            eng.wait_ge(d_init, 64)

            def step_a(tau, b):
                if real(tau):
                    wait_apart(eng, as_h, tau - 1)
                    gather(xg[b][:, :], x, pick("xa", tau, b, xidx, [a_x]), N, a_x[b])
                if real(tau - 2):
                    wait_apart(eng, av_P, tau - 1)
                    wait_apart(eng, as_S, tau - 1)
                    scatter(psort, pick("pa", tau - 2, b, rank_s, [a_scat]), Pt[b][:, :], ROWS, a_scat[b])
                if real(tau):
                    wait_apart(eng, av_rank, tau + 1)
                    scatter(skey, pick("ra", tau, b, rank_s, [a_skey]),
                            pick("ka", tau, b, key_col_i, [a_skey]), ROWS, a_skey[b])
                    base_add(tau, b)
            over_tiles(eng, 2, step_a)

            eng.wait_ge(bv_sk, 3)
            eng.wait_ge(d_wl1, 128)

            def step_b(tau, b):
                if real(tau):
                    wait_apart(eng, bv_x1, tau - 1)
                    gather(xg[b][:, :], x, pick("xb", tau, b, sx_i, [b_x]), N, b_x[b])
                    wait_apart(eng, bv_rank, tau + 1)
                    scatter(drec, pick("rb", tau, b, rank_d, [b_drec]),
                            pick("eb", tau, b, edge_i, [b_drec]), ROWS, b_drec[b])
                    scatter(table, pick("tb", tau, b, srow_i, [b_table]),
                            pick("slot", tau, b, slot_i, [b_table]), N, b_table[b])
                if real(tau - 2):
                    base_add(tau - 2 + NT, b)
            over_tiles(eng, 2, step_b)
            for t in range(NT):
                wait_apart(eng, b_x1c[t % 2], dma_count(t, t % 2))
                eng.tensor_tensor(XO[:, t, :], XO[:, t, :], bo_sb[:, :], ALU.add).then_inc(bg_xo, 1)

            eng.wait_ge(cv_dk, 2)
            for b in range(2):
                eng.wait_ge(b_table[b], 8 * NT)
                eng.wait_ge(b_x1c[b], 8 * NT)

            for b in range(2):
                eng.memset(va[b][:, D:D + H], 1.0).then_inc(g_ones, 1)

            td, ts = (td0, td1), (ts0, ts1)

            def lookups(t, b):
                dst_rows = pick("xc", t, b, dx_i, [c_x, c_td])
                gather(xd[b][:, :], x, dst_rows, N, c_x[b])
                gather(td[b][:, :], table, dst_rows, N, c_td[b])
                gather(ts[b][:, :], table, pick("sc", t, b, ds_i, [c_ts]), N, c_ts[b])

            def updated(t, b):
                wait_apart(eng, c_x[b], dma_count(t, b))
                wait_apart(eng, c_td[b], dma_count(t, b))
                gather(xd[b][:, :], x1c, td[b][:, :], EP, c_xd[b])
                wait_apart(eng, c_ts[b], dma_count(t, b))
                gather(xg[b][:, :], x1c, ts[b][:, :], EP, c_xs[b])

            def step_c(tau, b):
                if real(tau - 1):
                    updated(tau - 1, 1 - b)
                if real(tau - 2):
                    t = tau - 2
                    wait_apart(eng, cv_y, t - 1)
                    wait_apart(eng, c_xd[b], dma_count(t, b))
                    eng.tensor_tensor(xb[b][:, :], xd[b][:, :], bo_sb[:, :], ALU.add).then_inc(cg_y, 1)
                if real(tau):
                    wait_apart(eng, cs_hs, tau - 1)
                    wait_apart(eng, cg_y, tau - 1)
                    lookups(tau, b)
                if real(tau - 4):
                    t = tau - 4
                    wait_apart(eng, cv_y, t + 1)
                    scatter(out, pick("oc", t, b, drow_i, [c_out]), y[b][:, :], N, c_out[b])
                if isinstance(tau, int) and tau == 1:
                    eng.wait_ge(bg_xo, NT)
                    for b in range(2):
                        eng.wait_ge(base_out[b], 16 * NT)
                    for t in range(NT):
                        scatter(out, srow_i[:, t:t + 1], XO[:, t, :], N, cg_src)
                    eng.wait_ge(cg_src, 16 * NT)
            over_tiles(eng, 4, step_c)
            for b in range(2):
                eng.wait_ge(c_out[b], 8 * NT)

        @block.scalar
        def _(eng):
            eng.wait_ge(v_unit, 1)
            eng.activation(rn[:, :], rn2[:, :], ACT.Sqrt).then_inc(s_unit, 1)
            eng.wait_ge(g_const, 8)
            for c in range(EP // D):
                eng.wait_ge(v_neg, c + 1)
                eng.activation(fe[:, c % 2, :], fe[:, c % 2, :], ACT.Exp).then_inc(s_exp, 1)
                eng.wait_ge(s_exp, c + 1)
                eng.activation(fe[:, c % 2, :], fe[:, c % 2, :], ACT.Ln, bias=half[:, :], scale=0.5)\
                   .then_inc(s_ln, 1)
                for k in range(4):
                    eng.wait_ge(p_filt, 4 * c + k + 1)
                    eng.activation(WT[:, k, c * D:(c + 1) * D], banks[2 + k][:, :], ACT.Identity,
                                   bias=bf2_sb[:, k:k + 1]).then_inc(s_filt, 1)

            def step_a(tau, b):
                if real(tau):
                    wait(eng, av_mom, tau + 1)
                    eng.activation(std[b][:, 0:1], mv[b][:, 1:2], ACT.Sqrt, bias=eps[:, :]).then_inc(as_std, 1)
                    wait(eng, av_nb, tau + 1)
                    wait(eng, ap_T, tau - 1)
                    eng.activation(h[b][:, :], xg[b][:, :], ACT.Relu, bias=nb[b][:, 0:1],
                                   scale=rstd[b][:, 0:1]).then_inc(as_h, 1)
                if real(tau - 2):
                    t = tau - 2
                    apart(eng, g_const, t + 1, t - 1)
                    wait(eng, ap_O, t + 1)
                    wait(eng, av_P, t - 1)
                    eng.activation(Dr[b][:, :], banks[4][:, 0:3 * C], ACT.Copy,
                                   scale=rcut[:, bass.ds(t, 1)]).then_inc(as_D, 1)
                    apart(eng, g_const, dma_count(t - 2, b))
                    wait(eng, a_scat[b], dma_count(t - 2, b))
                    eng.activation(Pt[b][:, 0:C], banks[4][:, 3 * C:4 * C], ACT.Copy,
                                   scale=rcut[:, bass.ds(t, 1)]).then_inc(as_S, 1)
                if real(tau):
                    wait(eng, ap_T, tau + 1)
                    wait(eng, ap_X, tau - 1)
                    eng.activation(hT[b][:, 0:C], banks[1][:, 0:C], ACT.Copy)
                    eng.activation(hT[b][:, C:5 * C], banks[0][:, :], ACT.Copy).then_inc(as_hT, 1)
            over_tiles(eng, 2, step_a)

            def step_b(tau, b):
                if real(tau - 1):
                    t, q = tau - 1, 1 - b
                    wait(eng, bv_neg, t + 1)
                    eng.activation(se[q][:, :], se[q][:, :], ACT.Exp).then_inc(bs_exp, 1)
                    wait(eng, bs_exp, t + 1)
                    eng.activation(se[q][:, :], se[q][:, :], ACT.Ln, bias=half[:, :], scale=0.5)\
                       .then_inc(bs_ln, 1)
            over_tiles(eng, 2, step_b)

            def step_c(tau, b):
                if real(tau):
                    wait(eng, cv_mom, 2 * (tau + 1))
                    eng.activation(std[b][:, :], mv[b][:, 1:4:2], ACT.Sqrt, bias=eps[:, :]).then_inc(cs_std, 1)
                    wait(eng, cv_nb, tau + 1)
                    wait(eng, cp_Td, tau - 1)
                    eng.activation(h[b][:, :], xd[b][:, :], ACT.Relu, bias=nb[b][:, 0:1],
                                   scale=rstd[b][:, 0:1]).then_inc(cs_hd, 1)
                    wait(eng, cp_Ts, tau - 1)
                    eng.activation(hs[b], xg[b][:, :], ACT.Relu, bias=nb[b][:, 1:2],
                                   scale=rstd[b][:, 1:2]).then_inc(cs_hs, 1)
                if real(tau - 2):
                    wait(eng, cp_E, tau - 1)
                    eng.activation(ex[b][:, :], banks[5][:, P:P + H], ACT.Exp).then_inc(cs_ex, 1)
                if real(tau):
                    wait(eng, cp_Td, tau + 1)
                    wait(eng, cp_q, tau - 1)
                    eng.activation(hTd[b], banks[0][:, :], ACT.Copy).then_inc(cs_hTd, 1)
                if real(tau - 2):
                    wait(eng, cp_oT, tau - 1)
                    wait(eng, cp_y, tau - 3)
                    eng.activation(oT[b][:, :], banks[6][:, :], ACT.Copy).then_inc(cs_oT, 1)
                if real(tau - 1):
                    t, q = tau - 1, 1 - b
                    wait(eng, cp_aT, t + 1)
                    wait(eng, cv_e, t - 1)
                    first = 0 if isinstance(t, int) and t == 0 else 1
                    eng.activation(aT[q][:, first:P], banks[5][0:H, first:P], ACT.Copy, scale=SCALE)\
                       .then_inc(cs_aT, 1)
            over_tiles(eng, 2, step_c)

        @block.tensor
        def _(eng):
            eng.wait_ge(d_wl0, 144)
            eng.matmul(banks[0][:, 0:C], w1v_t_sb[:, :], w2v_sb[:, :], start=True, stop=True)
            eng.matmul(banks[0][:, C:2 * C], w1vt_b_sb[:, :], w2v_sb[:, :], start=True, stop=True).then_inc(p_wv, 1)
            eng.wait_ge(d_wf, 80)

            def pre(c):
                wait(eng, v_neg, c - 1)
                eng.matmul(banks[6 + c % 2][:, :], wf1_sb[:, :], f_sb[:, c * D:(c + 1) * D],
                           start=True, stop=True).then_inc(p_pre, 1)
            pre(0)
            for c in range(EP // D):
                if c + 1 < EP // D:
                    pre(c + 1)
                eng.wait_ge(v_hid, c + 1)
                for k in range(4):
                    wait(eng, s_filt, 4 * (c - 1) + k + 1)
                    eng.matmul(banks[2 + k][:, :], wf2_sb[:, k, :], hid[:, c % 2, :],
                               start=True, stop=True).then_inc(p_filt, 1)
            eng.wait_ge(s_filt, EP // D * 4)
            eng.wait_ge(v_wv, 1)
            eng.wait_ge(v_const, 3)

            def step_a(tau, b):
                if real(tau - 1):
                    t, q = tau - 1, 1 - b
                    wait(eng, as_hT, t + 1)
                    wait(eng, av_M, t)
                    eng.matmul(banks[3][:, 0:C], w_s_sb[:, :], hT[q][:, 0:C], start=True, stop=True)
                    eng.matmul(banks[2][:, :], w_v_sb[:, :], hT[q][:, C:5 * C], start=True, stop=True)\
                       .then_inc(ap_X, 1)
                if real(tau - 2):
                    t = tau - 2
                    wait(eng, av_M, t + 1)
                    wait(eng, as_S, t)
                    wait(eng, av_P, t)
                    for i in range(3):
                        eng.matmul(banks[4][:, i * C:(i + 1) * C], M[b][:, 3 + i, :], wvb[:, :],
                                   start=True, stop=True)
                    eng.matmul(banks[4][:, 3 * C:4 * C], M[b][:, 0, :], w1s_sb[:, 0, :], start=True, stop=False)
                    eng.matmul(banks[4][:, 3 * C:4 * C], M[b][:, 1, :], w1s_sb[:, 1, :], start=False, stop=True)
                    eng.matmul(banks[5][:, 0:C], M[b][:, 2, :], wva[:, :], start=True, stop=True)\
                       .then_inc(ap_O, 1)
                if real(tau):
                    wait(eng, as_h, tau + 1)
                    wait(eng, as_hT, tau)
                    eng.transpose(banks[1][:, 0:C], h[b][:, 0:C], ident[:, :])
                    hv = h[b][:, C:4 * C].rearrange("p (c i) -> p i c", i=3)
                    for i in range(3):
                        eng.transpose(banks[0][:, i * C:(i + 1) * C], hv[:, i, :], ident[:, :])
                    wait(eng, av_hd, tau + 1)
                    eng.transpose(banks[0][:, 3 * C:4 * C], hd[b][:, :], ident[:, :]).then_inc(ap_T, 1)
            over_tiles(eng, 2, step_a)

            def step_b(tau, b):
                if real(tau - 1):
                    t, q = tau - 1, 1 - b
                    wait(eng, bv_mask, t + 1)
                    wait(eng, b_P[q], dma_count(t, q))
                    wait(eng, bv_carry, t + 1)
                    wait(eng, bv_x1, t - 1)
                    eng.matmul(banks[q][:, :], mask[q][:, :], Pt[q][:, :], start=True, stop=True).then_inc(bp_cum, 1)
                    wait(eng, bv_neg, t)
                    eng.matmul(banks[2][:, 0:P], Pt[q][:, 0:C], mask[q][:, :], start=True, stop=True)\
                       .then_inc(bp_st, 1)
                if real(tau - 2):
                    t = tau - 2
                    wait(eng, bv_sp, t + 1)
                    wait(eng, bv_x1, t)
                    eng.matmul(banks[3][:, 0:C], sp[b][:, :], w2s_sb[:, :], start=True, stop=True).then_inc(bp_s2, 1)
            over_tiles(eng, 2, step_b)
            eng.wait_ge(d_wl1, 128)

            def project(bank, hT_, w, s):
                for k in range(4):
                    last = eng.matmul(bank[:, :], hT_[:, k * C:(k + 1) * C], w[:, k, :], start=(k == 0), stop=(k == 3))
                last.then_inc(s, 1)

            def step_c(tau, b):
                if real(tau - 1):
                    t, q = tau - 1, 1 - b
                    wait(eng, cs_hTd, t + 1)
                    wait(eng, cv_q, t)
                    project(banks[1], hTd[q], wq_sb, cp_q)
                if real(tau - 2):
                    apart(eng, g_const, tau - 1)
                    wait(eng, cv_e, tau - 1)
                    wait(eng, cs_aT, tau - 1)
                    eng.transpose(banks[5][:, P:P + H], eT[b][:, :], ident[0:H, 0:H]).then_inc(cp_E, 1)
                if real(tau - 1):
                    wait(eng, cv_hTs, t + 1)
                    wait(eng, cv_k, t)
                    project(banks[2], hTs[q], wk_sb, cp_k)
                if real(tau - 2):
                    t2 = tau - 2
                    wait(eng, cv_vw, t2 + 1)
                    wait(eng, cv_carry, t2 + 1)
                    wait(eng, cv_y, t2)
                    wait(eng, cv_o, t2)
                    eng.matmul(banks[4][:, :], mask[b][:, :], vw[b][:, 0:D], start=True, stop=True)
                    eng.matmul(banks[7][:, 0:H], mask[b][:, :], vw[b][:, D:D + H], start=True, stop=True)\
                       .then_inc(cp_cum, 1)
                if real(tau):
                    wait(eng, cs_hd, tau + 1)
                    wait(eng, cv_hTs, tau)
                    for k in range(4):
                        last = eng.transpose(banks[0][:, k * C:(k + 1) * C], h[b][:, k * C:(k + 1) * C], ident[:, :])
                    last.then_inc(cp_Td, 1)
                if real(tau - 1):
                    wait(eng, cv_v, t)
                    project(banks[3], hTs[q], wv_sb, cp_v)
                if real(tau):
                    wait(eng, cs_hs, tau + 1)
                    wait(eng, cs_hTd, tau + 1)
                    for k in range(4):
                        last = eng.transpose(banks[0][:, k * C:(k + 1) * C], hs[b][:, k * C:(k + 1) * C], ident[:, :])
                    last.then_inc(cp_Ts, 1)
                if real(tau - 2):
                    wait(eng, cv_o, t2 + 1)
                    wait(eng, cs_oT, t2)
                    for k in range(4):
                        last = eng.transpose(banks[6][:, k * C:(k + 1) * C], o_sb[b][:, k * C:(k + 1) * C], ident[:, :])
                    last.then_inc(cp_oT, 1)
                if real(tau - 1):
                    wait(eng, cv_a, t + 1)
                    wait(eng, cs_ex, t)
                    eng.transpose(banks[5][0:H, 0:P], a_sb[q][:, :], ident[:, :]).then_inc(cp_aT, 1)
                if real(tau - 2):
                    wait(eng, cs_oT, t2 + 1)
                    if not isinstance(t2, int) or t2 < NT - 1:
                        wait(eng, cv_carry, t2 + 2)
                    project(banks[7], oT[b], wo_sb, cp_y)
            over_tiles(eng, 2, step_c)

        @block.vector
        def _(eng):
            def by_tile(row):
                return row[:, :].rearrange("p (t e) -> p t e", t=NT)

            def link(ins, s, n):
                ins.then_inc(s, 1)
                wait(eng, s, n)

            eng.wait_ge(g_const, 8)
            eng.tensor_scalar(ident[:, :], dist[:, :], 0.0, None, ALU.is_equal).then_inc(v_const, 1)
            eng.tensor_scalar(upto[:, :], dist[:, :], 0.0, None, ALU.is_ge).then_inc(v_const, 1)
            eng.tensor_scalar(before[:, :], dist[:, :], 0.0, None, ALU.is_lt).then_inc(v_const, 1)
            eng.wait_ge(d_row, 16)
            eng.wait_ge(d_cols, 32)
            eng.scalar_tensor_tensor(by_tile(key_row), by_tile(row_i), 32.0, tile_row, ALU.mult, ALU.add)\
               .then_inc(v_keys, 1)
            eng.scalar_tensor_tensor(skey_col[:, :], key_col_i[:, :], 32.0, tile_no[:, :], ALU.mult, ALU.add)
            eng.scalar_tensor_tensor(dkey_col[:, :], edge_i[:, :, 0], 32.0, tile_no[:, :], ALU.mult, ALU.add)\
               .then_inc(s_keys, 1)
            eng.tensor_scalar(xidx[:, :], edge_i[:, :, 0], float(N - 1), None, ALU.min).then_inc(v_keys, 1)
            eng.wait_ge(d_wl0, 144)
            v3 = [rcut[:, :].unsqueeze(2).broadcast_to([P, NT, 3]), rn2[:, :].unsqueeze(2).broadcast_to([P, NT, 3])]
            link(eng.tensor_tensor(r_sq[:, :, :], r_sb[:, :, :], r_sb[:, :, :], ALU.mult), s_keys, 2)
            eng.tensor_reduce(rn2[:, :], r_sq[:, :, :], AX.X, ALU.add).then_inc(v_unit, 1)
            eng.wait_ge(s_unit, 1)
            link(eng.reciprocal(rn2[:, :], rn[:, :]), v_unit, 2)
            link(eng.tensor_tensor(u[:, :, :], r_sb[:, :, :], v3[1], ALU.mult), v_unit, 3)
            eng.tensor_tensor(ur[:, :, :], u[:, :, :], v3[0], ALU.mult).then_inc(v_unit, 1)
            eng.wait_ge(v_unit, 4)
            eng.wait_ge(p_wv, 1)
            eng.tensor_copy(wva[:, :], banks[0][:, 0:C])
            eng.tensor_copy(wvb[:, :], banks[0][:, C:2 * C]).then_inc(v_wv, 1)
            for c in range(EP // D):
                k = c % 2
                eng.wait_ge(p_pre, c + 1)
                wait(eng, p_filt, 4 * (c - 1))
                link(eng.tensor_scalar(fz[:, k, :], banks[6 + k][:, :], bf1_sb[:, :], None, ALU.add), s_z, c + 1)
                eng.scalar_tensor_tensor(fe[:, k, :], fz[:, k, :], -1.0, fz[:, k, :], ALU.mult, ALU.min)\
                   .then_inc(v_neg, 1)
                eng.wait_ge(s_ln, c + 1)
                eng.scalar_tensor_tensor(hid[:, k, :], fz[:, k, :], 0.0, fe[:, k, :], ALU.max, ALU.add)\
                   .then_inc(v_hid, 1)
            eng.wait_ge(v_const, 3)
            eng.wait_ge(v_keys, 2)
            eng.wait_ge(s_filt, EP // D * 4)

            def ranks(t, b, row, col, out_i, s_count, s_rank):
                wait(eng, s_count, 2 * t)
                eng.tensor_scalar(junk[:, :], row[:, :], col[:, bass.ds(t, 1)], 0.0, ALU.is_lt, ALU.add,
                                  accum_out=count[b][:, :]).then_inc(s_count, 1)
                eng.scalar_tensor_tensor(junk_t[:, :], row[:, bass.ds(P * t, P)], col[:, bass.ds(t, 1)],
                                         before[:, :], ALU.is_equal, ALU.mult,
                                         accum_out=ties[b][:, :]).then_inc(s_count, 1)
                wait(eng, s_count, 2 * (t + 1))
                eng.scalar_tensor_tensor(out_i[:, bass.ds(t, 1)], count[b][:, :], 1.0, ties[b][:, :],
                                         ALU.add, ALU.add).then_inc(s_rank, 1)

            def step_a(tau, b):
                if real(tau):
                    wait(eng, a_x[b], dma_count(tau, b))
                    eng.bn_stats(st[b][:, 0:6], xg[b][:, :]).then_inc(av_stats, 1)
                    apart(eng, g_const, tau + 1)
                    wait(eng, av_stats, tau + 1)
                    eng.bn_aggr(mv[b][:, 0:2], st[b][:, 0:6]).then_inc(av_mom, 1)
                    ranks(tau, b, key_row, skey_col, rank_s, av_count, av_rank)
                    wait(eng, as_std, tau + 1)
                    eng.reciprocal(rstd[b][:, 0:1], std[b][:, 0:1]).then_inc(av_rstd, 1)
                    wait(eng, av_rstd, tau + 1)
                    eng.scalar_tensor_tensor(nb[b][:, 0:1], mv[b][:, 0:1], -1.0, rstd[b][:, 0:1],
                                             ALU.mult, ALU.mult).then_inc(av_nb, 1)
                if real(tau - 1):
                    t, q = tau - 1, 1 - b
                    wait(eng, ap_X, t + 1)
                    wait(eng, ap_O, t - 1)
                    w = [WT[:, k, bass.ds(P * t, P)] for k in range(4)]
                    stt = eng.scalar_tensor_tensor
                    stt(M[q][:, 0, :], banks[3][:, 0:C], SC_A, w[0], ALU.mult, ALU.mult)
                    stt(M[q][:, 2, :], banks[3][:, 0:C], SC_C, w[2], ALU.mult, ALU.mult)
                    stt(M[q][:, 1, :], banks[2][:, 3 * C:4 * C], SC_B, w[1], ALU.mult, ALU.mult)
                    stt(M[q][:, 3:6, :], banks[2][:, 0:3 * C].rearrange("p (i c) -> p i c", i=3), SC_D,
                        w[3].unsqueeze(1).broadcast_to([P, 3, C]), ALU.mult, ALU.mult).then_inc(av_M, 1)
                if real(tau):
                    wait(eng, as_h, tau + 1)
                    wait(eng, ap_T, tau - 1)
                    hv = h[b][:, C:4 * C].rearrange("p (c i) -> p i c", i=3)
                    eng.tensor_scalar(hd[b][:, :], hv[:, 0, :], u[:, tau, 0:1], None, ALU.mult).then_inc(av_hdp, 1)
                    wait(eng, av_hdp, 2 * tau + 1)
                    eng.scalar_tensor_tensor(hd[b][:, :], hv[:, 1, :], u[:, tau, 1:2], hd[b][:, :],
                                             ALU.mult, ALU.add).then_inc(av_hdp, 1)
                    wait(eng, av_hdp, 2 * tau + 2)
                    eng.scalar_tensor_tensor(hd[b][:, :], hv[:, 2, :], u[:, tau, 2:3], hd[b][:, :],
                                             ALU.mult, ALU.add).then_inc(av_hd, 1)
                if real(tau - 2):
                    t = tau - 2
                    wait(eng, as_D, t + 1)
                    wait(eng, a_scat[b], dma_count(t - 2, b))
                    pv = Pt[b][:, C:4 * C].rearrange("p (c i) -> p i c", i=3)
                    for i in range(3):
                        last = eng.scalar_tensor_tensor(pv[:, i, :], banks[5][:, 0:C], ur[:, t, i:i + 1],
                                                        Dr[b][:, i * C:(i + 1) * C], ALU.mult, ALU.add)
                    last.then_inc(av_P, 1)
            over_tiles(eng, 2, step_a)

            eng.wait_ge(d_rowd, 16)
            eng.scalar_tensor_tensor(by_tile(key_row), by_tile(row_d), 32.0, tile_row, ALU.mult, ALU.add)\
               .then_inc(bv_sk, 1)
            eng.wait_ge(d_sk, 48)
            eng.tensor_copy(sk_f[:, :], row_i[:, 0:KW + 1])
            eng.tensor_copy(kn_f[:, :], kn_i[:, :, 0])
            eng.tensor_scalar(sx_i[:, :], ko_i[:, :, 0], float(N - 1), None, ALU.min)
            eng.tensor_copy(sk_c[:, :], ko_i[:, :, 0]).then_inc(bv_sk, 1)
            eng.wait_ge(bv_sk, 2)

            def last_rows(key_c, rows_i, s, n):
                eng.tensor_tensor(cont[:, :], key_c[:, :], kn_f[:, :], ALU.is_equal).then_inc(s, 1)
                eng.wait_ge(s, n)
                eng.scalar_tensor_tensor(cont[:, :], cont[:, :], float(OFF), key_c[:, :], ALU.mult, ALU.add)\
                   .then_inc(s, 1)
                eng.wait_ge(s, n + 1)
                eng.memset(cont[0:1, :], float(OFF)).then_inc(s, 1)
                eng.wait_ge(s, n + 2)
                eng.tensor_copy(rows_i[:, :], cont[:, :]).then_inc(s, 1)
                eng.wait_ge(s, n + 3)
            last_rows(sk_c, srow_i, bv_sk, 3)

            def masks(t, b, keys, col, s):
                eng.scalar_tensor_tensor(mask[b][:, 1:P], keys[:, bass.ds(G * t + 1, G)], col[:, bass.ds(t, 1)],
                                         upto[:, 1:P], ALU.is_equal, ALU.mult)
                eng.tensor_scalar(mask[b][:, 0:1], keys[:, bass.ds(G * t + G, 1)], col[:, bass.ds(t, 1)], None,
                                  ALU.is_equal).then_inc(s, 1)

            def step_b(tau, b):
                if real(tau - 1) and (not isinstance(tau, int) or tau - 1 > 0):
                    t, q = tau - 1, 1 - b
                    wait(eng, b_P[q], dma_count(t, q))
                    wait(eng, bp_cum, t)
                    eng.tensor_copy(Pt[q][0:1, :], banks[b][0:1, :]).then_inc(bv_carry, 1)
                elif real(tau - 1):
                    eng.nop().then_inc(bv_carry, 1)
                if real(tau):
                    wait(eng, bp_st, tau - 1)
                    masks(tau, b, sk_f, sk_c, bv_mask)
                    ranks(tau, b, key_row, dkey_col, rank_d, bv_count, bv_rank)
                if real(tau - 1):
                    t, q = tau - 1, 1 - b
                    wait(eng, bp_st, t + 1)
                    wait(eng, bp_s2, t - 1)
                    eng.tensor_scalar(sz[q][:, :], banks[2][:, 0:P], 0.0, None, ALU.max).then_inc(bv_pos, 1)
                    wait(eng, bv_pos, t + 1)
                    eng.scalar_tensor_tensor(se[q][:, :], sz[q][:, :], -2.0, banks[2][:, 0:P], ALU.mult, ALU.add)\
                       .then_inc(bv_neg, 1)
                if real(tau - 2):
                    t = tau - 2
                    wait(eng, bp_s2, t + 1)
                    wait(eng, b_x[b], dma_count(t, b))
                    eng.scalar_tensor_tensor(XO[:, t, 0:C], banks[3][:, 0:C], SC_S2, xg[b][:, 0:C],
                                             ALU.mult, ALU.add)
                    eng.tensor_tensor(XO[:, t, C:D], banks[b][:, C:D], xg[b][:, C:D], ALU.add).then_inc(bv_x1, 1)
                if real(tau - 1):
                    t, q = tau - 1, 1 - b
                    wait(eng, bs_ln, t + 1)
                    wait(eng, bv_pos, t + 1)
                    eng.tensor_tensor(sp[q][:, :], sz[q][:, :], se[q][:, :], ALU.add).then_inc(bv_sp, 1)
            over_tiles(eng, 2, step_b)

            eng.wait_ge(d_dk, 48)
            rec = records\
                .rearrange("p (e two) -> p e two", two=2)
            eng.tensor_copy(dk_f[:, :], rec[:, :, 0])
            eng.tensor_copy(kn_f[:, :], kn_i[:, :, 0])
            eng.tensor_scalar(dx_i[:, :], ko_i[:, :, 0], float(N - 1), None, ALU.min)
            eng.tensor_scalar(ds_i[:, :], ko_i[:, :, 1], float(N - 1), None, ALU.min)
            eng.tensor_copy(dk_c[:, :], ko_i[:, :, 0]).then_inc(bv_sk, 1)
            eng.wait_ge(bv_sk, 7)
            eng.tensor_tensor(same[:, 1:KW + 1], dk_f[0:H, 1:KW + 1], dk_f[0:H, 0:KW], ALU.is_equal)
            eng.memset(same[:, 0:1], 0.0).then_inc(bv_sk, 1)
            last_rows(dk_c, drow_i, bv_sk, 9)
            eng.tensor_scalar(same[:, :], same[:, :], 0.5, BIG, ALU.subtract, ALU.mult)\
               .then_inc(bv_sk, 1)
            eng.wait_ge(bv_sk, 13)
            eng.nop().then_inc(cv_dk, 2)
            eng.wait_ge(g_ones, 2)

            def step_c(tau, b):
                if real(tau):
                    wait(eng, c_xd[b], dma_count(tau, b))
                    eng.bn_stats(st[b][:, 0:6], xd[b][:, :])
                    wait(eng, c_xs[b], dma_count(tau, b))
                    eng.bn_stats(st[b][:, 6:12], xg[b][:, :]).then_inc(cv_stats, 2)
                    apart(eng, g_const, 2 * (tau + 1))
                    wait(eng, cv_stats, 2 * (tau + 1))
                    eng.bn_aggr(mv[b][:, 0:2], st[b][:, 0:6])
                    eng.bn_aggr(mv[b][:, 2:4], st[b][:, 6:12]).then_inc(cv_mom, 2)
                if real(tau - 2):
                    t = tau - 2
                    wait(eng, cs_aT, t + 1)
                    if not isinstance(t, int) or t > 0:
                        eng.tensor_copy(aT[b][:, 0:1], mT[1 - b][:, P - 1:P]).then_inc(cv_fwd, 1)
                    else:
                        eng.nop().then_inc(cv_fwd, 1)
                    wait(eng, cv_fwd, 3 * t + 1)
                    wait(eng, cv_e, t - 1)
                    eng.tensor_tensor_scan(eT[b][:, 1:P], same[:, bass.ds(G * t + 1, G)], aT[b][:, 1:P],
                                           aT[b][:, 0:1], ALU.min, ALU.max).then_inc(cv_fwd, 1)
                    eng.tensor_copy(eT[b][:, 0:1], aT[b][:, 0:1])
                    eng.tensor_copy(same_back[:, ::-1], same[:, bass.ds(G * t + 1, P)]).then_inc(cv_fwd, 1)
                    wait(eng, cv_fwd, 3 * t + 3)
                    eng.tensor_tensor_scan(mT[b][:, :][:, ::-1], same_back[:, :],
                                           eT[b][:, :][:, ::-1], -BIG, ALU.min, ALU.max).then_inc(cv_bwd, 1)
                    wait(eng, cv_bwd, t + 1)
                    eng.tensor_tensor(eT[b][:, :], aT[b][:, :], mT[b][:, :], ALU.subtract).then_inc(cv_e, 1)
                    wait(eng, cp_cum, t - 1)
                    masks(t, b, dk_f, dk_c, cv_mask)
                if real(tau):
                    wait(eng, cs_std, tau + 1)
                    eng.reciprocal(rstd[b][:, :], std[b][:, :]).then_inc(cv_rstd, 1)
                    wait(eng, cv_rstd, tau + 1)
                    eng.scalar_tensor_tensor(nb[b][:, :], mv[b][:, 0:4:2], -1.0, rstd[b][:, :],
                                             ALU.mult, ALU.mult).then_inc(cv_nb, 1)
                if real(tau - 1):
                    t, q = tau - 1, 1 - b
                    wait(eng, cp_q, t + 1)
                    eng.tensor_tensor(qs[q], banks[1][:, :], bq_sb[:, :], ALU.add).then_inc(cv_q, 1)
                if real(tau - 2):
                    t2 = tau - 2
                    wait(eng, cs_ex, t2 + 1)
                    wait(eng, cp_cum, t2 - 1)
                    wait(eng, cv_carry, t2 + 1)
                    wait(eng, cv_v, t2 + 1)
                    eng.tensor_tensor(vw[b][:, 0:D].rearrange("p (h d) -> p h d", h=H),
                                      va[b][:, 0:D].rearrange("p (h d) -> p h d", h=H),
                                      ex[b][:, :].unsqueeze(2).broadcast_to([P, H, DH]), ALU.mult)
                    eng.tensor_tensor(vw[b][:, D:D + H], va[b][:, D:D + H], ex[b][:, :], ALU.mult).then_inc(cv_vw, 1)
                if real(tau - 1):
                    wait(eng, cp_k, t + 1)
                    eng.tensor_tensor(ks[q], banks[2][:, :], bk_sb[:, :], ALU.add).then_inc(cv_k, 1)
                    wait(eng, cv_k, t + 1)
                    eng.tensor_tensor(ks[q], ks[q], qs[q], ALU.mult).then_inc(cv_prod, 1)
                    wait(eng, cv_prod, t + 1)
                    wait(eng, cp_aT, t - 1)
                    eng.tensor_reduce(a_sb[q][:, :], ks[q].rearrange("p (h d) -> p h d", h=H), AX.X, ALU.add)\
                       .then_inc(cv_a, 1)
                if real(tau - 2):
                    wait(eng, cp_cum, t2 + 1)
                    eng.tensor_scalar(rden[b][:, :], banks[7][:, 0:H], 1e-30, None, ALU.max).then_inc(cv_den, 1)
                    wait(eng, cv_den, t2 + 1)
                    eng.reciprocal(rden[b][:, :], rden[b][:, :]).then_inc(cv_rden, 1)
                    wait(eng, cv_rden, t2 + 1)
                    wait(eng, cp_oT, t2 - 1)
                    eng.tensor_tensor(o_sb[b].rearrange("p (h d) -> p h d", h=H),
                                      banks[4][:, :].rearrange("p (h d) -> p h d", h=H),
                                      rden[b][:, :].unsqueeze(2).broadcast_to([P, H, DH]), ALU.mult)\
                       .then_inc(cv_o, 1)
                if real(tau - 1):
                    wait(eng, cp_v, t + 1)
                    eng.tensor_tensor(va[q][:, 0:D], banks[3][:, :], bv_sb[:, :], ALU.add).then_inc(cv_v, 1)
                    if not isinstance(t, int) or t > 0:
                        wait(eng, cv_v, t + 1)
                        eng.tensor_copy(va[q][0:1, 0:D], banks[4][0:1, :])
                        eng.tensor_copy(va[q][0:1, D:D + H], banks[7][0:1, 0:H]).then_inc(cv_carry, 1)
                    else:
                        eng.nop().then_inc(cv_carry, 1)
                if real(tau):
                    wait(eng, cp_Ts, tau + 1)
                    eng.tensor_copy(hTs[b], banks[0][:, :]).then_inc(cv_hTs, 1)
                if real(tau - 2):
                    wait(eng, cp_y, t2 + 1)
                    wait(eng, c_out[b], dma_count(t2 - 2, b))
                    wait(eng, cg_y, t2 + 1)
                    eng.tensor_tensor(y[b][:, :], banks[7][:, :], xb[b][:, :], ALU.add).then_inc(cv_y, 1)
            over_tiles(eng, 2, step_c)


def _tiles(a, fill):
    rest = np.full((EP - E,) + a.shape[1:], fill, a.dtype)
    a = np.concatenate([a, rest]).reshape((NT, P) + a.shape[1:])
    return np.ascontiguousarray(np.swapaxes(a, 0, 1))


def _row(a, fill):
    return np.concatenate([a, np.full((EP - E,), fill, a.dtype)]).reshape(1, EP)


def _blocks(w):
    return np.ascontiguousarray(w.T.reshape(4, C, D).transpose(1, 0, 2))


def kernel(**inputs):
    import concourse.bacc as _bacc
    from concourse.bass_utils import run_bass_kernel_spmd as _run

    a = {k: np.asarray(v) for k, v in inputs.items()}
    src, dst = a["src"], a["dst"]
    l0 = {k[len("L0_gnn_"):]: v for k, v in a.items() if k.startswith("L0_gnn_")}
    l1 = {k[len("L1_gnn_"):]: v for k, v in a.items() if k.startswith("L1_gnn_")}
    w_kv = l1["Wkv"].reshape(H, 2, DH, D)
    b_kv = l1["bkv"].reshape(H, 2, DH)
    order = [
        ("x", a["x"]),
        ("src_row", _row(src, NONE)), ("dst_row", _row(dst, NONE)),
        ("src_cols", _tiles(src, NONE)), ("edge_cols", _tiles(np.stack([dst, src], 1), NONE)),
        ("f_t", np.ascontiguousarray(np.concatenate(
            [a["edge_attr_20"], np.zeros((EP - E, NRBF), a["edge_attr_20"].dtype)]).T)),
        ("rcut_cols", _tiles(a["edge_weight"], 0)), ("r_cols", _tiles(a["edge_attr_3"], 1)),
        ("w_s", l0["W_in2f_s"]), ("w_v", l0["W_in2f_v"]),
        ("wf1", l0["Wf1"]), ("bf1", l0["bf1"].reshape(C, 1)),
        ("wf2", l0["Wf2"][:, :4 * C].reshape(C, 2, C, 2).transpose(0, 1, 3, 2).reshape(C, 4, C)),
        ("bf2", l0["bf2"][:4 * C].reshape(2, C, 2).transpose(1, 0, 2).reshape(C, 4)),
        ("w1s", l0["W1_s"].reshape(C, 2, C)),
        ("w1v_t", l0["W1_v"].reshape(C, 2, C).transpose(1, 2, 0)),
        ("w2s", l0["W2_s"]), ("w2v", l0["W2_v"]),
        ("wq", _blocks(l1["Wq"])), ("bq", l1["bq"].reshape(1, D)),
        ("wk", _blocks(w_kv[:, 0].reshape(D, D))), ("bk", b_kv[:, 0].reshape(1, D)),
        ("wv", _blocks(w_kv[:, 1].reshape(D, D))), ("bv", b_kv[:, 1].reshape(1, D)),
        ("wo", _blocks(l1["Wo"])), ("bo2", np.concatenate([l1["bo"], l1["bo"]]).reshape(1, 2 * D)),
    ]
    nc = _bacc.Bacc("TRN2", target_bir_lowering=False, num_devices=1)
    arrays, args = {}, {}
    for name, v in order:
        v = np.ascontiguousarray(v)
        arrays[name + "_dram"] = v
        args[name] = nc.dram_tensor(name + "_dram", v.shape, mybir.dt.from_np(v.dtype), kind="ExternalInput").ap()
    f32, i32 = mybir.dt.float32, mybir.dt.int32
    args["out"] = nc.dram_tensor("out_dram", (N, D), f32, kind="ExternalOutput").ap()
    for name, shape, dt in (("psort", (ROWS, D), f32), ("skey", (ROWS, 1), i32), ("drec", (ROWS, 2), i32),
                            ("table", (P * 80, 1), i32), ("x1c", (EP, D), f32)):
        args[name] = nc.dram_tensor(name + "_scratch", shape, dt).ap()
    gnn_kernel(nc, **args)
    r = _run(nc, [arrays], core_ids=[0])
    return r.results[0]["out_dram"]
```

```python
import math

import numpy as np

import concourse.bass as bass
from concourse import mybir
from contextlib import ExitStack

P = 128
N = 10000
E = 2500
D = 512
C = 128
H = 8
DH = D // H
NRBF = 20
NT = 20
EP = NT * P
G = P - 1
ROWS = EP + 1
KW = G * NT + 1
NHI = N // P + 1
Q = 4
NONE = N
NOROW = 30000
OFF = 20000
PEEL = 4
PEEL_A = 6
CH = 1024
FLAT = N * D // P
EPS = 1e-5
Y0 = 1.0 / math.sqrt(4.0 * math.pi)
Y1 = math.sqrt(3.0 / (4.0 * math.pi))
BIG = 3.0e38


def wait(eng, sem, n):
    if isinstance(n, int) and n <= 0:
        return
    eng.wait_ge(sem, n)


def dma_count(t, b):
    return 8 * (t - b) + 16


def apart(eng, made, *values):
    for v in values:
        if not isinstance(v, int):
            eng.lower_val(v)
    eng.wait_ge(made, 8)


def real(t):
    return not isinstance(t, int) or 0 <= t < NT


def chunk_width(c):
    return FLAT - c * CH if isinstance(c, int) and c == 2 * NT - 1 else CH


def over_tiles(eng, lag, step, peel=PEEL):
    for tau in range(peel):
        step(tau, tau % 2)
    with eng.Fori(0, (NT - peel) // 2) as k:
        step(2 * k + peel, 0)
        step(2 * k + peel + 1, 1)
    for tau in range(NT, NT + lag):
        step(tau, tau % 2)


def gnn_kernel(nc, x, src_cols, edge_cols, f_t, rcut_cols, r_cols,
               w_s, w_v, wf1, bf1, wf2, bf2, w1s, w1v_t, w2s, w2v,
               wq, bq, wk, bk, wv, bv, wo, bo2, out,
               psort, skey, drec, table, x1c):
    f32 = mybir.dt.float32
    i32 = mybir.dt.int32
    bf16 = mybir.dt.bfloat16
    f16 = mybir.dt.float16
    MID = EP // 2
    ALU = mybir.AluOpType
    ACT = mybir.ActivationFunctionType
    AX = mybir.AxisListType

    RC, RF = 1.0 / math.sqrt(C), 1.0 / math.sqrt(2 * C)
    SC_A = Y0 * RC * RF
    SC_B = Y1 / math.sqrt(3.0) * RC * RF
    SC_C = Y1 * RC * RF * RC
    SC_D = Y0 * RC * RF * RC
    SC_S2 = RC
    SCALE = 1.0 / math.sqrt(DH)

    x_flat = x.rearrange("n d -> (n d)").rearrange("(p f) -> p f", p=P)
    out_flat = out.rearrange("n d -> (n d)").rearrange("(p f) -> p f", p=P)

    ctx = ExitStack()
    with ctx:
        def sb(name, shape, dt=f32):
            return ctx.enter_context(nc.sbuf_tensor(name, shape, dt))

        def pb(name, shape, dt=f32):
            return ctx.enter_context(nc.psum_tensor(name, shape, dt))

        def sem(name):
            return ctx.enter_context(nc.semaphore(name))

        def pair(name, shape, dt=f32):
            return [sb(f"{name}{b}", shape, dt) for b in range(2)]

        def sems(name):
            return [sem(f"{name}{b}") for b in range(2)]

        WT = sb("WT", [P, 4, EP])
        records = WT[:, :, :].bitcast(i32).rearrange("p k e -> p (k e)")[:, 0:2 * (KW + 1)]
        XO = sb("XO", [P, NT, D])
        f_sb = XO[0:NRBF, 0:5, :].rearrange("p a d -> p (a d)")
        fz = XO[:, 10:15, :].rearrange("p a d -> p (a d)")
        fe = XO[:, 15:20, :].rearrange("p a d -> p (a d)")
        src_keys = XO[:, 10:15, :].bitcast(i32).rearrange("p a d -> p (a d)")[:, 0:KW + 1]

        WA = sb("WA", [P, 4, 4, D])
        wq_sb, wk_sb, wv_sb, wo_sb = (WA[:, k] for k in range(4))
        early = WA[:, 3].rearrange("p k d -> p (k d)")
        w_s_sb, w_v_sb, w1v_t_sb, w1vt_b_sb, w2v_sb, wva, wvb = (early[:, k * C:(k + 1) * C] for k in range(7))
        wf2_sb = early[:, 7 * C:11 * C].rearrange("p (k c) -> p k c", k=4)
        w1s_sb = early[:, 11 * C:13 * C].rearrange("p (k c) -> p k c", k=2)
        w2s_sb = sb("w2s_sb", [P, C])
        wf1_sb = sb("wf1_sb", [NRBF, C])
        bf1_sb = sb("bf1_sb", [P, 1])
        bf2_sb = sb("bf2_sb", [P, 4])
        bq_sb, bk_sb, bv_sb, bo_sb = (sb(n, [P, D]) for n in ("bq_sb", "bk_sb", "bv_sb", "bo_sb"))
        bo_rot = sb("bo_rot", [P, D])

        key_row = sb("key_row", [P, EP])
        key_col_i = sb("key_col_i", [P, NT], i32)
        edge_i = sb("edge_i", [P, NT, 2], i32)
        xidx = sb("xidx", [P, NT], i32)
        vw_f = sb("vw_f", [P, EP // 2])
        rank_s, rank_d = sb("rank_s", [P, NT], i32), sb("rank_d", [P, NT], i32)
        sk_row = sb("sk_row", [P, EP])
        sk_f = sk_row[:, 0:KW + 1]
        dk_f = key_row[:, 0:KW + 1]
        ko_i, kn_i = sb("ko_i", [P, NT, 2], i32), sb("kn_i", [P, NT, 2], i32)
        sk_c, dk_c = sb("sk_c", [P, NT]), sb("dk_c", [P, NT])
        kn_f = sb("kn_f", [P, NT])
        cont = sb("cont", [P, NT])
        srow_i, drow_i = sb("srow_i", [P, NT], i32), sb("drow_i", [P, NT], i32)
        sx_i, dx_i, ds_i = sb("sx_i", [P, NT], i32), sb("dx_i", [P, NT], i32), sb("ds_i", [P, NT], i32)
        slot_i = sb("slot_i", [P, NT], i32)

        mask = pair("mask", [P, P])
        dist, lane = mask
        ident, upto, before = sb("ident", [P, P]), sb("upto", [P, P]), sb("before", [P, P])
        ident_b = sb("ident_b", [P, P], bf16)
        eps = sb("eps", [P, 1])
        half = sb("half", [P, 1])
        zero_row = sb("zero_row", [1, D])
        none_i = sb("none_i", [1, 2], i32)
        norow_i = XO[:, 5, 0:80].bitcast(i32)

        rcut = sb("rcut", [P, NT])
        r_sb, r_sq, u, ur = (sb(n, [P, NT, 3]) for n in ("r_sb", "r_sq", "u", "ur"))
        rn2, rn = sb("rn2", [P, NT]), sb("rn", [P, NT])

        st, mv = pair("st", [P, 12]), pair("mv", [P, 4])
        std, rstd, nb = pair("std", [P, 2]), pair("rstd", [P, 2]), pair("nb", [P, 2])
        h = pair("h", [P, D])
        hd = pair("hd", [P, C])
        hT = pair("hT", [P, 5 * C])
        M = pair("M", [P, 6, C])
        Pt = pair("Pt", [P, D])
        Dr = pair("Dr", [P, 3 * C])
        xg = pair("xg", [P, D])
        base = pair("base", [P, CH + 2 * H])
        qk, hs_o = sb("qk", [P, 2, D]), sb("hs_o", [P, 4, D])
        sz, se, sp = ([Dr[b][:, k * C:(k + 1) * C] for b in range(2)] for k in range(3))

        hTd = [M[b][:, 0:4, :].rearrange("p k c -> p (k c)") for b in range(2)]
        hTs = [hT[b][:, 0:D] for b in range(2)]
        hs = [hs_o[:, b, :] for b in range(2)]
        late = WT[:, :, :].rearrange("p k e -> p (k e)")[:, 4 * EP - 4 * D:]
        xd, xb = ([late[:, (2 * k + b) * D:(2 * k + b + 1) * D] for b in range(2)] for k in range(2))
        qs, ks = [qk[:, 0, :]] * 2, [qk[:, 1, :]] * 2
        td0, td1, ts0, ts1 = (sb(n, [P, 1], i32) for n in ("td0", "td1", "ts0", "ts1"))
        a_sb = pair("a_sb", [P, H])
        aT, mT, eT = pair("aT", [H, P]), pair("mT", [H, P]), pair("eT", [H, P])
        same = sk_f[0:H, :]
        same_back = before[0:H, :]
        ex = pair("ex", [P, H])
        va = [base[b][:, D:2 * D + H] for b in range(2)]
        vw = [vw_f[:, b * (D + H):(b + 1) * (D + H)] for b in range(2)]
        rden = pair("rden", [P, H])
        o_sb = [hs_o[:, 2 + b, :] for b in range(2)]
        oT = [base[b][:, 0:D] for b in range(2)]
        y = Pt

        banks = [pb(f"bank{i}", [P, 512]) for i in range(8)]

        uses = {"xa": 1, "pa": 1, "ra": 1, "ea": 2, "xb": 1, "xc": 1, "sc": 1, "oc": 1}
        idx_all = sb("idx_all", [P, 2 * sum(uses.values())], i32)
        idx, at = {}, 0
        for n, k in uses.items():
            idx[n] = [idx_all[:, at + b * k:at + (b + 1) * k] for b in range(2)]
            at += 2 * k

        free = WA[:, 0:3].rearrange("p w k d -> p (w k d)")

        class Sort:
            def __init__(s, name, keys, rank, hi_hot, lo_hot, hi_rows, earlier, sums, bank, same_keys, looked_up):
                s.keys, s.rank, s.hi_hot, s.lo_hot = keys, rank, hi_hot, lo_hot
                s.hi_rows, s.earlier = hi_rows.bitcast(f16)[:, 0:EP], earlier.bitcast(f16)[:, 0:EP]
                s.hi, s.lo = sb(name + "_hi", [P, NT], i32), sb(name + "_lo", [P, NT], i32)
                s.total, s.run = sums[0:NHI, 0, :], sums[0:NHI, 1, :]
                s.first = sums[0:NHI, 2, 0:P // 2].bitcast(f16)
                s.sum, s.start = sb(name + "_sum", [NHI, 1]), sb(name + "_start", [NHI, 1])
                s.count = sb(name + "_count", [P, NT])
                s.sums_bank, s.rows_bank = banks[bank], banks[bank + 1]
                s.same_keys, s.looked_up = same_keys, looked_up
                (s.v_hot, s.p_turn, s.s_turn, s.p_hist, s.s_hist, s.v_first,
                 s.p_same, s.v_same, s.p_rank, s.v_prod, s.v_rank) = (
                    sem(name + "_" + n) for n in ("v_hot p_turn s_turn p_hist s_hist "
                                                  "v_first p_same v_same p_rank v_prod v_rank").split())

        spare = XO[:, 5:10, :].rearrange("p a d -> p (a d)")[:, 80:].bitcast(bf16)
        by_src = Sort("src", key_col_i[:, :], rank_s,
                      spare[:, EP:EP + NT * NHI].rearrange("p (t c) -> p t c", t=NT),
                      spare[:, 0:EP].rearrange("p (t c) -> p t c", t=NT),
                      free[0:NHI, 0:EP], key_row[0:NHI, :], M[0],
                      0, [hT[b][:, 0:Q * P // 2].bitcast(bf16) for b in range(2)], h)
        by_dst = Sort("dst", edge_i[:, :, 0], rank_d,
                      free[:, 2 * EP:2 * EP + NT * NHI // 2].bitcast(bf16).rearrange("p (t c) -> p t c", t=NT),
                      vw_f[:, :].bitcast(bf16).rearrange("p (t c) -> p t c", t=NT),
                      free[0:NHI, EP:2 * EP], sk_row[0:NHI, :], M[1],
                      2, [Dr[b][:, 0:Q * P // 2].bitcast(bf16) for b in range(2)], Pt)

        sorts = (by_src, by_dst)
        ident_h = free[0:NHI, 12 * D - P // 2:12 * D].bitcast(f16)[:, 0:NHI]

        g_idx = {n: sem("g_idx_" + n) for n in uses}
        d_cols, d_const = sem("d_cols"), sem("d_const")
        d_wf, d_wl0, d_wl1 = sem("d_wf"), sem("d_wl0"), sem("d_wl1")
        d_init, d_bias = sem("d_init"), sem("d_bias")
        g_const = sem("g_const")
        v_const = sem("v_const")
        v_keys = sem("v_keys")
        v_unit, s_unit = sem("v_unit"), sem("s_unit")
        p_wv, v_wv = sem("p_wv"), sem("v_wv")
        p_pre, v_z, v_neg, s_soft, v_hid, p_filt, s_filt, v_filt = (
            sem(n) for n in ("p_pre", "v_z", "v_neg", "s_soft", "v_hid", "p_filt", "s_filt", "v_filt"))
        base_in, base_out, v_base, g_base = sems("base_in"), sems("base_out"), sem("v_base"), sem("g_base")
        a_x = sems("a_x")
        av_stats, av_mom, as_std, av_rstd, av_nb, as_h, av_hd, ap_T, as_hT, ap_X, av_M, ap_O, as_D, as_S, av_P = (
            sem(n) for n in ("av_stats", "av_mom", "as_std", "av_rstd", "av_nb", "as_h", "av_hd", "ap_T",
                             "as_hT", "ap_X", "av_M", "ap_O", "as_D", "as_S", "av_P"))
        av_hdp = sem("av_hdp")
        a_scat = sems("a_scat")
        g_skey = sem("g_skey")
        d_sk, bv_sk = sem("d_sk"), sem("bv_sk")
        b_x, b_P = sems("b_x"), sems("b_P")
        bv_mask, bv_carry, bp_cum, bp_st, bv_neg, bv_pos, bs_exp, bs_ln, bv_sp, bp_s2, bv_x1, bv_xo = (
            sem(n) for n in ("bv_mask", "bv_carry", "bp_cum", "bp_st", "bv_neg", "bv_pos", "bs_exp", "bs_ln",
                             "bv_sp", "bp_s2", "bv_x1", "bv_xo"))
        v_sorted = sem("v_sorted")
        b_x1c = sems("b_x1c")
        a_drec, g_table = sems("a_drec"), sem("g_table")
        g_ones = sem("g_ones")
        d_dk, cg_src = sem("d_dk"), sem("cg_src")
        c_x, c_td, c_ts, c_xd, c_xs, c_out = (sems(n) for n in ("c_x", "c_td", "c_ts", "c_xd", "c_xs", "c_out"))
        (cv_stats, cv_mom, cs_std, cv_rstd, cv_nb, cs_hd, cs_hs, cp_Td, cs_hTd, cp_Ts, cv_hTs,
         cp_q, cp_k, cp_v, cv_q, cv_k, cv_prod, cv_a, cp_aT, cs_aT, cv_fwd, cv_bwd, cv_e, cp_E, cs_ex, cv_mask,
         cv_v, cv_carry, cv_vw, cp_cum, cv_den, cv_rden, cv_o, cp_oT, cs_oT, cp_y, cv_y, cg_y) = (
            sem("c_" + n) for n in (
                "stats mom std rstd nb hd hs Td hTd Ts hTs q k v qs ks prod a aTp aTs fwd bwd e E ex mask "
                "vs carry vw cum den rden o oTp oTs yp yv yg").split())

        def add_bias(eng, c, b, added):
            width = chunk_width(c)
            if not isinstance(c, int):
                apart(eng, g_const, dma_count(c, b))
            wait(eng, base_in[b], dma_count(c, b))
            k, w = max(width // D, 1), min(width, D)
            v = base[b][:, 0:width].rearrange("p (k d) -> p k d", k=k)
            eng.tensor_tensor(v, v, bo_rot[:, 0:w].unsqueeze(1).broadcast_to([P, k, w]), ALU.add)\
               .then_inc(added, 1)

        block = ctx.enter_context(nc.Block())

        @block.sync
        def _(sp_):
            eng = sp_
            eng.dma_start(edge_i[:, :, :], edge_cols).then_inc(d_cols, 16)
            eng.dma_start(key_col_i[:, :], src_cols).then_inc(d_cols, 16)
            eng.dma_start(f_sb, f_t).then_inc(d_wf, 16)
            eng.dma_start(wf1_sb[:, :], wf1).then_inc(d_wf, 16)
            eng.dma_start(bf1_sb[:, :], bf1).then_inc(d_wf, 16)
            eng.dma_start(wf2_sb[:, :, :], wf2).then_inc(d_wf, 16)
            eng.dma_start(bf2_sb[:, :], bf2).then_inc(d_wf, 16)
            eng.dma_start(rcut[:, :], rcut_cols).then_inc(d_wl0, 16)
            eng.dma_start(r_sb[:, :, :], r_cols).then_inc(d_wl0, 16)
            for dst, src in ((w_s_sb, w_s), (w_v_sb, w_v), (w1v_t_sb, w1v_t[0]), (w1vt_b_sb, w1v_t[1]),
                             (w2s_sb, w2s), (w2v_sb, w2v)):
                eng.dma_start(dst[:, :], src).then_inc(d_wl0, 16)
            eng.dma_start(w1s_sb[:, :, :], w1s).then_inc(d_wl0, 16)
            eng.dma_start(bo_rot[:, :], bass.AP(bo2.tensor, 0, [[0, P // 8], [D // 8, 8], [1, D]]))\
               .then_inc(d_const, 16)
            eng.wait_ge(g_const, 8)
            eng.dma_start(psort[0:1, :], zero_row[:, :]).then_inc(d_init, 16)
            eng.dma_start(skey[0:1, :], none_i[:, 0:1]).then_inc(d_init, 16)
            eng.dma_start(drec[0:1, :], none_i[:, :]).then_inc(d_init, 16)
            eng.dma_start(table.rearrange("(p f) one -> p (f one)", p=P), norow_i).then_inc(d_init, 16)
            for dst, src in ((bq_sb, bq), (bk_sb, bk), (bv_sb, bv), (bo_sb, bo2[:, 0:D])):
                eng.dma_start(dst[:, :], src.partition_broadcast(P)).then_inc(d_bias, 16)

            def sorted_columns(rows, w, s):
                with nc.allow_non_contiguous_dma(reason="columns of keys"):
                    for k, dst in enumerate((ko_i, kn_i)):
                        eng.dma_start(dst[:, :, 0:w], bass.AP(rows.tensor, w * k, [[w, P], [w * G, NT], [1, w]]))\
                           .then_inc(s, 16)

            def base_load(c, b):
                w = chunk_width(c)
                wait(eng, base_out[b], dma_count(c - 2, b))
                eng.dma_start(base[b][:, 0:w], x_flat[:, bass.ds(c * CH, w)]).then_inc(base_in[b], 16)

            def base_store(c, b, added, n):
                w = chunk_width(c)
                wait(eng, added, n)
                eng.dma_start(out_flat[:, bass.ds(c * CH, w)], base[b][:, 0:w]).then_inc(base_out[b], 16)

            def step_a(tau, b):
                if real(tau):
                    base_load(tau, b)
                if real(tau - 1):
                    base_store(tau - 1, 1 - b, v_base, tau)
                if isinstance(tau, int) and tau == 2:
                    eng.wait_ge(by_src.v_rank, NT // Q + 1)
                    eng.wait_ge(by_dst.v_rank, NT // Q + 1)
                    for dst, src in ((wq_sb, wq), (wk_sb, wk), (wv_sb, wv)):
                        eng.dma_start(dst, src).then_inc(d_wl1, 16)
                    eng.wait_ge(g_skey, 16 * NT)
                    eng.wait_ge(v_hid, 1)
                    eng.wait_ge(p_filt, 4 * EP // D)
                    sorted_columns(skey, 1, d_sk)
                    eng.dma_start(src_keys, bass.AP(skey.tensor, 0, [[0, P], [1, KW + 1]])).then_inc(d_sk, 16)
            over_tiles(eng, 2, step_a)
            eng.wait_ge(v_sorted, 1)
            for b in range(2):
                eng.wait_ge(a_drec[b], 8 * NT)
            eng.wait_ge(av_M, NT)
            sorted_columns(drec, 2, d_dk)
            eng.dma_start(records,
                          bass.AP(drec.tensor, 0, [[0, P], [1, 2 * (KW + 1)]])).then_inc(d_dk, 16)

            for b in range(2):
                eng.wait_ge(a_scat[b], 8 * NT)
            eng.dma_start(wo_sb, wo).then_inc(d_wl1, 16)

            def step_b(tau, b):
                if real(tau):
                    wait(eng, bp_st, tau - 1)
                    eng.dma_start(Pt[b][:, :], psort[bass.ds(G * tau, P), :]).then_inc(b_P[b], 16)
                if real(tau - 2):
                    base_load(tau - 2 + NT, b)
                    if not isinstance(tau, int) or tau > 2:
                        base_store(tau - 3 + NT, 1 - b, g_base, tau - 2)
                    wait(eng, bv_x1, tau - 1)
                    eng.dma_start(x1c[bass.ds(P * (tau - 2), P), :], XO[:, tau - 2, :]).then_inc(b_x1c[b], 16)
            over_tiles(eng, 2, step_b)
            base_store(2 * NT - 1, 1, g_base, NT)

            for b in range(2):
                eng.wait_ge(base_out[b], 16 * NT)
                eng.wait_ge(b_x1c[b], 8 * NT)
                eng.wait_ge(c_out[b], 8 * NT)

        @block.gpsimd
        def _(eng):
            eng.iota(dist[:, :], [[1, P]], base=0, channel_multiplier=-1,
                     allow_small_or_imprecise_dtypes=True).then_inc(g_const, 1)
            eng.memset(zero_row[:, :], 0.0).then_inc(g_const, 1)
            eng.memset(none_i[:, :], NONE).then_inc(g_const, 1)
            eng.memset(eps[:, :], EPS).then_inc(g_const, 1)
            eng.memset(half[:, :], 0.5).then_inc(g_const, 1)
            eng.memset(norow_i, NOROW).then_inc(g_const, 1)
            eng.iota(slot_i[:, :], [[P, NT]], base=0, channel_multiplier=1).then_inc(g_const, 1)
            eng.iota(lane[:, :], [[1, P]], base=0, channel_multiplier=0,
                     allow_small_or_imprecise_dtypes=True).then_inc(g_const, 1)

            def wait_apart(eng, s, n):
                if not isinstance(n, int):
                    apart(eng, g_const, n)
                wait(eng, s, n)

            def gather(dst, src, idx, rows, s):
                eng.indirect_dma_start(out=dst, out_offset=None, in_=src,
                                       in_offset=bass.IndirectOffsetOnAxis(ap=idx, axis=0),
                                       bounds_check=rows - 1, oob_is_err=False).then_inc(s, 16)

            def scatter(dst, idx, src, rows, s):
                eng.indirect_dma_start(out=dst, out_offset=bass.IndirectOffsetOnAxis(ap=idx, axis=0),
                                       in_=src, in_offset=None,
                                       bounds_check=rows - 1, oob_is_err=False).then_inc(s, 16)

            def pick(name, t, b, column, users):
                s = g_idx[name]
                for u_ in users:
                    wait_apart(eng, u_[b], dma_count(t - 2, b))
                eng.tensor_copy(idx[name][b][:, :], column[:, t] if len(column.shape) == 3
                                else column[:, bass.ds(t, 1)]).then_inc(s, 1)
                wait_apart(eng, s, t + 1)
                return idx[name][b][:, :]

            eng.wait_ge(v_keys, 1)
            for tau in range(2):
                gather(xg[tau][:, :], x, pick("xa", tau, tau, xidx, []), N, a_x[tau])
            eng.wait_ge(d_const, 16)
            eng.wait_ge(d_init, 64)
            eng.wait_ge(by_src.v_rank, NT // Q + 1)
            for t in range(NT):
                scatter(skey, rank_s[:, t:t + 1], key_col_i[:, t:t + 1], ROWS, g_skey)
            eng.wait_ge(by_dst.v_rank, NT // Q + 1)

            def step_a(tau, b):
                if real(tau) and not (isinstance(tau, int) and tau < 2):
                    wait_apart(eng, as_h, tau - 1)
                    gather(xg[b][:, :], x, pick("xa", tau, b, xidx, [a_x]), N, a_x[b])
                if real(tau - 5):
                    t = tau - 5
                    wait_apart(eng, av_P, t + 1)
                    wait_apart(eng, as_S, t + 1)
                    scatter(psort, pick("pa", t, 1 - b, rank_s, [a_scat]), Pt[1 - b][:, :], ROWS, a_scat[1 - b])
                if real(tau):
                    scatter(drec, pick("ra", tau, b, rank_d, [a_drec]),
                            pick("ea", tau, b, edge_i, [a_drec]), ROWS, a_drec[b])
            over_tiles(eng, 5, step_a, PEEL_A + 2)

            eng.wait_ge(v_sorted, 1)

            def step_b(tau, b):
                if real(tau):
                    wait_apart(eng, bv_x1, tau - 1)
                    gather(xg[b][:, :], x, pick("xb", tau, b, sx_i, [b_x]), N, b_x[b])
                if isinstance(tau, int) and tau == 1:
                    for t in range(NT):
                        scatter(table, srow_i[:, t:t + 1], slot_i[:, t:t + 1], N, g_table)
                if real(tau - 2):
                    add_bias(eng, tau - 2 + NT, b, g_base)
            over_tiles(eng, 2, step_b)

            eng.wait_ge(v_sorted, 2)
            eng.wait_ge(g_table, 16 * NT)
            for b in range(2):
                eng.wait_ge(base_out[b], 16 * NT)
                eng.memset(va[b][:, D:D + H], 1.0).then_inc(g_ones, 1)

            td, ts = (td0, td1), (ts0, ts1)

            def lookups(t, b):
                dst_rows = pick("xc", t, b, dx_i, [c_x, c_td])
                gather(xd[b][:, :], x, dst_rows, N, c_x[b])
                gather(td[b][:, :], table, dst_rows, N, c_td[b])
                gather(ts[b][:, :], table, pick("sc", t, b, ds_i, [c_ts]), N, c_ts[b])

            def updated(t, b):
                wait_apart(eng, c_x[b], dma_count(t, b))
                wait_apart(eng, c_td[b], dma_count(t, b))
                gather(xd[b][:, :], x1c, td[b][:, :], EP, c_xd[b])
                wait_apart(eng, c_ts[b], dma_count(t, b))
                gather(xg[b][:, :], x1c, ts[b][:, :], EP, c_xs[b])

            def step_c(tau, b):
                if real(tau - 1):
                    if isinstance(tau, int) and tau == 1:
                        for q in range(2):
                            eng.wait_ge(b_x1c[q], 8 * NT)
                    updated(tau - 1, 1 - b)
                if real(tau - 2):
                    t = tau - 2
                    wait_apart(eng, cv_y, t - 1)
                    wait_apart(eng, c_xd[b], dma_count(t, b))
                    eng.tensor_tensor(xb[b][:, :], xd[b][:, :], bo_sb[:, :], ALU.add).then_inc(cg_y, 1)
                if real(tau):
                    wait_apart(eng, cs_hs, tau - 1)
                    wait_apart(eng, cg_y, tau - 1)
                    lookups(tau, b)
                if real(tau - 4):
                    t = tau - 4
                    wait_apart(eng, cv_y, t + 1)
                    scatter(out, pick("oc", t, b, drow_i, [c_out]), y[b][:, :], N, c_out[b])
                if isinstance(tau, int) and 1 <= tau < PEEL:
                    if tau == 1:
                        eng.wait_ge(bv_xo, NT)
                    for t in range(NT):
                        if t % (PEEL - 1) == tau - 1:
                            scatter(out, srow_i[:, t:t + 1], XO[:, t, :], N, cg_src)
                    if tau == PEEL - 1:
                        eng.wait_ge(cg_src, 16 * NT)
            over_tiles(eng, 4, step_c)
            for b in range(2):
                eng.wait_ge(c_out[b], 8 * NT)

        @block.scalar
        def _(eng):
            eng.wait_ge(g_const, 8)

            def high_rows(s):
                for r in range(-(-NT // 8)):
                    eng.wait_ge(s.p_turn, r + 1)
                    w = min(8, NT - 8 * r) * P
                    eng.activation(s.hi_rows[:, 8 * P * r:8 * P * r + w],
                                   s.rows_bank[:, :].bitcast(bf16)[0:NHI, 0:w], ACT.Copy).then_inc(s.s_turn, 1)

            def earlier(s, g):
                eng.wait_ge(s.p_hist, g + 1)
                w = Q if g < NT // Q - 1 else Q - 1
                last = eng.activation(s.earlier[:, (Q * g + 1) * P:(Q * g + 1 + w) * P],
                                      s.sums_bank[0:NHI, 0:w * P], ACT.Copy)
                if w < Q:
                    last = eng.activation(s.total, s.sums_bank[0:NHI, w * P:Q * P], ACT.Copy)
                last.then_inc(s.s_hist, 1)

            for s in sorts:
                high_rows(s)
            for g in range(NT // Q):
                for s in sorts:
                    earlier(s, g)
                if g == 0:
                    eng.wait_ge(v_neg, 1)
                    eng.activation(fe[:, :], fe[:, :], ACT.Exp).then_inc(s_soft, 1)
                    eng.wait_ge(s_soft, 1)
                    eng.activation(fe[:, :], fe[:, :], ACT.Ln, bias=half[:, :], scale=0.5).then_inc(s_soft, 1)
            for c in range(EP // D):
                for k in (0, 2):
                    eng.wait_ge(p_filt, 4 * c + k + 1)
                    eng.activation(WT[:, k, c * D:(c + 1) * D], banks[4 + k][:, :], ACT.Identity,
                                   bias=bf2_sb[:, k:k + 1]).then_inc(s_filt, 1)
            eng.wait_ge(v_unit, 1)
            eng.activation(rn[:, :], rn2[:, :], ACT.Sqrt).then_inc(s_unit, 1)

            def step_a(tau, b):
                if real(tau):
                    wait(eng, av_mom, tau + 1)
                    eng.activation(std[b][:, 0:1], mv[b][:, 1:2], ACT.Sqrt, bias=eps[:, :]).then_inc(as_std, 1)
                    wait(eng, av_nb, tau + 1)
                    wait(eng, ap_T, tau - 1)
                    eng.activation(h[b][:, :], xg[b][:, :], ACT.Relu, bias=nb[b][:, 0:1],
                                   scale=rstd[b][:, 0:1]).then_inc(as_h, 1)
                if real(tau - 1):
                    t, q = tau - 1, 1 - b
                    wait(eng, ap_T, t + 1)
                    wait(eng, ap_X, t - 1)
                    eng.activation(hT[q][:, 0:C], banks[1][:, 0:C], ACT.Copy)
                    eng.activation(hT[q][:, C:5 * C], banks[0][:, :], ACT.Copy).then_inc(as_hT, 1)
                if real(tau - 3):
                    t, q = tau - 3, 1 - b
                    apart(eng, g_const, t + 1, t - 1)
                    wait(eng, ap_O, t + 1)
                    wait(eng, av_P, t - 1)
                    eng.activation(Dr[q][:, :], banks[4][:, 0:3 * C], ACT.Copy,
                                   scale=rcut[:, bass.ds(t, 1)]).then_inc(as_D, 1)
                    apart(eng, g_const, dma_count(t - 2, q))
                    wait(eng, a_scat[q], dma_count(t - 2, q))
                    eng.activation(Pt[q][:, 0:C], banks[4][:, 3 * C:4 * C], ACT.Copy,
                                   scale=rcut[:, bass.ds(t, 1)]).then_inc(as_S, 1)
            over_tiles(eng, 3, step_a, PEEL_A)

            def step_b(tau, b):
                if real(tau - 1):
                    t, q = tau - 1, 1 - b
                    wait(eng, bv_neg, t + 1)
                    eng.activation(se[q][:, :], se[q][:, :], ACT.Exp).then_inc(bs_exp, 1)
                    wait(eng, bs_exp, t + 1)
                    eng.activation(se[q][:, :], se[q][:, :], ACT.Ln, bias=half[:, :], scale=0.5)\
                       .then_inc(bs_ln, 1)
            over_tiles(eng, 2, step_b)

            def step_c(tau, b):
                if real(tau):
                    wait(eng, cv_mom, 2 * (tau + 1))
                    eng.activation(std[b][:, :], mv[b][:, 1:4:2], ACT.Sqrt, bias=eps[:, :]).then_inc(cs_std, 1)
                    wait(eng, cv_nb, tau + 1)
                    wait(eng, cp_Td, tau - 1)
                    eng.activation(h[b][:, :], xd[b][:, :], ACT.Relu, bias=nb[b][:, 0:1],
                                   scale=rstd[b][:, 0:1]).then_inc(cs_hd, 1)
                    wait(eng, cp_Ts, tau - 1)
                    eng.activation(hs[b], xg[b][:, :], ACT.Relu, bias=nb[b][:, 1:2],
                                   scale=rstd[b][:, 1:2]).then_inc(cs_hs, 1)
                if real(tau - 2):
                    wait(eng, cp_E, tau - 1)
                    eng.activation(ex[b][:, :], banks[5][:, P:P + H], ACT.Exp).then_inc(cs_ex, 1)
                if real(tau):
                    wait(eng, cp_Td, tau + 1)
                    wait(eng, cp_q, tau - 1)
                    eng.activation(hTd[b], banks[0][:, :], ACT.Copy).then_inc(cs_hTd, 1)
                if real(tau - 2):
                    wait(eng, cp_oT, tau - 1)
                    wait(eng, cp_y, tau - 3)
                    eng.activation(oT[b][:, :], banks[6][:, :], ACT.Copy).then_inc(cs_oT, 1)
                if real(tau - 1):
                    t, q = tau - 1, 1 - b
                    wait(eng, cp_aT, t + 1)
                    wait(eng, cv_e, t - 1)
                    first = 0 if isinstance(t, int) and t == 0 else 1
                    eng.activation(aT[q][:, first:P], banks[5][0:H, first:P], ACT.Copy, scale=SCALE)\
                       .then_inc(cs_aT, 1)
            over_tiles(eng, 2, step_c)

        @block.tensor
        def _(eng):
            eng.wait_ge(d_wf, 80)
            for c in range(EP // D):
                if c >= 4:
                    eng.wait_ge(v_z, c - 3)
                eng.matmul(banks[4 + c % 4][:, :], wf1_sb[:, :], f_sb[:, c * D:(c + 1) * D],
                           start=True, stop=True).then_inc(p_pre, 1)

            def turn(s):
                eng.wait_ge(s.v_hot, 2)
                for r in range(-(-NT // 8)):
                    wait(eng, s.s_turn, r)
                    for t in range(8 * r, min(8 * r + 8, NT)):
                        last = eng.transpose(s.rows_bank[:, :].bitcast(bf16)[0:NHI, (t % 8) * P:(t % 8 + 1) * P],
                                             s.hi_hot[:, t, :], ident_b[:, :])
                    last.then_inc(s.p_turn, 1)

            def histogram(s, g):
                eng.wait_ge(s.v_hot, 3)
                wait(eng, s.s_hist, g)
                for j in range(Q):
                    o = s.sums_bank[0:NHI, j * P:(j + 1) * P]
                    for t in range(Q * g, Q * g + j + 1):
                        last = eng.matmul(o, s.hi_hot[:, t, :], s.lo_hot[:, t, :],
                                          start=(t == Q * g), stop=False)
                    last = eng.matmul(o, ident_h, s.earlier[:, Q * g * P:(Q * g + 1) * P], start=False, stop=True)
                last.then_inc(s.p_hist, 1)

            def starts(s):
                eng.wait_ge(s.v_first, 2)
                eng.wait_ge(v_const, 7)
                eng.matmul(s.sums_bank[0:NHI, P:P + 1], upto[0:NHI, 0:NHI], s.sum[:, :], start=True, stop=True)\
                   .then_inc(s.p_hist, 1)

            def same_high(s, r):
                wait(eng, s.v_same, r)
                eng.wait_ge(s.s_turn, -(-NT // 8))
                for t in range(Q * r, Q * r + Q):
                    rows = s.hi_rows[:, t * P:(t + 1) * P]
                    last = eng.matmul(s.rows_bank[:, (t % Q) * P:(t % Q + 1) * P], rows, rows, start=True, stop=True)
                last.then_inc(s.p_same, 1)

            def ranks(s, r):
                eng.wait_ge(s.v_first, 5)
                eng.wait_ge(s.s_hist, NT // Q)
                wait(eng, s.v_prod, r)
                eng.wait_ge(s.v_same, r + 1)
                for t in range(Q * r, Q * r + Q):
                    o = s.sums_bank[:, (t % Q) * P:(t % Q + 1) * P]
                    rows = s.hi_rows[:, t * P:(t + 1) * P]
                    eng.matmul(o, rows, s.first, start=True, stop=False)
                    eng.matmul(o, rows, s.earlier[:, t * P:(t + 1) * P], start=False, stop=False)
                    last = eng.matmul(o, s.same_keys[r % 2][:, (t % Q) * P:(t % Q + 1) * P], s.lo_hot[:, t, :],
                                      start=False, stop=True)
                last.then_inc(s.p_rank, 1)

            eng.wait_ge(v_const, 5)
            for s in sorts:
                turn(s)
            for g in range(NT // Q):
                for s in sorts:
                    histogram(s, g)
            for s in sorts:
                starts(s)
                same_high(s, 0)
            for c in range(EP // D):
                eng.wait_ge(v_hid, 1)
                for k in range(4):
                    if c > 0:
                        eng.wait_ge(v_filt if k % 2 else s_filt, 2 * (c - 1) + k // 2 + 1)
                    eng.matmul(banks[4 + k][:, :], wf2_sb[:, k, :], fz[:, c * D:(c + 1) * D],
                               start=True, stop=True).then_inc(p_filt, 1)
                for s in sorts:
                    if c + 1 < NT // Q:
                        same_high(s, c + 1)
                    ranks(s, c)
            eng.wait_ge(d_wl0, 144)
            eng.wait_ge(by_src.v_prod, NT // Q)
            eng.matmul(banks[0][:, 0:C], w1v_t_sb[:, :], w2v_sb[:, :], start=True, stop=True)
            eng.matmul(banks[0][:, C:2 * C], w1vt_b_sb[:, :], w2v_sb[:, :], start=True, stop=True).then_inc(p_wv, 1)
            eng.wait_ge(s_filt, NT // 2)
            eng.wait_ge(v_filt, NT // 2)
            eng.wait_ge(v_wv, 1)
            eng.wait_ge(by_dst.v_rank, NT // Q + 1)

            def step_a(tau, b):
                if real(tau - 2):
                    t = tau - 2
                    wait(eng, as_hT, t + 1)
                    wait(eng, av_M, t)
                    eng.matmul(banks[3][:, 0:C], w_s_sb[:, :], hT[b][:, 0:C], start=True, stop=True)
                    eng.matmul(banks[2][:, :], w_v_sb[:, :], hT[b][:, C:5 * C], start=True, stop=True)\
                       .then_inc(ap_X, 1)
                if real(tau - 1):
                    t, q = tau - 1, 1 - b
                    wait(eng, as_h, t + 1)
                    wait(eng, as_hT, t)
                    eng.transpose(banks[1][:, 0:C], h[q][:, 0:C], ident[:, :])
                    hv = h[q][:, C:4 * C].rearrange("p (c i) -> p i c", i=3)
                    for i in range(3):
                        eng.transpose(banks[0][:, i * C:(i + 1) * C], hv[:, i, :], ident[:, :])
                    wait(eng, av_hd, t + 1)
                    eng.transpose(banks[0][:, 3 * C:4 * C], hd[q][:, :], ident[:, :]).then_inc(ap_T, 1)
                if real(tau - 3):
                    t, q = tau - 3, 1 - b
                    wait(eng, av_M, t + 1)
                    wait(eng, as_S, t)
                    wait(eng, av_P, t)
                    for i in range(3):
                        eng.matmul(banks[4][:, i * C:(i + 1) * C], M[q][:, 3 + i, :], wvb[:, :],
                                   start=True, stop=True)
                    eng.matmul(banks[4][:, 3 * C:4 * C], M[q][:, 0, :], w1s_sb[:, 0, :], start=True, stop=False)
                    eng.matmul(banks[4][:, 3 * C:4 * C], M[q][:, 1, :], w1s_sb[:, 1, :], start=False, stop=True)
                    eng.matmul(banks[5][:, 0:C], M[q][:, 2, :], wva[:, :], start=True, stop=True)\
                       .then_inc(ap_O, 1)
            over_tiles(eng, 3, step_a, PEEL_A)

            def step_b(tau, b):
                if real(tau - 1):
                    t, q = tau - 1, 1 - b
                    wait(eng, bv_mask, t + 1)
                    wait(eng, b_P[q], dma_count(t, q))
                    wait(eng, bv_carry, t + 1)
                    wait(eng, bv_x1, t - 1)
                    eng.matmul(banks[q][:, :], mask[q][:, :], Pt[q][:, :], start=True, stop=True).then_inc(bp_cum, 1)
                    wait(eng, bv_neg, t)
                    eng.matmul(banks[2][:, 0:P], Pt[q][:, 0:C], mask[q][:, :], start=True, stop=True)\
                       .then_inc(bp_st, 1)
                if real(tau - 2):
                    t = tau - 2
                    wait(eng, bv_sp, t + 1)
                    wait(eng, bv_x1, t)
                    eng.matmul(banks[3][:, 0:C], sp[b][:, :], w2s_sb[:, :], start=True, stop=True).then_inc(bp_s2, 1)
            over_tiles(eng, 2, step_b)
            eng.wait_ge(d_wl1, 64)

            def project(bank, hT_, w, s):
                for k in range(4):
                    last = eng.matmul(bank[:, :], hT_[:, k * C:(k + 1) * C], w[:, k, :], start=(k == 0), stop=(k == 3))
                last.then_inc(s, 1)

            def step_c(tau, b):
                if real(tau - 1):
                    t, q = tau - 1, 1 - b
                    wait(eng, cs_hTd, t + 1)
                    wait(eng, cv_q, t)
                    project(banks[1], hTd[q], wq_sb, cp_q)
                if real(tau - 2):
                    apart(eng, g_const, tau - 1)
                    wait(eng, cv_e, tau - 1)
                    wait(eng, cs_aT, tau - 1)
                    eng.transpose(banks[5][:, P:P + H], eT[b][:, :], ident[0:H, 0:H]).then_inc(cp_E, 1)
                if real(tau - 1):
                    wait(eng, cv_hTs, t + 1)
                    wait(eng, cv_k, t)
                    project(banks[2], hTs[q], wk_sb, cp_k)
                if real(tau - 2):
                    t2 = tau - 2
                    wait(eng, cv_vw, t2 + 1)
                    wait(eng, cv_carry, t2 + 1)
                    wait(eng, cv_y, t2)
                    wait(eng, cv_o, t2)
                    eng.matmul(banks[4][:, :], mask[b][:, :], vw[b][:, 0:D], start=True, stop=True)
                    eng.matmul(banks[7][:, 0:H], mask[b][:, :], vw[b][:, D:D + H], start=True, stop=True)\
                       .then_inc(cp_cum, 1)
                if real(tau):
                    wait(eng, cs_hd, tau + 1)
                    wait(eng, cv_hTs, tau)
                    for k in range(4):
                        last = eng.transpose(banks[0][:, k * C:(k + 1) * C], h[b][:, k * C:(k + 1) * C], ident[:, :])
                    last.then_inc(cp_Td, 1)
                if real(tau - 1):
                    wait(eng, cv_v, t)
                    project(banks[3], hTs[q], wv_sb, cp_v)
                if real(tau):
                    wait(eng, cs_hs, tau + 1)
                    wait(eng, cs_hTd, tau + 1)
                    for k in range(4):
                        last = eng.transpose(banks[0][:, k * C:(k + 1) * C], hs[b][:, k * C:(k + 1) * C], ident[:, :])
                    last.then_inc(cp_Ts, 1)
                if real(tau - 2):
                    wait(eng, cv_o, t2 + 1)
                    wait(eng, cs_oT, t2)
                    for k in range(4):
                        last = eng.transpose(banks[6][:, k * C:(k + 1) * C], o_sb[b][:, k * C:(k + 1) * C], ident[:, :])
                    last.then_inc(cp_oT, 1)
                if real(tau - 1):
                    wait(eng, cv_a, t + 1)
                    wait(eng, cs_ex, t)
                    eng.transpose(banks[5][0:H, 0:P], a_sb[q][:, :], ident[:, :]).then_inc(cp_aT, 1)
                if real(tau - 2):
                    wait(eng, cs_oT, t2 + 1)
                    if not isinstance(t2, int) or t2 < NT - 1:
                        wait(eng, cv_carry, t2 + 2)
                    project(banks[7], oT[b], wo_sb, cp_y)
            over_tiles(eng, 2, step_c)

        @block.vector
        def _(eng):
            def by_tile(row):
                return row[:, :].rearrange("p (t e) -> p t e", t=NT)

            def link(ins, s, n):
                ins.then_inc(s, 1)
                wait(eng, s, n)

            eng.wait_ge(g_const, 8)
            eng.tensor_scalar(ident_b[:, :], dist[:, :], 0.0, None, ALU.is_equal).then_inc(v_const, 1)
            eng.tensor_scalar(ident[:, :], dist[:, :], 0.0, None, ALU.is_equal).then_inc(v_const, 1)
            eng.tensor_scalar(ident_h, dist[0:NHI, 0:NHI], 0.0, None, ALU.is_equal).then_inc(v_const, 1)
            eng.wait_ge(d_cols, 32)

            for s in sorts:
                eng.tensor_scalar(s.hi[:, :], s.keys, 7, None, ALU.logical_shift_right)
                eng.tensor_scalar(s.lo[:, :], s.keys, P - 1, None, ALU.bitwise_and).then_inc(s.v_hot, 1)
            for s in sorts:
                eng.memset(s.earlier[:, 0:P], -float(MID)).then_inc(v_const, 1)
                eng.wait_ge(s.v_hot, 1)
                for digit, hot, w in ((s.hi, s.hi_hot, NHI), (s.lo, s.lo_hot, P)):
                    eng.tensor_tensor(hot, lane[:, 0:w].unsqueeze(1).broadcast_to([P, NT, w]),
                                      digit[:, :].unsqueeze(2).broadcast_to([P, NT, w]), ALU.is_equal)\
                       .then_inc(s.v_hot, 1)

            def first_rows(s):
                eng.wait_ge(s.s_hist, NT // Q)
                eng.tensor_scalar(s.total, s.total, float(MID), None, ALU.add).then_inc(s.v_first, 1)
                eng.wait_ge(s.v_first, 1)
                eng.tensor_reduce(s.sum[:, :], s.total, AX.X, ALU.add).then_inc(s.v_first, 1)
                eng.wait_ge(s.p_hist, NT // Q + 1)
                eng.scalar_tensor_tensor(s.start[:, :], s.sums_bank[0:NHI, P:P + 1], 1.0, s.sum[:, :],
                                         ALU.add, ALU.subtract).then_inc(s.v_first, 1)
                eng.wait_ge(s.v_first, 3)
                eng.tensor_tensor_scan(s.run, s.total, s.total, s.start[:, :],
                                       ALU.add, ALU.max).then_inc(s.v_first, 1)
                eng.wait_ge(s.v_first, 4)
                eng.scalar_tensor_tensor(s.first, s.run, float(MID), s.total, ALU.subtract, ALU.subtract)\
                   .then_inc(s.v_first, 1)

            def same_before(s, r):
                eng.wait_ge(s.p_same, r + 1)
                wait(eng, s.p_rank, r - 1)
                eng.tensor_tensor(s.same_keys[r % 2].rearrange("p (t e) -> p t e", t=Q),
                                  s.rows_bank[:, :].rearrange("p (t e) -> p t e", t=Q),
                                  before[:, :].unsqueeze(1).broadcast_to([P, Q, P]), ALU.mult).then_inc(s.v_same, 1)

            def take_ranks(s, r):
                eng.wait_ge(s.p_rank, r + 1)
                p = s.looked_up[r % 2][:, :].rearrange("p (t e) -> p t e", t=Q)
                wait(eng, s.v_rank, r - 1)
                eng.tensor_tensor(p, s.sums_bank[:, :].rearrange("p (t e) -> p t e", t=Q),
                                  s.lo_hot[:, Q * r:Q * r + Q, :], ALU.mult).then_inc(s.v_prod, 1)
                eng.wait_ge(s.v_prod, r + 1)
                eng.tensor_reduce(s.count[:, Q * r:Q * r + Q], p, AX.X, ALU.add).then_inc(s.v_rank, 1)

            eng.tensor_scalar(xidx[:, :], edge_i[:, :, 0], float(N - 1), None, ALU.min).then_inc(v_keys, 1)
            for c in range(EP // D):
                eng.wait_ge(p_pre, c + 1)
                eng.tensor_scalar(fz[:, c * D:(c + 1) * D], banks[4 + c % 4][:, :], bf1_sb[:, :], None, ALU.add)\
                   .then_inc(v_z, 1)
            eng.wait_ge(v_z, EP // D)
            eng.scalar_tensor_tensor(fe[:, :], fz[:, :], -1.0, fz[:, :], ALU.mult, ALU.min)\
               .then_inc(v_neg, 1)
            eng.tensor_scalar(upto[:, :], dist[:, :], 0.0, None, ALU.is_ge).then_inc(v_const, 1)
            eng.tensor_scalar(before[:, :], dist[:, :], 0.0, None, ALU.is_gt).then_inc(v_const, 1)
            eng.wait_ge(d_wl0, 144)
            v3 = [rcut[:, :].unsqueeze(2).broadcast_to([P, NT, 3]), rn2[:, :].unsqueeze(2).broadcast_to([P, NT, 3])]
            link(eng.tensor_tensor(r_sq[:, :, :], r_sb[:, :, :], r_sb[:, :, :], ALU.mult), v_keys, 2)
            eng.tensor_reduce(rn2[:, :], r_sq[:, :, :], AX.X, ALU.add).then_inc(v_unit, 1)
            eng.wait_ge(s_soft, 2)
            eng.scalar_tensor_tensor(fz[:, :], fz[:, :], 0.0, fe[:, :], ALU.max, ALU.add).then_inc(v_hid, 1)
            eng.wait_ge(v_const, 7)
            for s in sorts:
                first_rows(s)
                same_before(s, 0)
            for c in range(EP // D):
                for k in (1, 3):
                    eng.wait_ge(p_filt, 4 * c + k + 1)
                    eng.tensor_scalar(WT[:, k, c * D:(c + 1) * D], banks[4 + k][:, :], bf2_sb[:, k:k + 1], None,
                                      ALU.add).then_inc(v_filt, 1)
                for s in sorts:
                    if c + 1 < NT // Q:
                        same_before(s, c + 1)
                    take_ranks(s, c)
            for s in sorts:
                eng.wait_ge(s.v_rank, NT // Q)
                eng.tensor_scalar(s.rank[:, :], s.count[:, :], float(2 * MID), None, ALU.add).then_inc(s.v_rank, 1)
            eng.wait_ge(s_unit, 1)
            link(eng.reciprocal(rn2[:, :], rn[:, :]), v_unit, 2)
            link(eng.tensor_tensor(u[:, :, :], r_sb[:, :, :], v3[1], ALU.mult), v_unit, 3)
            eng.tensor_tensor(ur[:, :, :], u[:, :, :], v3[0], ALU.mult).then_inc(v_unit, 1)
            eng.wait_ge(v_unit, 4)
            eng.wait_ge(p_wv, 1)
            eng.tensor_copy(wva[:, :], banks[0][:, 0:C])
            eng.tensor_copy(wvb[:, :], banks[0][:, C:2 * C]).then_inc(v_wv, 1)
            eng.wait_ge(s_filt, NT // 2)
            eng.wait_ge(v_filt, NT // 2)
            eng.wait_ge(v_wv, 1)
            eng.wait_ge(d_const, 16)

            def step_a(tau, b):
                if real(tau):
                    wait(eng, a_x[b], dma_count(tau, b))
                    eng.bn_stats(st[b][:, 0:6], xg[b][:, :]).then_inc(av_stats, 1)
                    apart(eng, g_const, tau + 1)
                    wait(eng, av_stats, tau + 1)
                    eng.bn_aggr(mv[b][:, 0:2], st[b][:, 0:6]).then_inc(av_mom, 1)
                if real(tau - 1):
                    t, q = tau - 1, 1 - b
                    wait(eng, as_h, t + 1)
                    wait(eng, ap_T, t - 1)
                    hv = h[q][:, C:4 * C].rearrange("p (c i) -> p i c", i=3)
                    eng.tensor_scalar(hd[q][:, :], hv[:, 0, :], u[:, t, 0:1], None, ALU.mult).then_inc(av_hdp, 1)
                    wait(eng, av_hdp, 2 * t + 1)
                    eng.scalar_tensor_tensor(hd[q][:, :], hv[:, 1, :], u[:, t, 1:2], hd[q][:, :],
                                             ALU.mult, ALU.add).then_inc(av_hdp, 1)
                    wait(eng, av_hdp, 2 * t + 2)
                    eng.scalar_tensor_tensor(hd[q][:, :], hv[:, 2, :], u[:, t, 2:3], hd[q][:, :],
                                             ALU.mult, ALU.add).then_inc(av_hd, 1)
                if real(tau - 4):
                    t = tau - 4
                    wait(eng, as_D, t + 1)
                    wait(eng, a_scat[b], dma_count(t - 2, b))
                    pv = Pt[b][:, C:4 * C].rearrange("p (c i) -> p i c", i=3)
                    for i in range(3):
                        last = eng.scalar_tensor_tensor(pv[:, i, :], banks[5][:, 0:C], ur[:, t, i:i + 1],
                                                        Dr[b][:, i * C:(i + 1) * C], ALU.mult, ALU.add)
                    last.then_inc(av_P, 1)
                if real(tau):
                    wait(eng, as_std, tau + 1)
                    eng.reciprocal(rstd[b][:, 0:1], std[b][:, 0:1]).then_inc(av_rstd, 1)
                    wait(eng, av_rstd, tau + 1)
                    eng.scalar_tensor_tensor(nb[b][:, 0:1], mv[b][:, 0:1], -1.0, rstd[b][:, 0:1],
                                             ALU.mult, ALU.mult).then_inc(av_nb, 1)
                if real(tau - 2):
                    t = tau - 2
                    wait(eng, ap_X, t + 1)
                    wait(eng, ap_O, t - 1)
                    w = [WT[:, k, bass.ds(P * t, P)] for k in range(4)]
                    stt = eng.scalar_tensor_tensor
                    stt(M[b][:, 0, :], banks[3][:, 0:C], SC_A, w[0], ALU.mult, ALU.mult)
                    stt(M[b][:, 2, :], banks[3][:, 0:C], SC_C, w[2], ALU.mult, ALU.mult)
                    stt(M[b][:, 1, :], banks[2][:, 3 * C:4 * C], SC_B, w[1], ALU.mult, ALU.mult)
                    stt(M[b][:, 3:6, :], banks[2][:, 0:3 * C].rearrange("p (i c) -> p i c", i=3), SC_D,
                        w[3].unsqueeze(1).broadcast_to([P, 3, C]), ALU.mult, ALU.mult).then_inc(av_M, 1)
                if real(tau):
                    add_bias(eng, tau, b, v_base)
            over_tiles(eng, 4, step_a, PEEL_A)

            eng.wait_ge(d_sk, 48)
            eng.tensor_copy(sk_f[:, :], src_keys)
            eng.tensor_copy(kn_f[:, :], kn_i[:, :, 0])
            eng.tensor_scalar(sx_i[:, :], ko_i[:, :, 0], float(N - 1), None, ALU.min)
            eng.tensor_copy(sk_c[:, :], ko_i[:, :, 0]).then_inc(bv_sk, 1)
            eng.wait_ge(bv_sk, 1)

            def last_rows(key_c, rows_i, s, n):
                eng.tensor_tensor(cont[:, :], key_c[:, :], kn_f[:, :], ALU.is_equal).then_inc(s, 1)
                eng.wait_ge(s, n)
                eng.scalar_tensor_tensor(cont[:, :], cont[:, :], float(OFF), key_c[:, :], ALU.mult, ALU.add)\
                   .then_inc(s, 1)
                eng.wait_ge(s, n + 1)
                eng.memset(cont[0:1, :], float(OFF)).then_inc(s, 1)
                eng.wait_ge(s, n + 2)
                eng.tensor_copy(rows_i[:, :], cont[:, :]).then_inc(s, 1)
                eng.wait_ge(s, n + 3)
            last_rows(sk_c, srow_i, bv_sk, 2)
            eng.nop().then_inc(v_sorted, 1)

            def masks(t, b, keys, col, s):
                eng.scalar_tensor_tensor(mask[b][:, 1:P], keys[:, bass.ds(G * t + 1, G)], col[:, bass.ds(t, 1)],
                                         upto[:, 1:P], ALU.is_equal, ALU.mult)
                eng.tensor_scalar(mask[b][:, 0:1], keys[:, bass.ds(G * t + G, 1)], col[:, bass.ds(t, 1)], None,
                                  ALU.is_equal).then_inc(s, 1)

            def dst_records():
                eng.wait_ge(d_dk, 48)
                rec = records.rearrange("p (e two) -> p e two", two=2)
                eng.tensor_copy(dk_f[:, :], rec[:, :, 0])
                eng.tensor_copy(kn_f[:, :], kn_i[:, :, 0])
                eng.tensor_scalar(dx_i[:, :], ko_i[:, :, 0], float(N - 1), None, ALU.min)
                eng.tensor_scalar(ds_i[:, :], ko_i[:, :, 1], float(N - 1), None, ALU.min)
                eng.tensor_copy(dk_c[:, :], ko_i[:, :, 0]).then_inc(bv_sk, 1)
                eng.wait_ge(bv_sk, 6)
                last_rows(dk_c, drow_i, bv_sk, 7)
                eng.nop().then_inc(v_sorted, 1)

            eng.wait_ge(d_bias, 64)

            def step_b(tau, b):
                if isinstance(tau, int) and tau == PEEL - 1:
                    dst_records()
                if real(tau - 1) and (not isinstance(tau, int) or tau - 1 > 0):
                    t, q = tau - 1, 1 - b
                    wait(eng, b_P[q], dma_count(t, q))
                    wait(eng, bp_cum, t)
                    eng.tensor_copy(Pt[q][0:1, :], banks[b][0:1, :]).then_inc(bv_carry, 1)
                elif real(tau - 1):
                    eng.nop().then_inc(bv_carry, 1)
                if real(tau):
                    wait(eng, bp_st, tau - 1)
                    masks(tau, b, sk_f, sk_c, bv_mask)
                if real(tau - 1):
                    t, q = tau - 1, 1 - b
                    wait(eng, bp_st, t + 1)
                    wait(eng, bp_s2, t - 1)
                    eng.tensor_scalar(sz[q][:, :], banks[2][:, 0:P], 0.0, None, ALU.max).then_inc(bv_pos, 1)
                    wait(eng, bv_pos, t + 1)
                    eng.scalar_tensor_tensor(se[q][:, :], sz[q][:, :], -2.0, banks[2][:, 0:P], ALU.mult, ALU.add)\
                       .then_inc(bv_neg, 1)
                if real(tau - 2):
                    t = tau - 2
                    wait(eng, bp_s2, t + 1)
                    wait(eng, b_x[b], dma_count(t, b))
                    eng.scalar_tensor_tensor(XO[:, t, 0:C], banks[3][:, 0:C], SC_S2, xg[b][:, 0:C],
                                             ALU.mult, ALU.add)
                    eng.tensor_tensor(XO[:, t, C:D], banks[b][:, C:D], xg[b][:, C:D], ALU.add).then_inc(bv_x1, 1)
                if real(tau - 1):
                    t, q = tau - 1, 1 - b
                    wait(eng, bs_ln, t + 1)
                    wait(eng, bv_pos, t + 1)
                    eng.tensor_tensor(sp[q][:, :], sz[q][:, :], se[q][:, :], ALU.add).then_inc(bv_sp, 1)
                if real(tau - 4):
                    t = tau - 4
                    wait(eng, b_x1c[b], dma_count(t, b))
                    eng.tensor_tensor(XO[:, t, :], XO[:, t, :], bo_sb[:, :], ALU.add).then_inc(bv_xo, 1)
            over_tiles(eng, 4, step_b)
            eng.tensor_tensor(same[:, 1:KW + 1], dk_f[0:H, 1:KW + 1], dk_f[0:H, 0:KW], ALU.is_equal)
            eng.memset(same[:, 0:1], 0.0).then_inc(bv_sk, 1)
            eng.wait_ge(bv_sk, 11)
            eng.tensor_scalar(same[:, :], same[:, :], 0.5, BIG, ALU.subtract, ALU.mult)\
               .then_inc(bv_sk, 1)
            eng.wait_ge(bv_sk, 12)
            eng.wait_ge(g_ones, 2)

            def step_c(tau, b):
                if real(tau):
                    wait(eng, c_xd[b], dma_count(tau, b))
                    eng.bn_stats(st[b][:, 0:6], xd[b][:, :])
                    wait(eng, c_xs[b], dma_count(tau, b))
                    eng.bn_stats(st[b][:, 6:12], xg[b][:, :]).then_inc(cv_stats, 2)
                    apart(eng, g_const, 2 * (tau + 1))
                    wait(eng, cv_stats, 2 * (tau + 1))
                    eng.bn_aggr(mv[b][:, 0:2], st[b][:, 0:6])
                    eng.bn_aggr(mv[b][:, 2:4], st[b][:, 6:12]).then_inc(cv_mom, 2)
                if real(tau - 2):
                    t = tau - 2
                    wait(eng, cs_aT, t + 1)
                    if not isinstance(t, int) or t > 0:
                        eng.tensor_copy(aT[b][:, 0:1], mT[1 - b][:, P - 1:P]).then_inc(cv_fwd, 1)
                    else:
                        eng.nop().then_inc(cv_fwd, 1)
                    wait(eng, cv_fwd, 3 * t + 1)
                    wait(eng, cv_e, t - 1)
                    eng.tensor_tensor_scan(eT[b][:, 1:P], same[:, bass.ds(G * t + 1, G)], aT[b][:, 1:P],
                                           aT[b][:, 0:1], ALU.min, ALU.max).then_inc(cv_fwd, 1)
                    eng.tensor_copy(eT[b][:, 0:1], aT[b][:, 0:1])
                    eng.tensor_copy(same_back[:, ::-1], same[:, bass.ds(G * t + 1, P)]).then_inc(cv_fwd, 1)
                    wait(eng, cv_fwd, 3 * t + 3)
                    eng.tensor_tensor_scan(mT[b][:, :][:, ::-1], same_back[:, :],
                                           eT[b][:, :][:, ::-1], -BIG, ALU.min, ALU.max).then_inc(cv_bwd, 1)
                    wait(eng, cv_bwd, t + 1)
                    eng.tensor_tensor(eT[b][:, :], aT[b][:, :], mT[b][:, :], ALU.subtract).then_inc(cv_e, 1)
                    wait(eng, cp_cum, t - 1)
                    masks(t, b, dk_f, dk_c, cv_mask)
                if real(tau):
                    wait(eng, cs_std, tau + 1)
                    eng.reciprocal(rstd[b][:, :], std[b][:, :]).then_inc(cv_rstd, 1)
                    wait(eng, cv_rstd, tau + 1)
                    eng.scalar_tensor_tensor(nb[b][:, :], mv[b][:, 0:4:2], -1.0, rstd[b][:, :],
                                             ALU.mult, ALU.mult).then_inc(cv_nb, 1)
                if real(tau - 1):
                    t, q = tau - 1, 1 - b
                    wait(eng, cp_q, t + 1)
                    eng.tensor_tensor(qs[q], banks[1][:, :], bq_sb[:, :], ALU.add).then_inc(cv_q, 1)
                if real(tau - 2):
                    t2 = tau - 2
                    wait(eng, cs_ex, t2 + 1)
                    wait(eng, cp_cum, t2 - 1)
                    wait(eng, cv_carry, t2 + 1)
                    wait(eng, cv_v, t2 + 1)
                    eng.tensor_tensor(vw[b][:, 0:D].rearrange("p (h d) -> p h d", h=H),
                                      va[b][:, 0:D].rearrange("p (h d) -> p h d", h=H),
                                      ex[b][:, :].unsqueeze(2).broadcast_to([P, H, DH]), ALU.mult)
                    eng.tensor_tensor(vw[b][:, D:D + H], va[b][:, D:D + H], ex[b][:, :], ALU.mult).then_inc(cv_vw, 1)
                if real(tau - 1):
                    wait(eng, cp_k, t + 1)
                    eng.tensor_tensor(ks[q], banks[2][:, :], bk_sb[:, :], ALU.add).then_inc(cv_k, 1)
                    wait(eng, cv_k, t + 1)
                    eng.tensor_tensor(ks[q], ks[q], qs[q], ALU.mult).then_inc(cv_prod, 1)
                    wait(eng, cv_prod, t + 1)
                    wait(eng, cp_aT, t - 1)
                    eng.tensor_reduce(a_sb[q][:, :], ks[q].rearrange("p (h d) -> p h d", h=H), AX.X, ALU.add)\
                       .then_inc(cv_a, 1)
                if real(tau - 2):
                    wait(eng, cp_cum, t2 + 1)
                    eng.tensor_scalar(rden[b][:, :], banks[7][:, 0:H], 1e-30, None, ALU.max).then_inc(cv_den, 1)
                    wait(eng, cv_den, t2 + 1)
                    eng.reciprocal(rden[b][:, :], rden[b][:, :]).then_inc(cv_rden, 1)
                    wait(eng, cv_rden, t2 + 1)
                    wait(eng, cp_oT, t2 - 1)
                    eng.tensor_tensor(o_sb[b].rearrange("p (h d) -> p h d", h=H),
                                      banks[4][:, :].rearrange("p (h d) -> p h d", h=H),
                                      rden[b][:, :].unsqueeze(2).broadcast_to([P, H, DH]), ALU.mult)\
                       .then_inc(cv_o, 1)
                if real(tau - 1):
                    wait(eng, cp_v, t + 1)
                    eng.tensor_tensor(va[q][:, 0:D], banks[3][:, :], bv_sb[:, :], ALU.add).then_inc(cv_v, 1)
                    if not isinstance(t, int) or t > 0:
                        wait(eng, cv_v, t + 1)
                        eng.tensor_copy(va[q][0:1, 0:D], banks[4][0:1, :])
                        eng.tensor_copy(va[q][0:1, D:D + H], banks[7][0:1, 0:H]).then_inc(cv_carry, 1)
                    else:
                        eng.nop().then_inc(cv_carry, 1)
                if real(tau):
                    wait(eng, cp_Ts, tau + 1)
                    eng.tensor_copy(hTs[b], banks[0][:, :]).then_inc(cv_hTs, 1)
                if real(tau - 2):
                    wait(eng, cp_y, t2 + 1)
                    wait(eng, c_out[b], dma_count(t2 - 2, b))
                    wait(eng, cg_y, t2 + 1)
                    eng.tensor_tensor(y[b][:, :], banks[7][:, :], xb[b][:, :], ALU.add).then_inc(cv_y, 1)
            over_tiles(eng, 2, step_c)


def _tiles(a, fill):
    rest = np.full((EP - E,) + a.shape[1:], fill, a.dtype)
    a = np.concatenate([a, rest]).reshape((NT, P) + a.shape[1:])
    return np.ascontiguousarray(np.swapaxes(a, 0, 1))


def _blocks(w):
    return np.ascontiguousarray(w.T.reshape(4, C, D).transpose(1, 0, 2))


def kernel(**inputs):
    import concourse.bacc as _bacc
    from concourse.bass_utils import run_bass_kernel_spmd as _run

    a = {k: np.asarray(v) for k, v in inputs.items()}
    src, dst = a["src"], a["dst"]
    l0 = {k[len("L0_gnn_"):]: v for k, v in a.items() if k.startswith("L0_gnn_")}
    l1 = {k[len("L1_gnn_"):]: v for k, v in a.items() if k.startswith("L1_gnn_")}
    w_kv = l1["Wkv"].reshape(H, 2, DH, D)
    b_kv = l1["bkv"].reshape(H, 2, DH)
    order = [
        ("x", a["x"]),
        ("src_cols", _tiles(src, NONE)), ("edge_cols", _tiles(np.stack([dst, src], 1), NONE)),
        ("f_t", np.ascontiguousarray(np.concatenate(
            [a["edge_attr_20"], np.zeros((EP - E, NRBF), a["edge_attr_20"].dtype)]).T)),
        ("rcut_cols", _tiles(a["edge_weight"], 0)), ("r_cols", _tiles(a["edge_attr_3"], 1)),
        ("w_s", l0["W_in2f_s"]), ("w_v", l0["W_in2f_v"]),
        ("wf1", l0["Wf1"]), ("bf1", l0["bf1"].reshape(C, 1)),
        ("wf2", l0["Wf2"][:, :4 * C].reshape(C, 2, C, 2).transpose(0, 1, 3, 2).reshape(C, 4, C)),
        ("bf2", l0["bf2"][:4 * C].reshape(2, C, 2).transpose(1, 0, 2).reshape(C, 4)),
        ("w1s", l0["W1_s"].reshape(C, 2, C)),
        ("w1v_t", l0["W1_v"].reshape(C, 2, C).transpose(1, 2, 0)),
        ("w2s", l0["W2_s"]), ("w2v", l0["W2_v"]),
        ("wq", _blocks(l1["Wq"])), ("bq", l1["bq"].reshape(1, D)),
        ("wk", _blocks(w_kv[:, 0].reshape(D, D))), ("bk", b_kv[:, 0].reshape(1, D)),
        ("wv", _blocks(w_kv[:, 1].reshape(D, D))), ("bv", b_kv[:, 1].reshape(1, D)),
        ("wo", _blocks(l1["Wo"])), ("bo2", np.concatenate([l1["bo"], l1["bo"]]).reshape(1, 2 * D)),
    ]
    nc = _bacc.Bacc("TRN2", target_bir_lowering=False, num_devices=1)
    arrays, args = {}, {}
    for name, v in order:
        v = np.ascontiguousarray(v)
        arrays[name + "_dram"] = v
        args[name] = nc.dram_tensor(name + "_dram", v.shape, mybir.dt.from_np(v.dtype), kind="ExternalInput").ap()
    f32, i32 = mybir.dt.float32, mybir.dt.int32
    args["out"] = nc.dram_tensor("out_dram", (N, D), f32, kind="ExternalOutput").ap()
    for name, shape, dt in (("psort", (ROWS, D), f32), ("skey", (ROWS, 1), i32), ("drec", (ROWS, 2), i32),
                            ("table", (P * 80, 1), i32), ("x1c", (EP, D), f32)):
        args[name] = nc.dram_tensor(name + "_scratch", shape, dt).ap()
    gnn_kernel(nc, **args)
    r = _run(nc, [arrays], core_ids=[0])
    return r.results[0]["out_dram"]
```

```python
import math

import numpy as np

import concourse.bass as bass
from concourse import mybir
from contextlib import ExitStack

P = 128
N = 10000
E = 2500
D = 512
C = 128
H = 8
DH = D // H
NRBF = 20
NT = 20
EP = NT * P
G = P - 1
ROWS = EP + 1
KW = G * NT + 1
NHI = N // P + 1
Q = 4
NONE = N
NOROW = 30000
OFF = 20000
PEEL = 4
PEEL_A = 6
CH = 1024
FLAT = N * D // P
NCH = -(-FLAT // CH)
FIRST = 12
REST = NCH - FIRST - NT
EPS = 1e-5
Y0 = 1.0 / math.sqrt(4.0 * math.pi)
Y1 = math.sqrt(3.0 / (4.0 * math.pi))
BIG = 3.0e38
H_SCALE = 2.0 ** 11
W_TOP = 2.0 ** 14
EXPONENT = 0x7F800000
ONE_OVER = 254 << 23


def wait(eng, sem, n):
    if isinstance(n, int) and n <= 0:
        return
    eng.wait_ge(sem, n)


def dma_count(t, b):
    return 8 * (t - b) + 16


def apart(eng, made, *values):
    for v in values:
        if not isinstance(v, int):
            eng.lower_val(v)
    eng.wait_ge(made, 8)


def real(t):
    return not isinstance(t, int) or 0 <= t < NT


def sent_with(step):
    return NT * (step - 1) // (PEEL - 1), NT * step // (PEEL - 1)


def chunk_width(c):
    return FLAT - c * CH if isinstance(c, int) and c == NCH - 1 else CH


def over_tiles(eng, lag, step, peel=PEEL):
    for tau in range(peel):
        step(tau, tau % 2)
    with eng.Fori(0, (NT - peel) // 2) as k:
        step(2 * k + peel, 0)
        step(2 * k + peel + 1, 1)
    for tau in range(NT, NT + lag):
        step(tau, tau % 2)


def gnn_kernel(nc, x, src_cols, edge_cols, f_t, rcut_cols, r_cols,
               w_s, w_v, wf1, bf1, wf2, bf2, w1s, w1v_t, w2s, w2v,
               wq, bq, wk, bk, wv, bv, wo, bo2, out,
               psort, skey, drec, table, x1c):
    f32 = mybir.dt.float32
    i32 = mybir.dt.int32
    bf16 = mybir.dt.bfloat16
    f16 = mybir.dt.float16
    MID = EP // 2
    ALU = mybir.AluOpType
    ACT = mybir.ActivationFunctionType
    AX = mybir.AxisListType

    RC, RF = 1.0 / math.sqrt(C), 1.0 / math.sqrt(2 * C)
    SC_A = Y0 * RC * RF
    SC_B = Y1 / math.sqrt(3.0) * RC * RF
    SC_C = Y1 * RC * RF * RC
    SC_D = Y0 * RC * RF * RC
    SC_S2 = RC
    SCALE = 1.0 / math.sqrt(DH)

    x_flat = x.rearrange("n d -> (n d)").rearrange("(p f) -> p f", p=P)
    out_flat = out.rearrange("n d -> (n d)").rearrange("(p f) -> p f", p=P)

    ctx = ExitStack()
    with ctx:
        def sb(name, shape, dt=f32):
            return ctx.enter_context(nc.sbuf_tensor(name, shape, dt))

        def pb(name, shape, dt=f32):
            return ctx.enter_context(nc.psum_tensor(name, shape, dt))

        def sem(name):
            return ctx.enter_context(nc.semaphore(name))

        def pair(name, shape, dt=f32):
            return [sb(f"{name}{b}", shape, dt) for b in range(2)]

        def sems(name):
            return [sem(f"{name}{b}") for b in range(2)]

        WT = sb("WT", [P, 4, EP])
        XO = sb("XO", [P, NT, D])
        f_sb = XO[0:NRBF, 0:5, :].rearrange("p a d -> p (a d)")
        records = XO[:, 10:20, :].bitcast(i32).rearrange("p a d -> p (a d)")[:, 0:2 * (KW + 1)]
        fz = XO[:, 10:15, :].rearrange("p a d -> p (a d)")
        fe = XO[:, 15:20, :].rearrange("p a d -> p (a d)")
        src_keys = XO[:, 10:15, :].bitcast(i32).rearrange("p a d -> p (a d)")[:, 0:KW + 1]

        WA = sb("WA", [P, 4, 4, D])
        wq_sb, wk_sb, wv_sb, wo_sb = (WA[:, k] for k in range(4))
        early = WA[:, 3].rearrange("p k d -> p (k d)")
        w_s_sb, w_v_sb, w1v_t_sb, w1vt_b_sb, w2v_sb, wva, wvb = (early[:, k * C:(k + 1) * C] for k in range(7))
        wf2_sb = early[:, 7 * C:11 * C].rearrange("p (k c) -> p k c", k=4)
        w1s_sb = early[:, 11 * C:13 * C].rearrange("p (k c) -> p k c", k=2)
        w2s_sb = sb("w2s_sb", [P, C])
        wf1_sb = sb("wf1_sb", [NRBF, C])
        bf1_sb = sb("bf1_sb", [P, 1])
        bf2_sb = sb("bf2_sb", [P, 4])
        bq_sb, bk_sb, bv_sb, bo_sb = (sb(n, [P, D]) for n in ("bq_sb", "bk_sb", "bv_sb", "bo_sb"))
        bo_rot = sb("bo_rot", [P, D])

        key_row = sb("key_row", [P, EP])
        key_col_i = sb("key_col_i", [P, NT], i32)
        edge_i = sb("edge_i", [P, NT, 2], i32)
        xidx = sb("xidx", [P, NT], i32)
        vw_f = sb("vw_f", [P, EP // 2])
        rank_s, rank_d = sb("rank_s", [P, NT], i32), sb("rank_d", [P, NT], i32)
        sk_row = sb("sk_row", [P, EP])
        sk_f = sk_row[:, 0:KW + 1]
        dk_f = key_row[:, 0:KW + 1]
        ko_i, kn_i = sb("ko_i", [P, NT, 2], i32), sb("kn_i", [P, NT, 2], i32)
        sk_c, dk_c = sb("sk_c", [P, NT]), sb("dk_c", [P, NT])
        kn_f = sb("kn_f", [P, NT])
        cont = sb("cont", [P, NT])
        srow_i, drow_i = sb("srow_i", [P, NT], i32), sb("drow_i", [P, NT], i32)
        sx_i, dx_i, ds_i = sb("sx_i", [P, NT], i32), sb("dx_i", [P, NT], i32), sb("ds_i", [P, NT], i32)
        slot_i = sb("slot_i", [P, NT], i32)

        mask = pair("mask", [P, P])
        dist, lane = mask
        ident, upto, before = sb("ident", [P, P]), sb("upto", [P, P]), sb("before", [P, P])
        ident_b = sb("ident_b", [P, P], bf16)
        eps = sb("eps", [P, 1])
        half = sb("half", [P, 1])
        zero_row = sb("zero_row", [1, D])
        none_i = sb("none_i", [1, 2], i32)
        norow_i = XO[:, 5, 0:80].bitcast(i32)

        rcut = sb("rcut", [P, NT])
        r_sb, r_sq, u, ur = (sb(n, [P, NT, 3]) for n in ("r_sb", "r_sq", "u", "ur"))
        rn2, rn = sb("rn2", [P, NT]), sb("rn", [P, NT])

        st, mv = pair("st", [P, 12]), pair("mv", [P, 4])
        std, rstd, nb = pair("std", [P, 2]), pair("rstd", [P, 2]), pair("nb", [P, 2])
        h = pair("h", [P, D])
        hd = pair("hd", [P, C])
        hT = pair("hT", [P, 5 * C])
        M = pair("M", [P, 6, C])
        Pt = pair("Pt", [P, D])
        Dr = pair("Dr", [P, 3 * C])
        xg = pair("xg", [P, D])
        base = pair("base", [P, CH + 2 * H])
        qk, hs_o = sb("qk", [P, 2, D]), sb("hs_o", [P, 4, D])
        sz, se, sp = ([Dr[b][:, k * C:(k + 1) * C] for b in range(2)] for k in range(3))

        hTd, hTs = ([r.bitcast(f16).rearrange("p (part e) -> p part e", part=2) for r in rs] for rs in (
            [M[b][:, 0:4, :].rearrange("p k c -> p (k c)") for b in range(2)],
            [hT[b][:, 0:D] for b in range(2)]))
        hs = [hs_o[:, b, :] for b in range(2)]
        late = WT[:, :, :].rearrange("p k e -> p (k e)")[:, 4 * EP - 4 * D:]
        xd, xb = ([late[:, (2 * k + b) * D:(2 * k + b + 1) * D] for b in range(2)] for k in range(2))
        qs, ks = [qk[:, 0, :]] * 2, [qk[:, 1, :]] * 2
        td0, td1, ts0, ts1 = (sb(n, [P, 1], i32) for n in ("td0", "td1", "ts0", "ts1"))
        a_sb = pair("a_sb", [P, H])
        aT, mT, eT = pair("aT", [H, P]), pair("mT", [H, P]), pair("eT", [H, P])
        same = sk_f[0:H, :]
        same_back = before[0:H, :]
        ex = pair("ex", [P, H])
        va = [base[b][:, D:2 * D + H] for b in range(2)]
        vw = [vw_f[:, b * (D + H):(b + 1) * (D + H)] for b in range(2)]
        rden = pair("rden", [P, H])
        o_sb = [hs_o[:, 2 + b, :] for b in range(2)]
        oT = [base[b][:, 0:D] for b in range(2)]
        y = Pt

        banks = [pb(f"bank{i}", [P, 512]) for i in range(8)]

        uses = {"xa": 1, "pa": 1, "ra": 1, "ea": 2, "xb": 1, "xc": 1, "sc": 1, "oc": 1}
        idx_all = sb("idx_all", [P, 2 * sum(uses.values())], i32)
        idx, at = {}, 0
        for n, k in uses.items():
            idx[n] = [idx_all[:, at + b * k:at + (b + 1) * k] for b in range(2)]
            at += 2 * k

        w_parts = WT[:, :, :].rearrange("p k e -> p (k e)")[:, 0:12 * D].bitcast(f16)\
            .rearrange("p (w part k d) -> p w part k d", w=3, part=2, k=4)
        norm2, norm = sb("norm2", [P, 3]), sb("norm", [P, 3])
        pow2, inv2 = sb("pow2", [P, 3], i32), sb("inv2", [P, 3], i32)
        w_scale, descale = sb("w_scale", [P, 3]), sb("descale", [P, 3])
        squares = hs_o[:, :, :].rearrange("p k d -> p (k d)")
        ones = hs_o[:, 0, 0:P]

        free = WA[:, 0:3].rearrange("p w k d -> p (w k d)")

        class Sort:
            def __init__(s, name, keys, rank, hi_hot, lo_hot, hi_rows, earlier, sums, bank, same_keys, looked_up):
                s.keys, s.rank, s.hi_hot, s.lo_hot = keys, rank, hi_hot, lo_hot
                s.hi_rows, s.earlier = hi_rows.bitcast(f16)[:, 0:EP], earlier.bitcast(f16)[:, 0:EP]
                s.hi, s.lo = sb(name + "_hi", [P, NT], i32), sb(name + "_lo", [P, NT], i32)
                s.total, s.run = sums[0:NHI, 0, :], sums[0:NHI, 1, :]
                s.first = sums[0:NHI, 2, 0:P // 2].bitcast(f16)
                s.sum, s.start = sb(name + "_sum", [NHI, 1]), sb(name + "_start", [NHI, 1])
                s.count = sb(name + "_count", [P, NT])
                s.sums_bank, s.rows_bank = banks[bank], banks[bank + 1]
                s.same_keys, s.looked_up = same_keys, looked_up
                (s.v_hot, s.p_turn, s.s_turn, s.p_hist, s.s_hist, s.v_first,
                 s.p_same, s.v_same, s.p_rank, s.v_prod, s.v_rank) = (
                    sem(name + "_" + n) for n in ("v_hot p_turn s_turn p_hist s_hist "
                                                  "v_first p_same v_same p_rank v_prod v_rank").split())

        spare = XO[:, 5:10, :].rearrange("p a d -> p (a d)")[:, 80:].bitcast(bf16)
        by_src = Sort("src", key_col_i[:, :], rank_s,
                      spare[:, EP:EP + NT * NHI].rearrange("p (t c) -> p t c", t=NT),
                      spare[:, 0:EP].rearrange("p (t c) -> p t c", t=NT),
                      free[0:NHI, 0:EP], key_row[0:NHI, :], M[0],
                      0, [hT[b][:, 0:Q * P // 2].bitcast(bf16) for b in range(2)], h)
        by_dst = Sort("dst", edge_i[:, :, 0], rank_d,
                      free[:, 2 * EP:2 * EP + NT * NHI // 2].bitcast(bf16).rearrange("p (t c) -> p t c", t=NT),
                      vw_f[:, :].bitcast(bf16).rearrange("p (t c) -> p t c", t=NT),
                      free[0:NHI, EP:2 * EP], sk_row[0:NHI, :], M[1],
                      2, [Dr[b][:, 0:Q * P // 2].bitcast(bf16) for b in range(2)], Pt)

        sorts = (by_src, by_dst)
        ident_h = free[0:NHI, 12 * D - P // 2:12 * D].bitcast(f16)[:, 0:NHI]

        g_idx = {n: sem("g_idx_" + n) for n in uses}
        d_cols = sem("d_cols")
        d_wf, d_wl0, d_wl1 = sem("d_wf"), sem("d_wl0"), sem("d_wl1")
        d_init, d_bias = sem("d_init"), sem("d_bias")
        g_const = sem("g_const")
        v_const = sem("v_const")
        v_keys = sem("v_keys")
        v_unit, s_unit = sem("v_unit"), sem("s_unit")
        p_wv = sem("p_wv")
        p_pre, v_hid, s_soft, p_filt, s_filt = (
            sem(n) for n in ("p_pre", "v_hid", "s_soft", "p_filt", "s_filt"))
        base_in, base_out, v_base, g_base = sems("base_in"), sems("base_out"), sem("v_base"), sem("g_base")
        a_x = sems("a_x")
        av_mom, as_std, av_nb, as_h, av_hd, ap_T, as_hT, ap_X, av_M, ap_O, as_D, as_S, av_P = (
            sem(n) for n in ("av_mom", "as_std", "av_nb", "as_h", "av_hd", "ap_T",
                             "as_hT", "ap_X", "av_M", "ap_O", "as_D", "as_S", "av_P"))
        av_hdp = sem("av_hdp")
        a_scat = sems("a_scat")
        g_skey = sem("g_skey")
        d_sk, bv_sk = sem("d_sk"), sem("bv_sk")
        b_x, b_P = sems("b_x"), sems("b_P")
        bv_mask, bv_carry, bp_cum, bp_st, bv_neg, bv_pos, bs_exp, bs_ln, bv_sp, bp_s2, bv_x1, bv_s1, bv_xo = (
            sem(n) for n in ("bv_mask", "bv_carry", "bp_cum", "bp_st", "bv_neg", "bv_pos", "bs_exp", "bs_ln",
                             "bv_sp", "bp_s2", "bv_x1", "bv_s1", "bv_xo"))
        v_sorted = sem("v_sorted")
        b_x1c = sems("b_x1c")
        a_drec, g_table = sems("a_drec"), sem("g_table")
        g_ones = sem("g_ones")
        p_norm, s_norm, v_scale, s_w = (sem(n) for n in ("p_norm", "s_norm", "v_scale", "s_w"))
        d_dk, cg_src = sem("d_dk"), sem("cg_src")
        c_x, c_td, c_ts, c_xd, c_xs, c_out = (sems(n) for n in ("c_x", "c_td", "c_ts", "c_xd", "c_xs", "c_out"))
        (cv_stats, cv_mom, cs_std, cv_nb, cs_hd, cs_hs, cp_Td, cs_hTd, cv_hTd, cp_Ts, cs_hTs, cv_hTs,
         cp_q, cp_k, cp_v, cv_q, cv_k, cv_a, cp_aT, cs_aT, cv_fwd, cv_e, cp_E, cs_ex, cv_mask,
         cv_v, cv_carry, cv_vw, cp_cum, cv_den, cv_o, cp_oT, cs_oT, cp_y, cv_y, cg_y) = (
            sem("c_" + n) for n in (
                "stats mom std nb hd hs Td hTd_hi hTd_lo Ts hTs_hi hTs_lo q k v qs ks a aTp aTs fwd e E ex mask "
                "vs carry vw cum den o oTp oTs yp yv yg").split())

        def add_bias(eng, c, b, added):
            width = chunk_width(c)
            if not isinstance(c, int):
                apart(eng, g_const, dma_count(c, b))
            wait(eng, base_in[b], dma_count(c, b))
            k, w = max(width // D, 1), min(width, D)
            v = base[b][:, 0:width].rearrange("p (k d) -> p k d", k=k)
            eng.tensor_tensor(v, v, bo_rot[:, 0:w].unsqueeze(1).broadcast_to([P, k, w]), ALU.add)\
               .then_inc(added, 1)

        def high_rows(eng, s):
            for r in range(-(-NT // 8)):
                eng.wait_ge(s.p_turn, r + 1)
                w = min(8, NT - 8 * r) * P
                out, turned = s.hi_rows[:, 8 * P * r:8 * P * r + w], s.rows_bank[:, :].bitcast(bf16)[0:NHI, 0:w]
                if s is by_src:
                    eng.activation(out, turned, ACT.Copy).then_inc(s.s_turn, 1)
                else:
                    eng.tensor_copy(out, turned).then_inc(s.s_turn, 1)

        block = ctx.enter_context(nc.Block())

        @block.sync
        def _(sp_):
            eng = sp_
            eng.dma_start(edge_i[:, :, :], edge_cols).then_inc(d_cols, 16)
            eng.dma_start(key_col_i[:, :], src_cols).then_inc(d_cols, 16)
            eng.dma_start(f_sb, f_t).then_inc(d_wf, 16)
            eng.dma_start(wf1_sb[:, :], wf1).then_inc(d_wf, 16)
            eng.dma_start(bf1_sb[:, :], bf1).then_inc(d_wf, 16)
            eng.dma_start(wf2_sb[:, :, :], wf2).then_inc(d_wf, 16)
            eng.dma_start(bf2_sb[:, :], bf2).then_inc(d_wf, 16)
            eng.dma_start(rcut[:, :], rcut_cols).then_inc(d_wl0, 16)
            eng.dma_start(r_sb[:, :, :], r_cols).then_inc(d_wl0, 16)
            for dst, src in ((w_s_sb, w_s), (w_v_sb, w_v), (w1v_t_sb, w1v_t[0]), (w1vt_b_sb, w1v_t[1]),
                             (w2s_sb, w2s), (w2v_sb, w2v)):
                eng.dma_start(dst[:, :], src).then_inc(d_wl0, 16)
            eng.dma_start(w1s_sb[:, :, :], w1s).then_inc(d_wl0, 16)
            eng.dma_start(bo_rot[:, :], bass.AP(bo2.tensor, 0, [[0, P // 8], [D // 8, 8], [1, D]]))\
               .then_inc(d_bias, 16)
            eng.wait_ge(g_const, 8)
            eng.dma_start(psort[0:1, :], zero_row[:, :]).then_inc(d_init, 16)
            eng.dma_start(skey[0:1, :], none_i[:, 0:1]).then_inc(d_init, 16)
            eng.dma_start(drec[0:1, :], none_i[:, :]).then_inc(d_init, 16)
            eng.dma_start(table.rearrange("(p f) one -> p (f one)", p=P), norow_i).then_inc(d_init, 16)
            for dst, src in ((bq_sb, bq), (bk_sb, bk), (bv_sb, bv), (bo_sb, bo2[:, 0:D])):
                eng.dma_start(dst[:, :], src.partition_broadcast(P)).then_inc(d_bias, 16)

            def sorted_columns(rows, w, s):
                with nc.allow_non_contiguous_dma(reason="columns of keys"):
                    for k, dst in enumerate((ko_i, kn_i)):
                        eng.dma_start(dst[:, :, 0:w], bass.AP(rows.tensor, w * k, [[w, P], [w * G, NT], [1, w]]))\
                           .then_inc(s, 16)

            def base_load(c, b):
                w = chunk_width(c)
                wait(eng, base_out[b], dma_count(c - 2, b))
                eng.dma_start(base[b][:, 0:w], x_flat[:, bass.ds(c * CH, w)]).then_inc(base_in[b], 16)

            def base_store(c, b, added, n):
                w = chunk_width(c)
                wait(eng, added, n)
                eng.dma_start(out_flat[:, bass.ds(c * CH, w)], base[b][:, 0:w]).then_inc(base_out[b], 16)

            base_load(0, 0)
            base_load(1, 1)
            base_store(0, 0, g_base, 1)
            with eng.Fori(0, (FIRST - 2) // 2) as k:
                for b in range(2):
                    base_load(2 * k + 2 + b, b)
                    base_store(2 * k + 1 + b, 1 - b, g_base, 2 * k + 2 + b)

            def step_a(tau, b):
                if real(tau):
                    base_load(FIRST + tau, b)
                if isinstance(tau, int) and tau == 0:
                    base_store(FIRST - 1, 1, g_base, FIRST)
                elif real(tau - 1):
                    base_store(FIRST + tau - 1, 1 - b, v_base, tau)
                if isinstance(tau, int) and tau in (2, 4, 6):
                    eng.wait_ge(by_src.v_rank, NT // Q + 1)
                    eng.wait_ge(by_dst.v_rank, NT // Q + 1)
                    dst, src = ((wq_sb, wq), (wk_sb, wk), (wv_sb, wv))[tau // 2 - 1]
                    eng.dma_start(dst, src).then_inc(d_wl1, 16)
                if isinstance(tau, int) and tau == PEEL_A + 5:
                    eng.wait_ge(g_skey, 16 * NT)
                    eng.wait_ge(v_hid, EP // D + 2)
                    eng.wait_ge(p_filt, 4 * EP // D)
                    sorted_columns(skey, 1, d_sk)
                    eng.dma_start(src_keys, bass.AP(skey.tensor, 0, [[0, P], [1, KW + 1]])).then_inc(d_sk, 16)
            over_tiles(eng, 2, step_a, PEEL_A + 6)
            for b in range(2):
                eng.wait_ge(a_scat[b], 8 * NT)

            def step_b(tau, b):
                if real(tau):
                    wait(eng, bp_st, tau - 1)
                    eng.dma_start(Pt[b][:, :], psort[bass.ds(G * tau, P), :]).then_inc(b_P[b], 16)
                if isinstance(tau, int) and tau == 1:
                    eng.wait_ge(v_sorted, 1)
                    for q in range(2):
                        eng.wait_ge(a_drec[q], 8 * NT)
                    sorted_columns(drec, 2, d_dk)
                    eng.dma_start(records,
                                  bass.AP(drec.tensor, 0, [[0, P], [1, 2 * (KW + 1)]])).then_inc(d_dk, 16)
                if isinstance(tau, int) and tau == NT:
                    eng.wait_ge(d_wl1, 48)
                    eng.dma_start(wo_sb, wo).then_inc(d_wl1, 16)
                if isinstance(tau, int) and 0 <= tau - 2 < REST:
                    base_load(FIRST + NT + tau - 2, b)
                if isinstance(tau, int) and 0 <= tau - 3 < REST:
                    base_store(FIRST + NT + tau - 3, 1 - b, v_base, NT + tau - 2)
                if real(tau - 4):
                    t = tau - 4
                    if not isinstance(tau, int):
                        apart(eng, g_const, t + 1)
                    wait(eng, bv_s1, t + 1)
                    eng.dma_start(x1c[bass.ds(P * t, P), :], XO[:, t, :]).then_inc(b_x1c[b], 16)
            over_tiles(eng, 4, step_b, REST + 4)

            for b in range(2):
                eng.wait_ge(base_out[b], 8 * NCH)
                eng.wait_ge(b_x1c[b], 8 * NT)
                eng.wait_ge(c_out[b], 8 * NT)

        @block.gpsimd
        def _(eng):
            eng.iota(dist[:, :], [[1, P]], base=0, channel_multiplier=-1,
                     allow_small_or_imprecise_dtypes=True).then_inc(g_const, 1)
            eng.memset(zero_row[:, :], 0.0).then_inc(g_const, 1)
            eng.memset(none_i[:, :], NONE).then_inc(g_const, 1)
            eng.memset(eps[:, :], EPS).then_inc(g_const, 1)
            eng.memset(half[:, :], 0.5).then_inc(g_const, 1)
            eng.memset(norow_i, NOROW).then_inc(g_const, 1)
            eng.iota(slot_i[:, :], [[P, NT]], base=0, channel_multiplier=1).then_inc(g_const, 1)
            eng.iota(lane[:, :], [[1, P]], base=0, channel_multiplier=0,
                     allow_small_or_imprecise_dtypes=True).then_inc(g_const, 1)

            def wait_apart(eng, s, n):
                if not isinstance(n, int):
                    apart(eng, g_const, n)
                wait(eng, s, n)

            def gather(dst, src, idx, rows, s):
                eng.indirect_dma_start(out=dst, out_offset=None, in_=src,
                                       in_offset=bass.IndirectOffsetOnAxis(ap=idx, axis=0),
                                       bounds_check=rows - 1, oob_is_err=False).then_inc(s, 16)

            def scatter(dst, idx, src, rows, s):
                eng.indirect_dma_start(out=dst, out_offset=bass.IndirectOffsetOnAxis(ap=idx, axis=0),
                                       in_=src, in_offset=None,
                                       bounds_check=rows - 1, oob_is_err=False).then_inc(s, 16)

            def pick(name, t, b, column, users):
                s = g_idx[name]
                for u_ in users:
                    wait_apart(eng, u_[b], dma_count(t - 2, b))
                eng.tensor_copy(idx[name][b][:, :], column[:, t] if len(column.shape) == 3
                                else column[:, bass.ds(t, 1)]).then_inc(s, 1)
                wait_apart(eng, s, t + 1)
                return idx[name][b][:, :]

            eng.wait_ge(v_keys, 1)
            for tau in range(2):
                gather(xg[tau][:, :], x, pick("xa", tau, tau, xidx, []), N, a_x[tau])
            eng.wait_ge(d_init, 64)
            eng.wait_ge(d_bias, 80)
            with eng.Fori(0, FIRST // 2) as k:
                for b in range(2):
                    add_bias(eng, 2 * k + b, b, g_base)
            for s in sorts:
                eng.wait_ge(s.v_rank, NT // Q + 1)

            def spread(tau, steps):
                if not isinstance(tau, int) or not 0 <= tau < steps:
                    return ()
                return range(NT * tau // steps, NT * (tau + 1) // steps)

            def step_a(tau, b):
                if real(tau) and not (isinstance(tau, int) and tau < 2):
                    wait_apart(eng, as_h, tau - 1)
                    gather(xg[b][:, :], x, pick("xa", tau, b, xidx, [a_x]), N, a_x[b])
                if real(tau - 5):
                    t = tau - 5
                    wait_apart(eng, av_P, t + 1)
                    wait_apart(eng, as_S, t + 1)
                    scatter(psort, pick("pa", t, 1 - b, rank_s, [a_scat]), Pt[1 - b][:, :], ROWS, a_scat[1 - b])
                if real(tau - 2):
                    scatter(drec, pick("ra", tau - 2, b, rank_d, [a_drec]),
                            pick("ea", tau - 2, b, edge_i, [a_drec]), ROWS, a_drec[b])
                for t in spread(tau - 2, PEEL_A + 2):
                    scatter(skey, rank_s[:, t:t + 1], key_col_i[:, t:t + 1], ROWS, g_skey)
            over_tiles(eng, 5, step_a, PEEL_A + 4)

            eng.wait_ge(d_bias, 80)
            eng.wait_ge(v_sorted, 1)

            def step_b(tau, b):
                if real(tau):
                    wait_apart(eng, bv_x1, tau - 1)
                    gather(xg[b][:, :], x, pick("xb", tau, b, sx_i, [b_x]), N, b_x[b])
                for t in spread(tau, REST + 2):
                    scatter(table, srow_i[:, t:t + 1], slot_i[:, t:t + 1], N, g_table)
            over_tiles(eng, 2, step_b, REST + 2)

            eng.wait_ge(v_sorted, 2)
            eng.wait_ge(g_table, 16 * NT)
            td, ts = (td0, td1), (ts0, ts1)

            def lookups(t, b):
                dst_rows = pick("xc", t, b, dx_i, [c_x, c_td])
                gather(xd[b][:, :], x, dst_rows, N, c_x[b])
                gather(td[b][:, :], table, dst_rows, N, c_td[b])
                gather(ts[b][:, :], table, pick("sc", t, b, ds_i, [c_ts]), N, c_ts[b])

            def updated(t, b):
                wait_apart(eng, c_x[b], dma_count(t, b))
                wait_apart(eng, c_td[b], dma_count(t, b))
                gather(xd[b][:, :], x1c, td[b][:, :], EP, c_xd[b])
                wait_apart(eng, c_ts[b], dma_count(t, b))
                gather(xg[b][:, :], x1c, ts[b][:, :], EP, c_xs[b])

            def step_c(tau, b):
                if real(tau - 1):
                    if isinstance(tau, int) and tau == 1:
                        for q in range(2):
                            eng.wait_ge(b_x1c[q], 8 * NT)
                    updated(tau - 1, 1 - b)
                if real(tau - 2):
                    t = tau - 2
                    wait_apart(eng, cv_y, t - 1)
                    wait_apart(eng, c_xd[b], dma_count(t, b))
                    eng.tensor_tensor(xb[b][:, :], xd[b][:, :], bo_sb[:, :], ALU.add).then_inc(cg_y, 1)
                if real(tau):
                    wait_apart(eng, cs_hs, tau - 1)
                    wait_apart(eng, cg_y, tau - 1)
                    lookups(tau, b)
                if isinstance(tau, int) and tau == 0:
                    for q in range(2):
                        eng.wait_ge(base_out[q], 8 * NCH)
                        eng.memset(va[q][:, D:D + H], 1.0).then_inc(g_ones, 1)
                if real(tau - 4):
                    t = tau - 4
                    wait_apart(eng, cv_y, t + 1)
                    scatter(out, pick("oc", t, b, drow_i, [c_out]), y[b][:, :], N, c_out[b])
                if isinstance(tau, int) and 1 <= tau < PEEL:
                    eng.wait_ge(bv_xo, min(tau, 2))
                    for t in range(*sent_with(tau)):
                        scatter(out, srow_i[:, t:t + 1], XO[:, t, :], N, cg_src)
                    if tau == PEEL - 1:
                        eng.wait_ge(cg_src, 16 * NT)
            over_tiles(eng, 4, step_c)
            for b in range(2):
                eng.wait_ge(c_out[b], 8 * NT)

        @block.scalar
        def _(eng):
            eng.wait_ge(g_const, 8)

            def earlier(s, g):
                eng.wait_ge(s.p_hist, g + 1)
                w = Q if g < NT // Q - 1 else Q - 1
                last = eng.activation(s.earlier[:, (Q * g + 1) * P:(Q * g + 1 + w) * P],
                                      s.sums_bank[0:NHI, 0:w * P], ACT.Copy)
                if w < Q:
                    last = eng.activation(s.total, s.sums_bank[0:NHI, w * P:Q * P], ACT.Copy)
                last.then_inc(s.s_hist, 1)

            high_rows(eng, by_src)
            eng.wait_ge(v_hid, EP // D + 1)
            eng.activation(fe[:, :], fe[:, :], ACT.Exp).then_inc(s_soft, 1)
            eng.wait_ge(s_soft, 1)
            eng.activation(fe[:, :], fe[:, :], ACT.Ln, bias=half[:, :], scale=0.5).then_inc(s_soft, 1)
            for g in range(NT // Q):
                for s in sorts:
                    earlier(s, g)
            for c in range(EP // D):
                for k in range(4):
                    eng.wait_ge(p_filt, 4 * c + k + 1)
                    eng.activation(WT[:, k, c * D:(c + 1) * D], banks[4 + k][:, :], ACT.Identity,
                                   bias=bf2_sb[:, k:k + 1]).then_inc(s_filt, 1)
            eng.wait_ge(v_unit, 1)
            eng.activation(rn[:, :], rn2[:, :], ACT.Sqrt).then_inc(s_unit, 1)

            def step_a(tau, b):
                if isinstance(tau, int) and 0 <= tau - NT < 3:
                    i, w = tau - NT, (wq_sb, wk_sb, wv_sb)[tau - NT]
                    eng.wait_ge(d_wl1, 48)
                    wait(eng, s_norm, i)
                    eng.activation(squares, w.rearrange("p k d -> p (k d)"), ACT.Square,
                                   accum_out=norm2[:, i:i + 1]).then_inc(s_norm, 1)
                if real(tau):
                    wait(eng, av_mom, 2 * (tau + 1))
                    eng.activation(std[b][:, 0:1], mv[b][:, 1:2], ACT.Sqrt, bias=eps[:, :]).then_inc(as_std, 1)
                    wait(eng, av_nb, 2 * (tau + 1))
                    wait(eng, ap_T, tau - 1)
                    eng.activation(h[b][:, :], xg[b][:, :], ACT.Relu, bias=nb[b][:, 0:1],
                                   scale=rstd[b][:, 0:1]).then_inc(as_h, 1)
                if real(tau - 1):
                    t, q = tau - 1, 1 - b
                    wait(eng, ap_T, t + 1)
                    wait(eng, ap_X, t - 1)
                    eng.activation(hT[q][:, 0:C], banks[1][:, 0:C], ACT.Copy)
                    eng.activation(hT[q][:, C:5 * C], banks[0][:, :], ACT.Copy).then_inc(as_hT, 1)
                if real(tau - 3):
                    t, q = tau - 3, 1 - b
                    apart(eng, g_const, t + 1, t - 1)
                    wait(eng, ap_O, t + 1)
                    wait(eng, av_P, t - 1)
                    eng.activation(Dr[q][:, :], banks[4][:, 0:3 * C], ACT.Copy,
                                   scale=rcut[:, bass.ds(t, 1)]).then_inc(as_D, 1)
                    apart(eng, g_const, dma_count(t - 2, q))
                    wait(eng, a_scat[q], dma_count(t - 2, q))
                    eng.activation(Pt[q][:, 0:C], banks[4][:, 3 * C:4 * C], ACT.Copy,
                                   scale=rcut[:, bass.ds(t, 1)]).then_inc(as_S, 1)
            over_tiles(eng, 3, step_a, PEEL_A)

            eng.wait_ge(p_norm, 1)
            eng.activation(norm[:, :], banks[7][:, 0:3], ACT.Sqrt).then_inc(s_norm, 1)
            eng.wait_ge(av_M, NT)
            eng.wait_ge(v_scale, 5)
            for i, w in enumerate((wq_sb, wk_sb, wv_sb)):
                eng.activation(w_parts[:, i, 0], w, ACT.Copy, scale=w_scale[:, i:i + 1]).then_inc(s_w, 1)

            def step_b(tau, b):
                if real(tau - 1):
                    t, q = tau - 1, 1 - b
                    wait(eng, bv_neg, t + 1)
                    eng.activation(se[q][:, :], se[q][:, :], ACT.Exp).then_inc(bs_exp, 1)
                    wait(eng, bs_exp, t + 1)
                    eng.activation(se[q][:, :], se[q][:, :], ACT.Ln, bias=half[:, :], scale=0.5)\
                       .then_inc(bs_ln, 1)
            over_tiles(eng, 2, step_b)
            def step_c(tau, b):
                if real(tau - 2):
                    wait(eng, cp_E, tau - 1)
                    eng.activation(ex[b][:, :], banks[5][:, P:P + H], ACT.Exp).then_inc(cs_ex, 1)
                if real(tau):
                    wait(eng, cv_mom, 2 * (tau + 1))
                    eng.activation(std[b][:, :], mv[b][:, 1:4:2], ACT.Sqrt, bias=eps[:, :]).then_inc(cs_std, 1)
                    wait(eng, cv_nb, 2 * (tau + 1))
                    wait(eng, cp_Td, tau - 1)
                    eng.activation(h[b][:, :], xd[b][:, :], ACT.Relu, bias=nb[b][:, 0:1],
                                   scale=rstd[b][:, 0:1]).then_inc(cs_hd, 1)
                    wait(eng, cp_Ts, tau - 1)
                    eng.activation(hs[b], xg[b][:, :], ACT.Relu, bias=nb[b][:, 1:2],
                                   scale=rstd[b][:, 1:2]).then_inc(cs_hs, 1)
                if real(tau):
                    wait(eng, cp_Td, tau + 1)
                    wait(eng, cp_q, tau - 1)
                    eng.activation(hTd[b][:, 0], banks[0][:, :], ACT.Copy, scale=H_SCALE).then_inc(cs_hTd, 1)
                if real(tau - 2):
                    wait(eng, cp_oT, tau - 1)
                    wait(eng, cp_y, tau - 3)
                    eng.activation(oT[b][:, :], banks[6][:, :], ACT.Copy).then_inc(cs_oT, 1)
                if real(tau):
                    wait(eng, cp_Ts, tau + 1)
                    wait(eng, cp_v, tau - 1)
                    eng.activation(hTs[b][:, 0], banks[0][:, :], ACT.Copy, scale=H_SCALE).then_inc(cs_hTs, 1)
                if real(tau - 1):
                    t, q = tau - 1, 1 - b
                    wait(eng, cp_aT, t + 1)
                    wait(eng, cv_e, t - 1)
                    first = 0 if isinstance(t, int) and t == 0 else 1
                    eng.activation(aT[q][:, first:P], banks[5][0:H, first:P], ACT.Copy, scale=SCALE)\
                       .then_inc(cs_aT, 1)
            over_tiles(eng, 2, step_c)

        @block.tensor
        def _(eng):
            eng.wait_ge(d_wf, 80)
            for c in range(EP // D):
                if c >= 4:
                    eng.wait_ge(v_hid, c - 3)
                eng.matmul(banks[4 + c % 4][:, :], wf1_sb[:, :], f_sb[:, c * D:(c + 1) * D],
                           start=True, stop=True).then_inc(p_pre, 1)

            def turn(s):
                eng.wait_ge(s.v_hot, 2)
                for r in range(-(-NT // 8)):
                    wait(eng, s.s_turn, r)
                    for t in range(8 * r, min(8 * r + 8, NT)):
                        last = eng.transpose(s.rows_bank[:, :].bitcast(bf16)[0:NHI, (t % 8) * P:(t % 8 + 1) * P],
                                             s.hi_hot[:, t, :], ident_b[:, :])
                    last.then_inc(s.p_turn, 1)

            def histogram(s, g):
                eng.wait_ge(s.v_hot, 3)
                wait(eng, s.s_hist, g)
                for j in range(Q):
                    o = s.sums_bank[0:NHI, j * P:(j + 1) * P]
                    for t in range(Q * g, Q * g + j + 1):
                        last = eng.matmul(o, s.hi_hot[:, t, :], s.lo_hot[:, t, :],
                                          start=(t == Q * g), stop=False)
                    last = eng.matmul(o, ident_h, s.earlier[:, Q * g * P:(Q * g + 1) * P], start=False, stop=True)
                last.then_inc(s.p_hist, 1)

            def starts(s):
                eng.wait_ge(s.v_first, 2)
                eng.wait_ge(v_const, 7)
                eng.matmul(s.sums_bank[0:NHI, P:P + 1], upto[0:NHI, 0:NHI], s.sum[:, :], start=True, stop=True)\
                   .then_inc(s.p_hist, 1)

            def same_high(s, r):
                wait(eng, s.v_same, r)
                eng.wait_ge(s.s_turn, -(-NT // 8))
                for t in range(Q * r, Q * r + Q):
                    rows = s.hi_rows[:, t * P:(t + 1) * P]
                    last = eng.matmul(s.rows_bank[:, (t % Q) * P:(t % Q + 1) * P], rows, rows, start=True, stop=True)
                last.then_inc(s.p_same, 1)

            def ranks(s, r):
                eng.wait_ge(s.v_first, 5)
                eng.wait_ge(s.s_hist, NT // Q)
                wait(eng, s.v_prod, r)
                eng.wait_ge(s.v_same, r + 1)
                for t in range(Q * r, Q * r + Q):
                    o = s.sums_bank[:, (t % Q) * P:(t % Q + 1) * P]
                    rows = s.hi_rows[:, t * P:(t + 1) * P]
                    eng.matmul(o, rows, s.first, start=True, stop=False)
                    eng.matmul(o, rows, s.earlier[:, t * P:(t + 1) * P], start=False, stop=False)
                    last = eng.matmul(o, s.same_keys[r % 2][:, (t % Q) * P:(t % Q + 1) * P], s.lo_hot[:, t, :],
                                      start=False, stop=True)
                last.then_inc(s.p_rank, 1)

            eng.wait_ge(v_const, 5)
            for s in sorts:
                turn(s)
            for g in range(NT // Q):
                for s in sorts:
                    histogram(s, g)
            for s in sorts:
                starts(s)
                same_high(s, 0)
            for c in range(EP // D):
                eng.wait_ge(v_hid, EP // D + 2)
                for k in range(4):
                    if c > 0:
                        eng.wait_ge(s_filt, 4 * (c - 1) + k + 1)
                    eng.matmul(banks[4 + k][:, :], wf2_sb[:, k, :], fz[:, c * D:(c + 1) * D],
                               start=True, stop=True).then_inc(p_filt, 1)
                for s in sorts:
                    if c + 1 < NT // Q:
                        same_high(s, c + 1)
                    ranks(s, c)
            eng.wait_ge(d_wl0, 144)
            eng.wait_ge(by_src.v_prod, NT // Q)
            eng.matmul(banks[0][:, 0:C], w1v_t_sb[:, :], w2v_sb[:, :], start=True, stop=True)
            eng.matmul(banks[0][:, C:2 * C], w1vt_b_sb[:, :], w2v_sb[:, :], start=True, stop=True).then_inc(p_wv, 1)
            eng.wait_ge(s_filt, 4 * EP // D)
            eng.wait_ge(v_unit, 5)
            eng.wait_ge(by_dst.v_rank, NT // Q + 1)

            def step_a(tau, b):
                if real(tau - 2):
                    t = tau - 2
                    wait(eng, as_hT, t + 1)
                    wait(eng, av_M, t)
                    eng.matmul(banks[3][:, 0:C], w_s_sb[:, :], hT[b][:, 0:C], start=True, stop=True)
                    eng.matmul(banks[2][:, :], w_v_sb[:, :], hT[b][:, C:5 * C], start=True, stop=True)\
                       .then_inc(ap_X, 1)
                if real(tau - 1):
                    t, q = tau - 1, 1 - b
                    wait(eng, as_h, t + 1)
                    wait(eng, as_hT, t)
                    eng.transpose(banks[1][:, 0:C], h[q][:, 0:C], ident[:, :])
                    hv = h[q][:, C:4 * C].rearrange("p (c i) -> p i c", i=3)
                    for i in range(3):
                        eng.transpose(banks[0][:, i * C:(i + 1) * C], hv[:, i, :], ident[:, :])
                    wait(eng, av_hd, t + 1)
                    eng.transpose(banks[0][:, 3 * C:4 * C], hd[q][:, :], ident[:, :]).then_inc(ap_T, 1)
                if real(tau - 3):
                    t, q = tau - 3, 1 - b
                    wait(eng, av_M, t + 1)
                    wait(eng, as_S, t)
                    wait(eng, av_P, t)
                    for i in range(3):
                        eng.matmul(banks[4][:, i * C:(i + 1) * C], M[q][:, 3 + i, :], wvb[:, :],
                                   start=True, stop=True)
                    eng.matmul(banks[4][:, 3 * C:4 * C], M[q][:, 0, :], w1s_sb[:, 0, :], start=True, stop=False)
                    eng.matmul(banks[4][:, 3 * C:4 * C], M[q][:, 1, :], w1s_sb[:, 1, :], start=False, stop=True)
                    eng.matmul(banks[5][:, 0:C], M[q][:, 2, :], wva[:, :], start=True, stop=True)\
                       .then_inc(ap_O, 1)
            over_tiles(eng, 3, step_a, PEEL_A)

            eng.wait_ge(s_norm, 3)
            eng.wait_ge(v_scale, 1)
            eng.matmul(banks[7][:, 0:3], ones, norm2[:, :], start=True, stop=True).then_inc(p_norm, 1)

            def step_b(tau, b):
                if real(tau - 1):
                    t, q = tau - 1, 1 - b
                    wait(eng, bv_mask, t + 1)
                    wait(eng, b_P[q], dma_count(t, q))
                    wait(eng, bv_carry, t + 1)
                    wait(eng, bv_x1, t - 1)
                    eng.matmul(banks[q][:, :], mask[q][:, :], Pt[q][:, :], start=True, stop=True).then_inc(bp_cum, 1)
                    wait(eng, bv_neg, t)
                    eng.matmul(banks[2][:, 0:P], Pt[q][:, 0:C], mask[q][:, :], start=True, stop=True)\
                       .then_inc(bp_st, 1)
                if real(tau - 3):
                    t, q = tau - 3, 1 - b
                    wait(eng, bv_sp, t + 1)
                    wait(eng, bv_s1, t)
                    eng.matmul(banks[3][:, 0:C], sp[q][:, :], w2s_sb[:, :], start=True, stop=True).then_inc(bp_s2, 1)
            over_tiles(eng, 3, step_b, PEEL_A)
            eng.wait_ge(d_wl1, 64)
            eng.wait_ge(s_w, 3)
            eng.wait_ge(v_scale, 8)

            def project(bank, h_parts, w, s):
                parts = ((0, 0), (0, 1), (1, 0))
                for k in range(4):
                    for i, (a, c) in enumerate(parts):
                        last = eng.matmul(bank[:, :], h_parts[:, a, k * C:(k + 1) * C], w_parts[:, w, c, k, :],
                                          start=(k == 0 and i == 0), stop=(k == 3 and i == 2))
                last.then_inc(s, 1)

            def step_c(tau, b):
                if real(tau - 1):
                    t, q = tau - 1, 1 - b
                    wait(eng, cs_hTd, t + 1)
                    wait(eng, cv_hTd, t + 1)
                    wait(eng, cv_q, t)
                    project(banks[1], hTd[q], 0, cp_q)
                if real(tau - 2):
                    apart(eng, g_const, tau - 1)
                    wait(eng, cv_e, tau - 1)
                    wait(eng, cs_aT, tau - 1)
                    eng.transpose(banks[5][:, P:P + H], eT[b][:, :], ident[0:H, 0:H]).then_inc(cp_E, 1)
                if real(tau - 1):
                    wait(eng, cv_hTs, t + 1)
                    wait(eng, cv_k, 2 * t)
                    project(banks[2], hTs[q], 1, cp_k)
                if real(tau - 2):
                    t2 = tau - 2
                    wait(eng, cv_vw, t2 + 1)
                    wait(eng, cv_carry, t2 + 1)
                    wait(eng, cv_y, t2)
                    wait(eng, cv_o, t2)
                    eng.matmul(banks[4][:, :], mask[b][:, :], vw[b][:, 0:D], start=True, stop=True)
                    eng.matmul(banks[7][:, 0:H], mask[b][:, :], vw[b][:, D:D + H], start=True, stop=True)\
                       .then_inc(cp_cum, 1)
                if real(tau):
                    wait(eng, cs_hd, tau + 1)
                    wait(eng, cv_hTs, tau)
                    for k in range(4):
                        last = eng.transpose(banks[0][:, k * C:(k + 1) * C], h[b][:, k * C:(k + 1) * C], ident[:, :])
                    last.then_inc(cp_Td, 1)
                if real(tau - 1):
                    wait(eng, cv_v, t)
                    project(banks[3], hTs[q], 2, cp_v)
                if real(tau - 2):
                    wait(eng, cv_o, t2 + 1)
                    wait(eng, cs_oT, t2)
                    for k in range(4):
                        last = eng.transpose(banks[6][:, k * C:(k + 1) * C], o_sb[b][:, k * C:(k + 1) * C], ident[:, :])
                    last.then_inc(cp_oT, 1)
                if real(tau):
                    wait(eng, cs_hs, tau + 1)
                    wait(eng, cv_hTd, tau + 1)
                    for k in range(4):
                        last = eng.transpose(banks[0][:, k * C:(k + 1) * C], hs[b][:, k * C:(k + 1) * C], ident[:, :])
                    last.then_inc(cp_Ts, 1)
                if real(tau - 1):
                    wait(eng, cv_a, t + 1)
                    wait(eng, cs_ex, t)
                    eng.transpose(banks[5][0:H, 0:P], a_sb[q][:, :], ident[:, :]).then_inc(cp_aT, 1)
                if real(tau - 2):
                    wait(eng, cs_oT, t2 + 1)
                    if not isinstance(t2, int) or t2 < NT - 1:
                        wait(eng, cv_carry, t2 + 2)
                    for k in range(4):
                        last = eng.matmul(banks[7][:, :], oT[b][:, k * C:(k + 1) * C], wo_sb[:, k, :],
                                          start=(k == 0), stop=(k == 3))
                    last.then_inc(cp_y, 1)
            over_tiles(eng, 2, step_c)

        @block.vector
        def _(eng):
            def link(ins, s, n):
                ins.then_inc(s, 1)
                wait(eng, s, n)

            eng.wait_ge(g_const, 8)
            eng.tensor_scalar(ident_b[:, :], dist[:, :], 0.0, None, ALU.is_equal).then_inc(v_const, 1)
            eng.tensor_scalar(ident[:, :], dist[:, :], 0.0, None, ALU.is_equal).then_inc(v_const, 1)
            eng.tensor_scalar(ident_h, dist[0:NHI, 0:NHI], 0.0, None, ALU.is_equal).then_inc(v_const, 1)
            eng.wait_ge(d_cols, 32)

            for s in sorts:
                eng.tensor_scalar(s.hi[:, :], s.keys, 7, None, ALU.logical_shift_right)
                eng.tensor_scalar(s.lo[:, :], s.keys, P - 1, None, ALU.bitwise_and).then_inc(s.v_hot, 1)
            for s in sorts:
                eng.memset(s.earlier[:, 0:P], -float(MID)).then_inc(v_const, 1)
                eng.wait_ge(s.v_hot, 1)
                for digit, hot, w in ((s.hi, s.hi_hot, NHI), (s.lo, s.lo_hot, P)):
                    eng.tensor_tensor(hot, lane[:, 0:w].unsqueeze(1).broadcast_to([P, NT, w]),
                                      digit[:, :].unsqueeze(2).broadcast_to([P, NT, w]), ALU.is_equal)\
                       .then_inc(s.v_hot, 1)

            def first_rows(s):
                eng.wait_ge(s.s_hist, NT // Q)
                eng.tensor_scalar(s.total, s.total, float(MID), None, ALU.add).then_inc(s.v_first, 1)
                eng.wait_ge(s.v_first, 1)
                eng.tensor_reduce(s.sum[:, :], s.total, AX.X, ALU.add).then_inc(s.v_first, 1)
                eng.wait_ge(s.p_hist, NT // Q + 1)
                eng.scalar_tensor_tensor(s.start[:, :], s.sums_bank[0:NHI, P:P + 1], 1.0, s.sum[:, :],
                                         ALU.add, ALU.subtract).then_inc(s.v_first, 1)
                eng.wait_ge(s.v_first, 3)
                eng.tensor_tensor_scan(s.run, s.total, s.total, s.start[:, :],
                                       ALU.add, ALU.max).then_inc(s.v_first, 1)
                eng.wait_ge(s.v_first, 4)
                eng.scalar_tensor_tensor(s.first, s.run, float(MID), s.total, ALU.subtract, ALU.subtract)\
                   .then_inc(s.v_first, 1)

            def same_before(s, r):
                eng.wait_ge(s.p_same, r + 1)
                wait(eng, s.p_rank, r - 1)
                eng.tensor_tensor(s.same_keys[r % 2].rearrange("p (t e) -> p t e", t=Q),
                                  s.rows_bank[:, :].rearrange("p (t e) -> p t e", t=Q),
                                  before[:, :].unsqueeze(1).broadcast_to([P, Q, P]), ALU.mult).then_inc(s.v_same, 1)

            def take_ranks(s, r):
                eng.wait_ge(s.p_rank, r + 1)
                p = s.looked_up[r % 2][:, :].rearrange("p (t e) -> p t e", t=Q)
                wait(eng, s.v_rank, r - 1)
                eng.tensor_tensor(p, s.sums_bank[:, :].rearrange("p (t e) -> p t e", t=Q),
                                  s.lo_hot[:, Q * r:Q * r + Q, :], ALU.mult).then_inc(s.v_prod, 1)
                eng.wait_ge(s.v_prod, r + 1)
                eng.tensor_reduce(s.count[:, Q * r:Q * r + Q], p, AX.X, ALU.add).then_inc(s.v_rank, 1)

            eng.tensor_scalar(xidx[:, :], edge_i[:, :, 0], float(N - 1), None, ALU.min).then_inc(v_keys, 1)
            for c in range(EP // D):
                eng.wait_ge(p_pre, c + 1)
                eng.tensor_scalar(fz[:, c * D:(c + 1) * D], banks[4 + c % 4][:, :], bf1_sb[:, :], None, ALU.add)\
                   .then_inc(v_hid, 1)
            eng.wait_ge(v_hid, EP // D)
            eng.scalar_tensor_tensor(fe[:, :], fz[:, :], -1.0, fz[:, :], ALU.mult, ALU.min)\
               .then_inc(v_hid, 1)
            eng.tensor_scalar(upto[:, :], dist[:, :], 0.0, None, ALU.is_ge).then_inc(v_const, 1)
            eng.tensor_scalar(before[:, :], dist[:, :], 0.0, None, ALU.is_gt).then_inc(v_const, 1)
            high_rows(eng, by_dst)
            eng.wait_ge(d_wl0, 144)
            v3 = [rcut[:, :].unsqueeze(2).broadcast_to([P, NT, 3]), rn2[:, :].unsqueeze(2).broadcast_to([P, NT, 3])]
            link(eng.tensor_tensor(r_sq[:, :, :], r_sb[:, :, :], r_sb[:, :, :], ALU.mult), v_keys, 2)
            eng.tensor_reduce(rn2[:, :], r_sq[:, :, :], AX.X, ALU.add).then_inc(v_unit, 1)
            eng.wait_ge(s_soft, 2)
            eng.scalar_tensor_tensor(fz[:, :], fz[:, :], 0.0, fe[:, :], ALU.max, ALU.add).then_inc(v_hid, 1)
            eng.wait_ge(v_const, 7)
            for s in sorts:
                first_rows(s)
                same_before(s, 0)
            for c in range(EP // D):
                for s in sorts:
                    if c + 1 < NT // Q:
                        same_before(s, c + 1)
                    take_ranks(s, c)
            for s in sorts:
                eng.wait_ge(s.v_rank, NT // Q)
                eng.tensor_scalar(s.rank[:, :], s.count[:, :], float(2 * MID), None, ALU.add).then_inc(s.v_rank, 1)
            eng.wait_ge(s_unit, 1)
            link(eng.reciprocal(rn2[:, :], rn[:, :]), v_unit, 2)
            link(eng.tensor_tensor(u[:, :, :], r_sb[:, :, :], v3[1], ALU.mult), v_unit, 3)
            eng.tensor_tensor(ur[:, :, :], u[:, :, :], v3[0], ALU.mult).then_inc(v_unit, 1)
            eng.wait_ge(v_unit, 4)
            eng.wait_ge(p_wv, 1)
            eng.tensor_copy(wva[:, :], banks[0][:, 0:C])
            eng.tensor_copy(wvb[:, :], banks[0][:, C:2 * C]).then_inc(v_unit, 1)
            eng.wait_ge(s_filt, 4 * EP // D)
            eng.wait_ge(v_unit, 5)
            eng.wait_ge(d_bias, 80)

            def step_a(tau, b):
                if real(tau):
                    wait(eng, a_x[b], dma_count(tau, b))
                    eng.bn_stats(st[b][:, 0:6], xg[b][:, :]).then_inc(av_mom, 1)
                    apart(eng, g_const, 2 * tau + 1)
                    wait(eng, av_mom, 2 * tau + 1)
                    eng.bn_aggr(mv[b][:, 0:2], st[b][:, 0:6]).then_inc(av_mom, 1)
                if real(tau - 1):
                    t, q = tau - 1, 1 - b
                    wait(eng, as_h, t + 1)
                    wait(eng, ap_T, t - 1)
                    hv = h[q][:, C:4 * C].rearrange("p (c i) -> p i c", i=3)
                    eng.tensor_scalar(hd[q][:, :], hv[:, 0, :], u[:, t, 0:1], None, ALU.mult).then_inc(av_hdp, 1)
                    wait(eng, av_hdp, 2 * t + 1)
                    eng.scalar_tensor_tensor(hd[q][:, :], hv[:, 1, :], u[:, t, 1:2], hd[q][:, :],
                                             ALU.mult, ALU.add).then_inc(av_hdp, 1)
                    wait(eng, av_hdp, 2 * t + 2)
                    eng.scalar_tensor_tensor(hd[q][:, :], hv[:, 2, :], u[:, t, 2:3], hd[q][:, :],
                                             ALU.mult, ALU.add).then_inc(av_hd, 1)
                if real(tau - 4):
                    t = tau - 4
                    wait(eng, as_D, t + 1)
                    wait(eng, a_scat[b], dma_count(t - 2, b))
                    pv = Pt[b][:, C:4 * C].rearrange("p (c i) -> p i c", i=3)
                    for i in range(3):
                        last = eng.scalar_tensor_tensor(pv[:, i, :], banks[5][:, 0:C], ur[:, t, i:i + 1],
                                                        Dr[b][:, i * C:(i + 1) * C], ALU.mult, ALU.add)
                    last.then_inc(av_P, 1)
                if real(tau):
                    wait(eng, as_std, tau + 1)
                    eng.reciprocal(rstd[b][:, 0:1], std[b][:, 0:1]).then_inc(av_nb, 1)
                    wait(eng, av_nb, 2 * tau + 1)
                    eng.scalar_tensor_tensor(nb[b][:, 0:1], mv[b][:, 0:1], -1.0, rstd[b][:, 0:1],
                                             ALU.mult, ALU.mult).then_inc(av_nb, 1)
                if real(tau - 2):
                    t = tau - 2
                    wait(eng, ap_X, t + 1)
                    wait(eng, ap_O, t - 1)
                    w = [WT[:, k, bass.ds(P * t, P)] for k in range(4)]
                    stt = eng.scalar_tensor_tensor
                    stt(M[b][:, 0, :], banks[3][:, 0:C], SC_A, w[0], ALU.mult, ALU.mult)
                    stt(M[b][:, 2, :], banks[3][:, 0:C], SC_C, w[2], ALU.mult, ALU.mult)
                    stt(M[b][:, 1, :], banks[2][:, 3 * C:4 * C], SC_B, w[1], ALU.mult, ALU.mult)
                    stt(M[b][:, 3:6, :], banks[2][:, 0:3 * C].rearrange("p (i c) -> p i c", i=3), SC_D,
                        w[3].unsqueeze(1).broadcast_to([P, 3, C]), ALU.mult, ALU.mult).then_inc(av_M, 1)
                if real(tau):
                    add_bias(eng, FIRST + tau, b, v_base)
            over_tiles(eng, 4, step_a, PEEL_A)

            eng.wait_ge(d_sk, 48)
            eng.tensor_copy(sk_f[:, :], src_keys)
            eng.tensor_copy(kn_f[:, :], kn_i[:, :, 0])
            eng.tensor_scalar(sx_i[:, :], ko_i[:, :, 0], float(N - 1), None, ALU.min)
            eng.tensor_copy(sk_c[:, :], ko_i[:, :, 0]).then_inc(bv_sk, 1)
            eng.wait_ge(bv_sk, 1)

            def last_rows(key_c, rows_i, s, n):
                eng.tensor_tensor(cont[:, :], key_c[:, :], kn_f[:, :], ALU.is_equal).then_inc(s, 1)
                eng.wait_ge(s, n)
                eng.scalar_tensor_tensor(cont[:, :], cont[:, :], float(OFF), key_c[:, :], ALU.mult, ALU.add)\
                   .then_inc(s, 1)
                eng.wait_ge(s, n + 1)
                eng.memset(cont[0:1, :], float(OFF)).then_inc(s, 1)
                eng.wait_ge(s, n + 2)
                eng.tensor_copy(rows_i[:, :], cont[:, :]).then_inc(s, 1)
                eng.wait_ge(s, n + 3)
            last_rows(sk_c, srow_i, bv_sk, 2)
            eng.nop().then_inc(v_sorted, 1)

            eng.wait_ge(s_norm, 3)
            eng.memset(ones, 1.0).then_inc(v_scale, 1)
            eng.wait_ge(s_norm, 4)
            eng.tensor_scalar(norm[:, :], norm[:, :], 1e-18, 1e18, ALU.max, ALU.min).then_inc(v_scale, 1)
            eng.wait_ge(v_scale, 2)
            eng.tensor_scalar(pow2[:, :], norm[:, :].bitcast(i32), EXPONENT, None, ALU.bitwise_and).then_inc(v_scale, 1)
            eng.wait_ge(v_scale, 3)
            eng.tensor_scalar(inv2[:, :], pow2[:, :], -1.0, float(ONE_OVER), ALU.mult, ALU.add).then_inc(v_scale, 1)
            eng.wait_ge(v_scale, 4)
            eng.tensor_scalar(descale[:, :], pow2[:, :].bitcast(f32), 1.0 / (W_TOP * H_SCALE), None, ALU.mult)
            eng.tensor_scalar(w_scale[:, :], inv2[:, :].bitcast(f32), W_TOP, None, ALU.mult).then_inc(v_scale, 1)
            eng.wait_ge(v_scale, 5)
            for i, w in enumerate((wq_sb, wk_sb, wv_sb)):
                eng.wait_ge(s_w, i + 1)
                eng.scalar_tensor_tensor(w_parts[:, i, 1], w, w_scale[:, i:i + 1], w_parts[:, i, 0],
                                         ALU.mult, ALU.subtract).then_inc(v_scale, 1)

            def masks(t, b, keys, col, s):
                eng.scalar_tensor_tensor(mask[b][:, 1:P], keys[:, bass.ds(G * t + 1, G)], col[:, bass.ds(t, 1)],
                                         upto[:, 1:P], ALU.is_equal, ALU.mult)
                eng.tensor_scalar(mask[b][:, 0:1], keys[:, bass.ds(G * t + G, 1)], col[:, bass.ds(t, 1)], None,
                                  ALU.is_equal).then_inc(s, 1)

            def dst_records():
                eng.wait_ge(d_dk, 48)
                rec = records.rearrange("p (e two) -> p e two", two=2)
                eng.tensor_copy(dk_f[:, :], rec[:, :, 0])
                eng.tensor_copy(kn_f[:, :], kn_i[:, :, 0])
                eng.tensor_scalar(dx_i[:, :], ko_i[:, :, 0], float(N - 1), None, ALU.min)
                eng.tensor_scalar(ds_i[:, :], ko_i[:, :, 1], float(N - 1), None, ALU.min)
                eng.tensor_copy(dk_c[:, :], ko_i[:, :, 0]).then_inc(bv_sk, 1)
                eng.wait_ge(bv_sk, 6)
                last_rows(dk_c, drow_i, bv_sk, 7)
                eng.nop().then_inc(v_sorted, 1)

            def step_b(tau, b):
                if isinstance(tau, int) and tau == PEEL - 1:
                    dst_records()
                if real(tau - 1) and (not isinstance(tau, int) or tau - 1 > 0):
                    t, q = tau - 1, 1 - b
                    wait(eng, b_P[q], dma_count(t, q))
                    wait(eng, bp_cum, t)
                    eng.tensor_copy(Pt[q][0:1, :], banks[b][0:1, :]).then_inc(bv_carry, 1)
                elif real(tau - 1):
                    eng.nop().then_inc(bv_carry, 1)
                if real(tau):
                    wait(eng, bp_st, tau - 1)
                    masks(tau, b, sk_f, sk_c, bv_mask)
                if real(tau - 2):
                    t = tau - 2
                    wait(eng, bp_cum, t + 1)
                    wait(eng, b_x[b], dma_count(t, b))
                    eng.tensor_copy(XO[:, t, 0:C], xg[b][:, 0:C])
                    eng.tensor_tensor(XO[:, t, C:D], banks[b][:, C:D], xg[b][:, C:D], ALU.add).then_inc(bv_x1, 1)
                    wait(eng, bp_st, t + 1)
                    wait(eng, bp_s2, t - 1)
                    eng.tensor_scalar(sz[b][:, :], banks[2][:, 0:P], 0.0, None, ALU.max).then_inc(bv_pos, 1)
                    wait(eng, bv_pos, t + 1)
                    eng.scalar_tensor_tensor(se[b][:, :], sz[b][:, :], -2.0, banks[2][:, 0:P], ALU.mult, ALU.add)\
                       .then_inc(bv_neg, 1)
                if real(tau - 3):
                    t, q = tau - 3, 1 - b
                    wait(eng, bs_ln, t + 1)
                    wait(eng, bv_pos, t + 1)
                    eng.tensor_tensor(sp[q][:, :], sz[q][:, :], se[q][:, :], ALU.add).then_inc(bv_sp, 1)
                if real(tau - 4):
                    t = tau - 4
                    wait(eng, bp_s2, t + 1)
                    wait(eng, bv_x1, t + 1)
                    eng.scalar_tensor_tensor(XO[:, t, 0:C], banks[3][:, 0:C], SC_S2, XO[:, t, 0:C],
                                             ALU.mult, ALU.add).then_inc(bv_s1, 1)
                if isinstance(tau, int) and 0 <= tau - 2 < REST:
                    add_bias(eng, FIRST + NT + tau - 2, b, v_base)
            over_tiles(eng, 4, step_b, REST + 2)

            eng.tensor_tensor(same[:, 1:KW + 1], dk_f[0:H, 1:KW + 1], dk_f[0:H, 0:KW], ALU.is_equal)
            eng.memset(same[:, 0:1], 0.0).then_inc(bv_sk, 1)
            eng.wait_ge(bv_sk, 11)
            eng.tensor_scalar(same[:, :], same[:, :], 0.5, BIG, ALU.subtract, ALU.mult)\
               .then_inc(bv_sk, 1)
            eng.wait_ge(bv_sk, 12)

            def base_rows(t0, t1):
                rows = XO[:, t0:t1, :]
                eng.tensor_tensor(rows, rows, bo_sb[:, :].unsqueeze(1).broadcast_to([P, t1 - t0, D]), ALU.add)\
                   .then_inc(bv_xo, 1)
            for b in range(2):
                eng.wait_ge(b_x1c[b], 8 * NT)
            base_rows(0, sent_with(1)[1])

            def step_c(tau, b):
                if isinstance(tau, int) and tau == 1:
                    base_rows(sent_with(2)[0], NT)
                if real(tau - 2):
                    t = tau - 2
                    wait(eng, cs_aT, t + 1)
                    if not isinstance(t, int) or t > 0:
                        eng.tensor_copy(aT[b][:, 0:1], mT[1 - b][:, P - 1:P]).then_inc(cv_fwd, 1)
                    else:
                        eng.nop().then_inc(cv_fwd, 1)
                    wait(eng, cv_fwd, 4 * t + 1)
                    wait(eng, cv_e, t - 1)
                    eng.tensor_tensor_scan(eT[b][:, 1:P], same[:, bass.ds(G * t + 1, G)], aT[b][:, 1:P],
                                           aT[b][:, 0:1], ALU.min, ALU.max).then_inc(cv_fwd, 1)
                    eng.tensor_copy(eT[b][:, 0:1], aT[b][:, 0:1])
                    eng.tensor_copy(same_back[:, ::-1], same[:, bass.ds(G * t + 1, P)]).then_inc(cv_fwd, 1)
                    wait(eng, cv_fwd, 4 * t + 3)
                    eng.tensor_tensor_scan(mT[b][:, :][:, ::-1], same_back[:, :],
                                           eT[b][:, :][:, ::-1], -BIG, ALU.min, ALU.max).then_inc(cv_fwd, 1)
                    wait(eng, cv_fwd, 4 * (t + 1))
                    eng.tensor_tensor(eT[b][:, :], aT[b][:, :], mT[b][:, :], ALU.subtract).then_inc(cv_e, 1)
                    wait(eng, cp_cum, t - 1)
                    masks(t, b, dk_f, dk_c, cv_mask)
                if real(tau - 3):
                    t, q = tau - 3, 1 - b
                    wait(eng, cp_y, t + 1)
                    wait(eng, c_out[q], dma_count(t - 2, q))
                    wait(eng, cg_y, t + 1)
                    eng.tensor_tensor(y[q][:, :], banks[7][:, :], xb[q][:, :], ALU.add).then_inc(cv_y, 1)
                if real(tau):
                    wait(eng, c_xd[b], dma_count(tau, b))
                    eng.bn_stats(st[b][:, 0:6], xd[b][:, :])
                    wait(eng, c_xs[b], dma_count(tau, b))
                    eng.bn_stats(st[b][:, 6:12], xg[b][:, :]).then_inc(cv_stats, 2)
                    apart(eng, g_const, 2 * (tau + 1))
                    wait(eng, cv_stats, 2 * (tau + 1))
                    eng.bn_aggr(mv[b][:, 0:2], st[b][:, 0:6])
                    eng.bn_aggr(mv[b][:, 2:4], st[b][:, 6:12]).then_inc(cv_mom, 2)
                if real(tau - 2):
                    t2 = tau - 2
                    wait(eng, cs_ex, t2 + 1)
                    wait(eng, cp_cum, t2 - 1)
                    wait(eng, cv_carry, t2 + 1)
                    wait(eng, cv_v, t2 + 1)
                    eng.tensor_tensor(vw[b][:, 0:D].rearrange("p (h d) -> p h d", h=H),
                                      va[b][:, 0:D].rearrange("p (h d) -> p h d", h=H),
                                      ex[b][:, :].unsqueeze(2).broadcast_to([P, H, DH]), ALU.mult)
                    eng.tensor_tensor(vw[b][:, D:D + H], va[b][:, D:D + H], ex[b][:, :], ALU.mult).then_inc(cv_vw, 1)
                if real(tau):
                    wait(eng, cs_std, tau + 1)
                    eng.reciprocal(rstd[b][:, :], std[b][:, :]).then_inc(cv_nb, 1)
                    wait(eng, cv_nb, 2 * tau + 1)
                    eng.scalar_tensor_tensor(nb[b][:, :], mv[b][:, 0:4:2], -1.0, rstd[b][:, :],
                                             ALU.mult, ALU.mult).then_inc(cv_nb, 1)
                if isinstance(tau, int) and tau == 0:
                    eng.wait_ge(g_ones, 2)
                if real(tau - 1):
                    t, q = tau - 1, 1 - b
                    wait(eng, cp_q, t + 1)
                    eng.scalar_tensor_tensor(qs[q], banks[1][:, :], descale[:, 0:1], bq_sb[:, :],
                                             ALU.mult, ALU.add).then_inc(cv_q, 1)
                if real(tau - 1):
                    wait(eng, cp_k, t + 1)
                    eng.scalar_tensor_tensor(ks[q], banks[2][:, :], descale[:, 1:2], bk_sb[:, :],
                                             ALU.mult, ALU.add).then_inc(cv_k, 1)
                    wait(eng, cv_k, 2 * t + 1)
                    eng.tensor_tensor(ks[q], ks[q], qs[q], ALU.mult).then_inc(cv_k, 1)
                    wait(eng, cv_k, 2 * (t + 1))
                    wait(eng, cp_aT, t - 1)
                    eng.tensor_reduce(a_sb[q][:, :], ks[q].rearrange("p (h d) -> p h d", h=H), AX.X, ALU.add)\
                       .then_inc(cv_a, 1)
                if real(tau - 2):
                    wait(eng, cp_cum, t2 + 1)
                    eng.tensor_scalar(rden[b][:, :], banks[7][:, 0:H], 1e-30, None, ALU.max).then_inc(cv_den, 1)
                    wait(eng, cv_den, 2 * t2 + 1)
                    eng.reciprocal(rden[b][:, :], rden[b][:, :]).then_inc(cv_den, 1)
                    wait(eng, cv_den, 2 * (t2 + 1))
                    wait(eng, cp_oT, t2 - 1)
                    eng.tensor_tensor(o_sb[b].rearrange("p (h d) -> p h d", h=H),
                                      banks[4][:, :].rearrange("p (h d) -> p h d", h=H),
                                      rden[b][:, :].unsqueeze(2).broadcast_to([P, H, DH]), ALU.mult)\
                       .then_inc(cv_o, 1)
                if real(tau):
                    wait(eng, cs_hTd, tau + 1)
                    eng.scalar_tensor_tensor(hTd[b][:, 1], banks[0][:, :], H_SCALE, hTd[b][:, 0],
                                             ALU.mult, ALU.subtract).then_inc(cv_hTd, 1)
                if real(tau - 1):
                    wait(eng, cp_v, t + 1)
                    eng.scalar_tensor_tensor(va[q][:, 0:D], banks[3][:, :], descale[:, 2:3], bv_sb[:, :],
                                             ALU.mult, ALU.add).then_inc(cv_v, 1)
                    if not isinstance(t, int) or t > 0:
                        wait(eng, cv_v, t + 1)
                        eng.tensor_copy(va[q][0:1, 0:D], banks[4][0:1, :])
                        eng.tensor_copy(va[q][0:1, D:D + H], banks[7][0:1, 0:H]).then_inc(cv_carry, 1)
                    else:
                        eng.nop().then_inc(cv_carry, 1)
                if real(tau):
                    wait(eng, cs_hTs, tau + 1)
                    eng.scalar_tensor_tensor(hTs[b][:, 1], banks[0][:, :], H_SCALE, hTs[b][:, 0],
                                             ALU.mult, ALU.subtract).then_inc(cv_hTs, 1)
            over_tiles(eng, 3, step_c, PEEL_A)


def _tiles(a, fill):
    rest = np.full((EP - E,) + a.shape[1:], fill, a.dtype)
    a = np.concatenate([a, rest]).reshape((NT, P) + a.shape[1:])
    return np.ascontiguousarray(np.swapaxes(a, 0, 1))


def _blocks(w):
    return np.ascontiguousarray(w.T.reshape(4, C, D).transpose(1, 0, 2))


def kernel(**inputs):
    import concourse.bacc as _bacc
    from concourse.bass_utils import run_bass_kernel_spmd as _run

    a = {k: np.asarray(v) for k, v in inputs.items()}
    src, dst = a["src"], a["dst"]
    l0 = {k[len("L0_gnn_"):]: v for k, v in a.items() if k.startswith("L0_gnn_")}
    l1 = {k[len("L1_gnn_"):]: v for k, v in a.items() if k.startswith("L1_gnn_")}
    w_kv = l1["Wkv"].reshape(H, 2, DH, D)
    b_kv = l1["bkv"].reshape(H, 2, DH)
    order = [
        ("x", a["x"]),
        ("src_cols", _tiles(src, NONE)), ("edge_cols", _tiles(np.stack([dst, src], 1), NONE)),
        ("f_t", np.ascontiguousarray(np.concatenate(
            [a["edge_attr_20"], np.zeros((EP - E, NRBF), a["edge_attr_20"].dtype)]).T)),
        ("rcut_cols", _tiles(a["edge_weight"], 0)), ("r_cols", _tiles(a["edge_attr_3"], 1)),
        ("w_s", l0["W_in2f_s"]), ("w_v", l0["W_in2f_v"]),
        ("wf1", l0["Wf1"]), ("bf1", l0["bf1"].reshape(C, 1)),
        ("wf2", l0["Wf2"][:, :4 * C].reshape(C, 2, C, 2).transpose(0, 1, 3, 2).reshape(C, 4, C)),
        ("bf2", l0["bf2"][:4 * C].reshape(2, C, 2).transpose(1, 0, 2).reshape(C, 4)),
        ("w1s", l0["W1_s"].reshape(C, 2, C)),
        ("w1v_t", l0["W1_v"].reshape(C, 2, C).transpose(1, 2, 0)),
        ("w2s", l0["W2_s"]), ("w2v", l0["W2_v"]),
        ("wq", _blocks(l1["Wq"])), ("bq", l1["bq"].reshape(1, D)),
        ("wk", _blocks(w_kv[:, 0].reshape(D, D))), ("bk", b_kv[:, 0].reshape(1, D)),
        ("wv", _blocks(w_kv[:, 1].reshape(D, D))), ("bv", b_kv[:, 1].reshape(1, D)),
        ("wo", _blocks(l1["Wo"])), ("bo2", np.concatenate([l1["bo"], l1["bo"]]).reshape(1, 2 * D)),
    ]
    nc = _bacc.Bacc("TRN2", target_bir_lowering=False, num_devices=1)
    arrays, args = {}, {}
    for name, v in order:
        v = np.ascontiguousarray(v)
        arrays[name + "_dram"] = v
        args[name] = nc.dram_tensor(name + "_dram", v.shape, mybir.dt.from_np(v.dtype), kind="ExternalInput").ap()
    f32, i32 = mybir.dt.float32, mybir.dt.int32
    args["out"] = nc.dram_tensor("out_dram", (N, D), f32, kind="ExternalOutput").ap()
    for name, shape, dt in (("psort", (ROWS, D), f32), ("skey", (ROWS, 1), i32), ("drec", (ROWS, 2), i32),
                            ("table", (P * 80, 1), i32), ("x1c", (EP, D), f32)):
        args[name] = nc.dram_tensor(name + "_scratch", shape, dt).ap()
    gnn_kernel(nc, **args)
    r = _run(nc, [arrays], core_ids=[0])
    return r.results[0]["out_dram"]
```
